# Optimizing a Trainium2 kernel written in Bass

```python
import numpy as np
import jax
import jax.numpy as jnp

def _softmax(x, axis=-1):
    return jax.nn.softmax(x, axis=axis)

def _gelu(x):
    return jax.nn.gelu(x, approximate=True)

def _silu(x):
    return jax.nn.silu(x)

def _sigmoid(x):
    return jax.nn.sigmoid(x)

def _layernorm(x, axis=-1, eps=1e-05):
    m = jnp.mean(x, axis=axis, keepdims=True)
    v = jnp.var(x, axis=axis, keepdims=True)
    return (x - m) / jnp.sqrt(v + eps)

def _scatter_add(tgt, idx, src, axis=0):
    return tgt.at[idx].add(src)

def _segment_sum(src, seg, n):
    return jax.ops.segment_sum(src, seg, n)
kernel_name = 'mk_lm_tower_d4_tok_ids512_r4_111376'

def setup_inputs(seed: int=0):
    np.random.seed(seed)
    _w = jnp.asarray

    def _rec_inputs():
        import jax
        import jax.numpy as jnp
        _rk = jax.random.key(seed)
        x = jax.random.randint(jax.random.fold_in(_rk, 1), (16, 128), 0, 64, jnp.int32)
        return x
    x = _rec_inputs()

    def _L0_tok_setup():
        import jax, jax.numpy as jnp
        import numpy as np
        NGRAM_SIZES = (2, 3, 4)
        HASH_VOCAB = 25000
        EMBED_DIM = 128
        BATCH, SEQ = (8, 1024)

        def _ngram_hash_ids(byte_sequence, n):
            L = byte_sequence.shape[1] - n + 1
            h = jnp.zeros((byte_sequence.shape[0], L), dtype=jnp.int64)
            for j in range(n):
                h = (h * 64 + byte_sequence[:, j:j + L]) % HASH_VOCAB
            return h

        def _ngram_embed(byte_sequence, table, n):
            B, S = byte_sequence.shape
            ids = _ngram_hash_ids(byte_sequence, n)
            emb = table[ids]
            out = jnp.zeros((B, S, table.shape[1]), dtype=table.dtype)
            c = n // 2
            return out.at[:, c:c + emb.shape[1]].set(emb)
        key = jax.random.key(seed)
        ks = jax.random.split(key, 6)
        return {'byte_sequence': jax.random.randint(ks[0], (BATCH, SEQ), 0, 64, dtype=jnp.int64), 'emb_2': jax.random.normal(ks[1], (HASH_VOCAB, EMBED_DIM), dtype=jnp.float32), 'emb_3': jax.random.normal(ks[2], (HASH_VOCAB, EMBED_DIM), dtype=jnp.float32), 'emb_4': jax.random.normal(ks[3], (HASH_VOCAB, EMBED_DIM), dtype=jnp.float32), 'proj_w': jax.random.normal(ks[4], (EMBED_DIM, len(NGRAM_SIZES) * EMBED_DIM), dtype=jnp.float32) * 0.02, 'proj_b': jax.random.normal(ks[5], (EMBED_DIM,), dtype=jnp.float32) * 0.02}
    _L0_tok_all = _L0_tok_setup()
    _L0_tok_in = {k: v for k, v in _L0_tok_all.items() if k in ('emb_2', 'emb_3', 'emb_4', 'proj_w', 'proj_b')}
    del _L0_tok_all

    def _L0_attn_setup():
        import jax, jax.numpy as jnp
        import numpy as np
        B, T, D, H = (8, 256, 128, 8)
        DK = D // H

        def layer_norm(x, g, b, eps=1e-05):
            mu = jnp.mean(x, axis=-1, keepdims=True)
            var = jnp.var(x, axis=-1, keepdims=True)
            return (x - mu) * jax.lax.rsqrt(var + eps) * g + b

        def rel_shift(x):
            b, h, t1, t2 = x.shape
            xp = jnp.pad(x, ((0, 0), (0, 0), (0, 0), (1, 0)))
            xp = xp.reshape(b, h, t2 + 1, t1)[:, :, 1:, :]
            return xp.reshape(b, h, t1, t2)
        key = jax.random.key(seed)
        ks = jax.random.split(key, 6)
        s = 0.02
        return {'inputs': jax.random.normal(ks[0], (B, T, D), jnp.float32), 'ln1_g': jnp.ones((D,), jnp.float32), 'ln1_b': jnp.zeros((D,), jnp.float32), 'ln2_g': jnp.ones((D,), jnp.float32), 'ln2_b': jnp.zeros((D,), jnp.float32), 'W_qkv': jax.random.normal(ks[1], (3 * D, D), jnp.float32) * s, 'W_pos': jax.random.normal(ks[2], (D, D), jnp.float32) * s, 'W_out': jax.random.normal(ks[3], (D, D), jnp.float32) * s, 'b_out': jnp.zeros((D,), jnp.float32), 'pos_bias_u': jax.random.normal(ks[4], (H, DK), jnp.float32) * s, 'pos_bias_v': jax.random.normal(ks[5], (H, DK), jnp.float32) * s}
    _L0_attn_all = _L0_attn_setup()
    _L0_attn_in = {k: v for k, v in _L0_attn_all.items() if k in ('ln1_g', 'ln1_b', 'ln2_g', 'ln2_b', 'W_qkv', 'W_pos', 'W_out', 'b_out', 'pos_bias_u', 'pos_bias_v')}
    del _L0_attn_all

    def _L0_ffn_setup():
        import jax, jax.numpy as jnp
        import numpy as np
        E, TOPK, H, DK, DV, D = (4, 2, 8, 64, 64, 128)
        B, L = (4, 256)
        VDIM = H * DV

        def _silu(x):
            return x * jax.nn.sigmoid(x)

        def _l2norm(x):
            return x * jax.lax.rsqrt(jnp.sum(x * x, axis=-1, keepdims=True) + 1e-06)

        def _forward(h, Wq, Wgate, Wk, Wv, Wb, Wa, A_log, dt_bias, Wg, o_norm_weight, Wo):
            Bs, Ls, _ = h.shape
            scores = jax.nn.softmax((h @ Wgate).astype(jnp.float32), axis=-1)
            rw, sel = jax.lax.top_k(scores, TOPK)
            rw = rw / jnp.sum(rw, axis=-1, keepdims=True)
            bi = jnp.arange(Bs)[:, None, None]
            li = jnp.arange(Ls)[None, :, None]
            w_full = jnp.zeros((Bs, Ls, E), jnp.float32).at[bi, li, sel].set(rw)
            m = jnp.transpose(w_full > 0, (2, 0, 1))
            q = _l2norm(_silu(h @ Wq).reshape(Bs, Ls, H, DK))
            k = _l2norm(_silu(h @ Wk).reshape(Bs, Ls, H, DK))
            v = _silu(h @ Wv).reshape(Bs, Ls, H, DV)
            beta = jax.nn.sigmoid(h @ Wb)
            g = -jnp.exp(A_log) * jax.nn.softplus((h @ Wa).astype(jnp.float32) + dt_bias)
            beta_e = beta[None] * m[..., None]
            g_e = jnp.where(m[..., None], g[None], 0.0)
            scale = DK ** (-0.5)
            xs = (jnp.moveaxis(q, 1, 0), jnp.moveaxis(k, 1, 0), jnp.moveaxis(v, 1, 0), jnp.moveaxis(beta_e, 2, 0), jnp.moveaxis(g_e, 2, 0))

            def step(S, x):
                qt, kt, vt, bt, gt = x
                S = S * jnp.exp(gt)[..., None, None]
                kv = jnp.einsum('bhk,ebhkv->ebhv', kt, S)
                delta = (vt[None] - kv) * bt[..., None]
                S = S + kt[None, :, :, :, None] * delta[..., None, :]
                ot = jnp.einsum('bhk,ebhkv->ebhv', qt * scale, S)
                return (S, ot)
            S0 = jnp.zeros((E, Bs, H, DK, DV), jnp.float32)
            _, o = jax.lax.scan(step, S0, xs)
            o = jnp.moveaxis(o, 0, 2)
            core = jnp.einsum('ble,eblhv->blhv', w_full, o)
            gate = _silu((h @ Wg).reshape(Bs, Ls, H, DV))
            core = core * jax.lax.rsqrt(jnp.mean(core * core, axis=-1, keepdims=True) + 1e-05)
            core = core * o_norm_weight * gate
            return core.reshape(Bs, Ls, VDIM) @ Wo
        key = jax.random.key(seed)
        ks = jax.random.split(key, 12)
        std = 0.02
        h = jax.random.normal(ks[0], (B, L, D), jnp.float32)
        Wq = jax.random.normal(ks[1], (D, H * DK), jnp.float32) * std
        Wgate = jax.random.normal(ks[2], (D, E), jnp.float32) * std
        Wk = jax.random.normal(ks[3], (D, H * DK), jnp.float32) * std
        Wv = jax.random.normal(ks[4], (D, VDIM), jnp.float32) * std
        Wb = jax.random.normal(ks[5], (D, H), jnp.float32) * std
        Wa = jax.random.normal(ks[6], (D, H), jnp.float32) * std
        Wg = jax.random.normal(ks[7], (D, VDIM), jnp.float32) * std
        Wo = jax.random.normal(ks[8], (VDIM, D), jnp.float32) * std
        A = jax.random.uniform(ks[9], (H,), jnp.float32, 0.0001, 16.0)
        A_log = jnp.log(A)
        dt = jnp.exp(jax.random.uniform(ks[10], (H,), jnp.float32) * (np.float32(np.log(0.1)) - np.float32(np.log(0.001))) + np.float32(np.log(0.001)))
        dt = jnp.maximum(dt, 0.0001)
        dt_bias = dt + jnp.log(-jnp.expm1(-dt))
        o_norm_weight = jnp.ones((DV,), jnp.float32)
        return {'hidden_states': h, 'Wq': Wq, 'Wgate': Wgate, 'Wk': Wk, 'Wv': Wv, 'Wb': Wb, 'Wa': Wa, 'A_log': A_log, 'dt_bias': dt_bias, 'Wg': Wg, 'o_norm_weight': o_norm_weight, 'Wo': Wo}
    _L0_ffn_all = _L0_ffn_setup()
    _L0_ffn_in = {k: v for k, v in _L0_ffn_all.items() if k in ('Wq', 'Wgate', 'Wk', 'Wv', 'Wb', 'Wa', 'A_log', 'dt_bias', 'Wg', 'o_norm_weight', 'Wo')}
    del _L0_ffn_all

    def _L1_attn_setup():
        import jax, jax.numpy as jnp
        import numpy as np
        B, T, D = (64, 128, 128)
        H = 256
        I = 128
        MASK_VALUE = 0.0

        def _lstm_layer(x, mask, W, U, b):
            Hd = U.shape[0]
            xz = jnp.einsum('btd,dk->btk', x, W) + b
            xz_t = jnp.transpose(xz, (1, 0, 2))
            mask_t = jnp.transpose(mask, (1, 0))

            def step(carry, inp):
                h, c = carry
                z_in, m = inp
                z = z_in + h @ U
                i, f, g, o = jnp.split(z, 4, axis=-1)
                i = jax.nn.sigmoid(i)
                f = jax.nn.sigmoid(f)
                g = jnp.tanh(g)
                o = jax.nn.sigmoid(o)
                c_new = f * c + i * g
                h_new = o * jnp.tanh(c_new)
                m2 = m[:, None]
                h = jnp.where(m2, h_new, h)
                c = jnp.where(m2, c_new, c)
                return ((h, c), h)
            h0 = jnp.zeros((x.shape[0], Hd), dtype=x.dtype)
            c0 = jnp.zeros((x.shape[0], Hd), dtype=x.dtype)
            (_, _), hs = jax.lax.scan(step, (h0, c0), (xz_t, mask_t))
            return jnp.transpose(hs, (1, 0, 2))
        key = jax.random.key(seed)
        ks = jax.random.split(key, 7)
        s = 0.05
        inputs = jax.random.normal(ks[0], (B, T, D), dtype=jnp.float32)
        W0 = jax.random.normal(ks[1], (D, 4 * H), dtype=jnp.float32) * s
        U0 = jax.random.normal(ks[2], (H, 4 * H), dtype=jnp.float32) * s
        b0 = jnp.zeros((4 * H,), dtype=jnp.float32)
        W1 = jax.random.normal(ks[3], (H, 4 * I), dtype=jnp.float32) * s
        U1 = jax.random.normal(ks[4], (I, 4 * I), dtype=jnp.float32) * s
        b1 = jnp.zeros((4 * I,), dtype=jnp.float32)
        return {'inputs': inputs, 'W0': W0, 'U0': U0, 'b0': b0, 'W1': W1, 'U1': U1, 'b1': b1}
    _L1_attn_all = _L1_attn_setup()
    _L1_attn_in = {k: v for k, v in _L1_attn_all.items() if k in ('W0', 'U0', 'b0', 'W1', 'U1', 'b1')}
    del _L1_attn_all

    def _L1_ffn_setup():
        import jax, jax.numpy as jnp
        import numpy as np
        D, E, DR, K, DFF, DSH = (128, 64, 64, 2, 512, 256)
        TEMP = 0.7
        SHARED_SCALE = 0.25
        EPS = 1e-05

        def _ln(x, g, b):
            m = jnp.mean(x, axis=-1, keepdims=True)
            v = jnp.mean(jnp.square(x - m), axis=-1, keepdims=True)
            return (x - m) * jax.lax.rsqrt(v + EPS) * g + b
        key = jax.random.key(seed)
        ks = jax.random.split(key, 16)
        s = 0.02
        return {'x': jax.random.normal(ks[0], (1, 128, D), dtype=jnp.float32), 'ln1_g': jnp.ones((D,), jnp.float32), 'ln1_b': jnp.zeros((D,), jnp.float32), 'Wr': jax.random.normal(ks[1], (D, DR), jnp.float32) * s, 'codebook': jax.random.normal(ks[2], (E, DR), jnp.float32), 'W1': jax.random.normal(ks[3], (E, D, DFF), jnp.float32) * s, 'b1': jnp.zeros((E, DFF), jnp.float32), 'W2': jax.random.normal(ks[4], (E, DFF, D), jnp.float32) * s, 'b2': jnp.zeros((E, D), jnp.float32), 'Ws1': jax.random.normal(ks[5], (D, DSH), jnp.float32) * s, 'bs1': jnp.zeros((DSH,), jnp.float32), 'Ws2': jax.random.normal(ks[6], (DSH, D), jnp.float32) * s, 'bs2': jnp.zeros((D,), jnp.float32), 'ffln_g': jnp.ones((D,), jnp.float32), 'ffln_b': jnp.zeros((D,), jnp.float32), 'Wf1': jax.random.normal(ks[7], (D, DFF), jnp.float32) * s, 'bf1': jnp.zeros((DFF,), jnp.float32), 'Wf2': jax.random.normal(ks[8], (DFF, D), jnp.float32) * s, 'bf2': jnp.zeros((D,), jnp.float32)}
    _L1_ffn_all = _L1_ffn_setup()
    _L1_ffn_in = {k: v for k, v in _L1_ffn_all.items() if k in ('ln1_g', 'ln1_b', 'Wr', 'codebook', 'W1', 'b1', 'W2', 'b2', 'Ws1', 'bs1', 'Ws2', 'bs2', 'ffln_g', 'ffln_b', 'Wf1', 'bf1', 'Wf2', 'bf2')}
    del _L1_ffn_all

    def _L2_attn_setup():
        import jax, jax.numpy as jnp
        import numpy as np
        B, T, D = (8, 128, 128)
        key = jax.random.key(seed)
        ks = jax.random.split(key, 13)
        s = 1.0 / np.sqrt(D)
        inp = {'x': jax.random.normal(ks[0], (B, T, D), dtype=jnp.float32)}
        names = ['qf', 'kf', 'vf', 'qt', 'kt', 'vt']
        for i, n in enumerate(names):
            inp[f'W_{n}'] = jax.random.uniform(ks[1 + 2 * i], (D, D), dtype=jnp.float32, minval=-s, maxval=s)
            inp[f'b_{n}'] = jax.random.uniform(ks[2 + 2 * i], (D,), dtype=jnp.float32, minval=-s, maxval=s)
        return inp
    _L2_attn_all = _L2_attn_setup()
    _L2_attn_in = {k: v for k, v in _L2_attn_all.items() if k in ('W_qf', 'b_qf', 'W_kf', 'b_kf', 'W_vf', 'b_vf', 'W_qt', 'b_qt', 'W_kt', 'b_kt', 'W_vt', 'b_vt')}
    del _L2_attn_all

    def _L2_ffn_setup():
        import jax, jax.numpy as jnp
        import numpy as np
        import math
        B, T, D, H, E, TOPK = (8, 1024, 128, 512, 8, 2)
        CAP_FRAC = 1.0

        def _expert_ffn(x, w1, w2, w3):
            h = jax.nn.gelu(x @ w2 * (x @ w1), approximate=False)
            return h @ w3
        key = jax.random.key(seed)
        ks = jax.random.split(key, 6)
        x = jax.random.normal(ks[0], (B, T, D), dtype=jnp.float32)
        Wr = jax.random.normal(ks[1], (D, E), dtype=jnp.float32) * 0.02
        br = jnp.zeros((E,), dtype=jnp.float32)
        W1 = jax.random.normal(ks[2], (E, D, H), dtype=jnp.float32) * 0.02
        W2 = jax.random.normal(ks[3], (E, D, H), dtype=jnp.float32) * 0.02
        W3 = jax.random.normal(ks[4], (E, H, D), dtype=jnp.float32) * 0.02
        return {'x': x, 'Wr': Wr, 'br': br, 'W1': W1, 'W2': W2, 'W3': W3}
    _L2_ffn_all = _L2_ffn_setup()
    _L2_ffn_in = {k: v for k, v in _L2_ffn_all.items() if k in ('Wr', 'br', 'W1', 'W2', 'W3')}
    del _L2_ffn_all

    def _L3_attn_setup():
        import jax, jax.numpy as jnp
        import numpy as np
        D_MODEL = 128
        D_STATE = 16
        D_CONV = 4
        EXPAND = 2
        D_INNER = EXPAND * D_MODEL
        DT_RANK = (D_MODEL + 15) // 16
        BATCH, SEQ = (16, 512)
        LN_EPS = 1e-12

        def _selective_scan(u, dt, A, Bm, C, D):
            h0 = jnp.zeros((u.shape[0], u.shape[2], A.shape[1]), u.dtype)

            def step(h, inp):
                dt_t, B_t, u_t, C_t = inp
                dA = jnp.exp(dt_t[..., None] * A)
                h = dA * h + (dt_t * u_t)[..., None] * B_t[:, None, :]
                y = jnp.einsum('bdn,bn->bd', h, C_t)
                return (h, y)
            tswap = lambda x: jnp.swapaxes(x, 0, 1)
            _, ys = jax.lax.scan(step, h0, (tswap(dt), tswap(Bm), tswap(u), tswap(C)))
            return jnp.swapaxes(ys, 0, 1) + u * D

        def _mamba(x, in_proj_w, conv_w, conv_b, x_proj_w, dt_proj_w, dt_proj_b, A_log, D, out_proj_w):
            L = x.shape[1]
            xz = jnp.einsum('bld,ed->ble', x, in_proj_w)
            xc, z = jnp.split(xz, 2, axis=-1)
            P = D_CONV - 1
            xp = jnp.pad(xc, ((0, 0), (P, 0), (0, 0)))
            xconv = conv_b + sum((xp[:, k:k + L, :] * conv_w[:, k] for k in range(D_CONV)))
            xa = jax.nn.silu(xconv)
            dbl = jnp.einsum('bld,ed->ble', xa, x_proj_w)
            dt = jax.nn.softplus(jnp.einsum('blr,dr->bld', dbl[..., :DT_RANK], dt_proj_w) + dt_proj_b)
            Bm = dbl[..., DT_RANK:DT_RANK + D_STATE]
            C = dbl[..., DT_RANK + D_STATE:]
            A = -jnp.exp(A_log)
            y = _selective_scan(xa, dt, A, Bm, C, D)
            y = y * jax.nn.silu(z)
            return jnp.einsum('ble,de->bld', y, out_proj_w)
        key = jax.random.key(seed)
        ks = jax.random.split(key, 8)
        s = lambda k, shape, scale: jax.random.normal(k, shape, dtype=jnp.float32) * scale
        dt_init = float(np.log(np.expm1(0.01)))
        return {'input_tensor': s(ks[0], (BATCH, SEQ, D_MODEL), 1.0), 'in_proj_w': s(ks[1], (2 * D_INNER, D_MODEL), D_MODEL ** (-0.5)), 'conv_w': s(ks[2], (D_INNER, D_CONV), D_CONV ** (-0.5)), 'conv_b': jnp.zeros((D_INNER,), jnp.float32), 'x_proj_w': s(ks[3], (DT_RANK + 2 * D_STATE, D_INNER), D_INNER ** (-0.5)), 'dt_proj_w': s(ks[4], (D_INNER, DT_RANK), DT_RANK ** (-0.5)), 'dt_proj_b': jnp.full((D_INNER,), dt_init, jnp.float32), 'A_log': jnp.log(jnp.broadcast_to(jnp.arange(1, D_STATE + 1, dtype=jnp.float32), (D_INNER, D_STATE))), 'D': jnp.ones((D_INNER,), jnp.float32), 'out_proj_w': s(ks[5], (D_MODEL, D_INNER), D_INNER ** (-0.5)), 'ln_gamma': jnp.ones((D_MODEL,), jnp.float32), 'ln_beta': jnp.zeros((D_MODEL,), jnp.float32)}
    _L3_attn_all = _L3_attn_setup()
    _L3_attn_in = {k: v for k, v in _L3_attn_all.items() if k in ('in_proj_w', 'conv_w', 'conv_b', 'x_proj_w', 'dt_proj_w', 'dt_proj_b', 'A_log', 'D', 'out_proj_w', 'ln_gamma', 'ln_beta')}
    del _L3_attn_all

    def _L3_ffn_setup():
        import jax, jax.numpy as jnp
        import numpy as np
        D = 128
        H = 8
        K = 4
        HD = D // H

        def _ln(x, w, b, eps=1e-05):
            m = x.mean(-1, keepdims=True)
            v = ((x - m) ** 2).mean(-1, keepdims=True)
            return (x - m) / jnp.sqrt(v + eps) * w + b

        def _spatial_experts(xn, idx, in_w, in_b, out_w, out_b):
            W = in_w[idx]
            qkv = jnp.einsum('btd,bed->bte', xn, W) + in_b[idx][:, None, :]
            q, k, v = jnp.split(qkv, 3, axis=-1)
            B, T, _ = xn.shape
            q = q.reshape(B, T, H, HD) * HD ** (-0.5)
            k = k.reshape(B, T, H, HD)
            v = v.reshape(B, T, H, HD)
            att = jax.nn.softmax(jnp.einsum('bthd,bshd->bhts', q, k), axis=-1)
            o = jnp.einsum('bhts,bshd->bthd', att, v).reshape(B, T, D)
            return jnp.einsum('btd,bod->bto', o, out_w[idx]) + out_b[idx][:, None, :]

        def _temporal_experts(xt, idx, qw, qb, kw, kb, vw, vb, pw, pb):
            B, T, _ = xt.shape
            q = (jnp.einsum('btd,bod->bto', xt, qw[idx]) + qb[idx][:, None, :]).reshape(B, T, H, HD)
            k = (jnp.einsum('btd,bod->bto', xt, kw[idx]) + kb[idx][:, None, :]).reshape(B, T, H, HD)
            v = (jnp.einsum('btd,bod->bto', xt, vw[idx]) + vb[idx][:, None, :]).reshape(B, T, H, HD)
            logits = jnp.einsum('bthd,bshd->bhts', q, k) * HD ** (-0.5)
            causal = jnp.tril(jnp.ones((T, T), dtype=bool))
            logits = jnp.where(causal, logits, -jnp.inf)
            att = jax.nn.softmax(logits, axis=-1)
            o = jnp.einsum('bhts,bshd->bthd', att, v).reshape(B, T, D)
            o = jnp.einsum('btd,bod->bto', o, pw[idx]) + pb[idx][:, None, :]
            return xt + o

        def _cross_mha(q_in, kv_in, in_w, in_b, out_w, out_b):
            B, T, _ = q_in.shape
            S = kv_in.shape[1]
            Wq, Wk, Wv = (in_w[:D], in_w[D:2 * D], in_w[2 * D:])
            bq, bk, bv = (in_b[:D], in_b[D:2 * D], in_b[2 * D:])
            q = (q_in @ Wq.T + bq).reshape(B, T, H, HD) * HD ** (-0.5)
            k = (kv_in @ Wk.T + bk).reshape(B, S, H, HD)
            v = (kv_in @ Wv.T + bv).reshape(B, S, H, HD)
            att = jax.nn.softmax(jnp.einsum('bthd,bshd->bhts', q, k), axis=-1)
            o = jnp.einsum('bhts,bshd->bthd', att, v).reshape(B, T, D)
            return o @ out_w.T + out_b
        key = jax.random.key(seed)
        ks = iter(jax.random.split(key, 40))
        B, T = (64, 64)
        p = lambda *shape: jax.random.normal(next(ks), shape, dtype=jnp.float32) * 0.02
        inp = {'x': jax.random.normal(next(ks), (B, T, D), dtype=jnp.float32), 'router_w1': p(128, D), 'router_b1': jnp.zeros((128,), jnp.float32), 'router_w2': p(2 * K, 128), 'router_b2': jnp.zeros((2 * K,), jnp.float32), 'norm_s_w': jnp.ones((D,), jnp.float32), 'norm_s_b': jnp.zeros((D,), jnp.float32), 'norm_t_w': jnp.ones((D,), jnp.float32), 'norm_t_b': jnp.zeros((D,), jnp.float32), 'sp_in_w': p(K, 3 * D, D), 'sp_in_b': jnp.zeros((K, 3 * D), jnp.float32), 'sp_out_w': p(K, D, D), 'sp_out_b': jnp.zeros((K, D), jnp.float32), 'tq_w': p(K, D, D), 'tq_b': jnp.zeros((K, D), jnp.float32), 'tk_w': p(K, D, D), 'tk_b': jnp.zeros((K, D), jnp.float32), 'tv_w': p(K, D, D), 'tv_b': jnp.zeros((K, D), jnp.float32), 'tp_w': p(K, D, D), 'tp_b': jnp.zeros((K, D), jnp.float32), 'cross_in_w': p(3 * D, D), 'cross_in_b': jnp.zeros((3 * D,), jnp.float32), 'cross_out_w': p(D, D), 'cross_out_b': jnp.zeros((D,), jnp.float32), 'norm_mlp_w': jnp.ones((D,), jnp.float32), 'norm_mlp_b': jnp.zeros((D,), jnp.float32), 'mlp_w1': p(4 * D, D), 'mlp_b1': jnp.zeros((4 * D,), jnp.float32), 'mlp_w2': p(D, 4 * D), 'mlp_b2': jnp.zeros((D,), jnp.float32)}
        return inp
    _L3_ffn_all = _L3_ffn_setup()
    _L3_ffn_in = {k: v for k, v in _L3_ffn_all.items() if k in ('router_w1', 'router_b1', 'router_w2', 'router_b2', 'norm_s_w', 'norm_s_b', 'norm_t_w', 'norm_t_b', 'sp_in_w', 'sp_in_b', 'sp_out_w', 'sp_out_b', 'tq_w', 'tq_b', 'tk_w', 'tk_b', 'tv_w', 'tv_b', 'tp_w', 'tp_b', 'cross_in_w', 'cross_in_b', 'cross_out_w', 'cross_out_b', 'norm_mlp_w', 'norm_mlp_b', 'mlp_w1', 'mlp_b1', 'mlp_w2', 'mlp_b2')}
    del _L3_ffn_all
    return {'x': x, 'L0_tok_emb_2': _L0_tok_in['emb_2'], 'L0_tok_emb_3': _L0_tok_in['emb_3'], 'L0_tok_emb_4': _L0_tok_in['emb_4'], 'L0_tok_proj_w': _L0_tok_in['proj_w'], 'L0_tok_proj_b': _L0_tok_in['proj_b'], 'L0_attn_ln1_g': _L0_attn_in['ln1_g'], 'L0_attn_ln1_b': _L0_attn_in['ln1_b'], 'L0_attn_ln2_g': _L0_attn_in['ln2_g'], 'L0_attn_ln2_b': _L0_attn_in['ln2_b'], 'L0_attn_W_qkv': _L0_attn_in['W_qkv'], 'L0_attn_W_pos': _L0_attn_in['W_pos'], 'L0_attn_W_out': _L0_attn_in['W_out'], 'L0_attn_b_out': _L0_attn_in['b_out'], 'L0_attn_pos_bias_u': _L0_attn_in['pos_bias_u'], 'L0_attn_pos_bias_v': _L0_attn_in['pos_bias_v'], 'L0_ffn_Wq': _L0_ffn_in['Wq'], 'L0_ffn_Wgate': _L0_ffn_in['Wgate'], 'L0_ffn_Wk': _L0_ffn_in['Wk'], 'L0_ffn_Wv': _L0_ffn_in['Wv'], 'L0_ffn_Wb': _L0_ffn_in['Wb'], 'L0_ffn_Wa': _L0_ffn_in['Wa'], 'L0_ffn_A_log': _L0_ffn_in['A_log'], 'L0_ffn_dt_bias': _L0_ffn_in['dt_bias'], 'L0_ffn_Wg': _L0_ffn_in['Wg'], 'L0_ffn_o_norm_weight': _L0_ffn_in['o_norm_weight'], 'L0_ffn_Wo': _L0_ffn_in['Wo'], 'L1_attn_W0': _L1_attn_in['W0'], 'L1_attn_U0': _L1_attn_in['U0'], 'L1_attn_b0': _L1_attn_in['b0'], 'L1_attn_W1': _L1_attn_in['W1'], 'L1_attn_U1': _L1_attn_in['U1'], 'L1_attn_b1': _L1_attn_in['b1'], 'L1_ffn_ln1_g': _L1_ffn_in['ln1_g'], 'L1_ffn_ln1_b': _L1_ffn_in['ln1_b'], 'L1_ffn_Wr': _L1_ffn_in['Wr'], 'L1_ffn_codebook': _L1_ffn_in['codebook'], 'L1_ffn_W1': _L1_ffn_in['W1'], 'L1_ffn_b1': _L1_ffn_in['b1'], 'L1_ffn_W2': _L1_ffn_in['W2'], 'L1_ffn_b2': _L1_ffn_in['b2'], 'L1_ffn_Ws1': _L1_ffn_in['Ws1'], 'L1_ffn_bs1': _L1_ffn_in['bs1'], 'L1_ffn_Ws2': _L1_ffn_in['Ws2'], 'L1_ffn_bs2': _L1_ffn_in['bs2'], 'L1_ffn_ffln_g': _L1_ffn_in['ffln_g'], 'L1_ffn_ffln_b': _L1_ffn_in['ffln_b'], 'L1_ffn_Wf1': _L1_ffn_in['Wf1'], 'L1_ffn_bf1': _L1_ffn_in['bf1'], 'L1_ffn_Wf2': _L1_ffn_in['Wf2'], 'L1_ffn_bf2': _L1_ffn_in['bf2'], 'L2_attn_W_qf': _L2_attn_in['W_qf'], 'L2_attn_b_qf': _L2_attn_in['b_qf'], 'L2_attn_W_kf': _L2_attn_in['W_kf'], 'L2_attn_b_kf': _L2_attn_in['b_kf'], 'L2_attn_W_vf': _L2_attn_in['W_vf'], 'L2_attn_b_vf': _L2_attn_in['b_vf'], 'L2_attn_W_qt': _L2_attn_in['W_qt'], 'L2_attn_b_qt': _L2_attn_in['b_qt'], 'L2_attn_W_kt': _L2_attn_in['W_kt'], 'L2_attn_b_kt': _L2_attn_in['b_kt'], 'L2_attn_W_vt': _L2_attn_in['W_vt'], 'L2_attn_b_vt': _L2_attn_in['b_vt'], 'L2_ffn_Wr': _L2_ffn_in['Wr'], 'L2_ffn_br': _L2_ffn_in['br'], 'L2_ffn_W1': _L2_ffn_in['W1'], 'L2_ffn_W2': _L2_ffn_in['W2'], 'L2_ffn_W3': _L2_ffn_in['W3'], 'L3_attn_in_proj_w': _L3_attn_in['in_proj_w'], 'L3_attn_conv_w': _L3_attn_in['conv_w'], 'L3_attn_conv_b': _L3_attn_in['conv_b'], 'L3_attn_x_proj_w': _L3_attn_in['x_proj_w'], 'L3_attn_dt_proj_w': _L3_attn_in['dt_proj_w'], 'L3_attn_dt_proj_b': _L3_attn_in['dt_proj_b'], 'L3_attn_A_log': _L3_attn_in['A_log'], 'L3_attn_D': _L3_attn_in['D'], 'L3_attn_out_proj_w': _L3_attn_in['out_proj_w'], 'L3_attn_ln_gamma': _L3_attn_in['ln_gamma'], 'L3_attn_ln_beta': _L3_attn_in['ln_beta'], 'L3_ffn_router_w1': _L3_ffn_in['router_w1'], 'L3_ffn_router_b1': _L3_ffn_in['router_b1'], 'L3_ffn_router_w2': _L3_ffn_in['router_w2'], 'L3_ffn_router_b2': _L3_ffn_in['router_b2'], 'L3_ffn_norm_s_w': _L3_ffn_in['norm_s_w'], 'L3_ffn_norm_s_b': _L3_ffn_in['norm_s_b'], 'L3_ffn_norm_t_w': _L3_ffn_in['norm_t_w'], 'L3_ffn_norm_t_b': _L3_ffn_in['norm_t_b'], 'L3_ffn_sp_in_w': _L3_ffn_in['sp_in_w'], 'L3_ffn_sp_in_b': _L3_ffn_in['sp_in_b'], 'L3_ffn_sp_out_w': _L3_ffn_in['sp_out_w'], 'L3_ffn_sp_out_b': _L3_ffn_in['sp_out_b'], 'L3_ffn_tq_w': _L3_ffn_in['tq_w'], 'L3_ffn_tq_b': _L3_ffn_in['tq_b'], 'L3_ffn_tk_w': _L3_ffn_in['tk_w'], 'L3_ffn_tk_b': _L3_ffn_in['tk_b'], 'L3_ffn_tv_w': _L3_ffn_in['tv_w'], 'L3_ffn_tv_b': _L3_ffn_in['tv_b'], 'L3_ffn_tp_w': _L3_ffn_in['tp_w'], 'L3_ffn_tp_b': _L3_ffn_in['tp_b'], 'L3_ffn_cross_in_w': _L3_ffn_in['cross_in_w'], 'L3_ffn_cross_in_b': _L3_ffn_in['cross_in_b'], 'L3_ffn_cross_out_w': _L3_ffn_in['cross_out_w'], 'L3_ffn_cross_out_b': _L3_ffn_in['cross_out_b'], 'L3_ffn_norm_mlp_w': _L3_ffn_in['norm_mlp_w'], 'L3_ffn_norm_mlp_b': _L3_ffn_in['norm_mlp_b'], 'L3_ffn_mlp_w1': _L3_ffn_in['mlp_w1'], 'L3_ffn_mlp_b1': _L3_ffn_in['mlp_b1'], 'L3_ffn_mlp_w2': _L3_ffn_in['mlp_w2'], 'L3_ffn_mlp_b2': _L3_ffn_in['mlp_b2']}

def reference(x, L0_tok_emb_2, L0_tok_emb_3, L0_tok_emb_4, L0_tok_proj_w, L0_tok_proj_b, L0_attn_ln1_g, L0_attn_ln1_b, L0_attn_ln2_g, L0_attn_ln2_b, L0_attn_W_qkv, L0_attn_W_pos, L0_attn_W_out, L0_attn_b_out, L0_attn_pos_bias_u, L0_attn_pos_bias_v, L0_ffn_Wq, L0_ffn_Wgate, L0_ffn_Wk, L0_ffn_Wv, L0_ffn_Wb, L0_ffn_Wa, L0_ffn_A_log, L0_ffn_dt_bias, L0_ffn_Wg, L0_ffn_o_norm_weight, L0_ffn_Wo, L1_attn_W0, L1_attn_U0, L1_attn_b0, L1_attn_W1, L1_attn_U1, L1_attn_b1, L1_ffn_ln1_g, L1_ffn_ln1_b, L1_ffn_Wr, L1_ffn_codebook, L1_ffn_W1, L1_ffn_b1, L1_ffn_W2, L1_ffn_b2, L1_ffn_Ws1, L1_ffn_bs1, L1_ffn_Ws2, L1_ffn_bs2, L1_ffn_ffln_g, L1_ffn_ffln_b, L1_ffn_Wf1, L1_ffn_bf1, L1_ffn_Wf2, L1_ffn_bf2, L2_attn_W_qf, L2_attn_b_qf, L2_attn_W_kf, L2_attn_b_kf, L2_attn_W_vf, L2_attn_b_vf, L2_attn_W_qt, L2_attn_b_qt, L2_attn_W_kt, L2_attn_b_kt, L2_attn_W_vt, L2_attn_b_vt, L2_ffn_Wr, L2_ffn_br, L2_ffn_W1, L2_ffn_W2, L2_ffn_W3, L3_attn_in_proj_w, L3_attn_conv_w, L3_attn_conv_b, L3_attn_x_proj_w, L3_attn_dt_proj_w, L3_attn_dt_proj_b, L3_attn_A_log, L3_attn_D, L3_attn_out_proj_w, L3_attn_ln_gamma, L3_attn_ln_beta, L3_ffn_router_w1, L3_ffn_router_b1, L3_ffn_router_w2, L3_ffn_router_b2, L3_ffn_norm_s_w, L3_ffn_norm_s_b, L3_ffn_norm_t_w, L3_ffn_norm_t_b, L3_ffn_sp_in_w, L3_ffn_sp_in_b, L3_ffn_sp_out_w, L3_ffn_sp_out_b, L3_ffn_tq_w, L3_ffn_tq_b, L3_ffn_tk_w, L3_ffn_tk_b, L3_ffn_tv_w, L3_ffn_tv_b, L3_ffn_tp_w, L3_ffn_tp_b, L3_ffn_cross_in_w, L3_ffn_cross_in_b, L3_ffn_cross_out_w, L3_ffn_cross_out_b, L3_ffn_norm_mlp_w, L3_ffn_norm_mlp_b, L3_ffn_mlp_w1, L3_ffn_mlp_b1, L3_ffn_mlp_w2, L3_ffn_mlp_b2):
    import jax
    import jax.numpy as jnp

    def _L0_tok_ref(byte_sequence, emb_2, emb_3, emb_4, proj_w, proj_b):
        import jax, jax.numpy as jnp
        import numpy as np
        NGRAM_SIZES = (2, 3, 4)
        HASH_VOCAB = 25000
        EMBED_DIM = 128
        BATCH, SEQ = (8, 1024)

        def _ngram_hash_ids(byte_sequence, n):
            L = byte_sequence.shape[1] - n + 1
            h = jnp.zeros((byte_sequence.shape[0], L), dtype=jnp.int64)
            for j in range(n):
                h = (h * 64 + byte_sequence[:, j:j + L]) % HASH_VOCAB
            return h

        def _ngram_embed(byte_sequence, table, n):
            B, S = byte_sequence.shape
            ids = _ngram_hash_ids(byte_sequence, n)
            emb = table[ids]
            out = jnp.zeros((B, S, table.shape[1]), dtype=table.dtype)
            c = n // 2
            return out.at[:, c:c + emb.shape[1]].set(emb)
        tables = (emb_2, emb_3, emb_4)
        combined = jnp.concatenate([_ngram_embed(byte_sequence, t, n) for t, n in zip(tables, NGRAM_SIZES)], axis=-1)
        return jnp.einsum('bsk,dk->bsd', combined, proj_w) + proj_b

    def _L0_attn_ref(inputs, ln1_g, ln1_b, ln2_g, ln2_b, W_qkv, W_pos, W_out, b_out, pos_bias_u, pos_bias_v):
        import jax, jax.numpy as jnp
        import numpy as np
        B, T, D, H = (8, 256, 128, 8)
        DK = D // H

        def layer_norm(x, g, b, eps=1e-05):
            mu = jnp.mean(x, axis=-1, keepdims=True)
            var = jnp.var(x, axis=-1, keepdims=True)
            return (x - mu) * jax.lax.rsqrt(var + eps) * g + b

        def rel_shift(x):
            b, h, t1, t2 = x.shape
            xp = jnp.pad(x, ((0, 0), (0, 0), (0, 0), (1, 0)))
            xp = xp.reshape(b, h, t2 + 1, t1)[:, :, 1:, :]
            return xp.reshape(b, h, t1, t2)
        b, t, d = inputs.shape
        pos_seq = inputs[0, :, 0]
        inv_freq = 1.0 / 10000.0 ** (jnp.arange(0, d, 2, dtype=jnp.float32) / d)
        sin_inp = pos_seq[:, None] * inv_freq[None, :]
        pos_emb = jnp.concatenate([jnp.sin(sin_inp), jnp.cos(sin_inp)], axis=-1)
        x = layer_norm(inputs, ln1_g, ln1_b)
        xn = layer_norm(x, ln2_g, ln2_b)
        qkv = xn @ W_qkv.T
        q, k, v = jnp.split(qkv, 3, axis=-1)
        q = q.reshape(b, t, H, DK)
        k = k.reshape(b, t, H, DK).transpose(0, 2, 1, 3)
        v = v.reshape(b, t, H, DK).transpose(0, 2, 1, 3)
        p = (pos_emb @ W_pos.T).reshape(t, H, DK)
        qu = (q + pos_bias_u).transpose(0, 2, 1, 3)
        qv = (q + pos_bias_v).transpose(0, 2, 1, 3)
        ac = jnp.einsum('bhqd,bhkd->bhqk', qu, k)
        bd = jnp.einsum('bhqd,khd->bhqk', qv, p)
        bd = rel_shift(bd)
        scores = (ac + bd) / jnp.sqrt(jnp.float32(DK))
        attn = jax.nn.softmax(scores, axis=-1)
        out = jnp.einsum('bhqk,bhkd->bqhd', attn, v).reshape(b, t, d)
        return out @ W_out.T + b_out

    def _L0_ffn_ref(hidden_states, Wq, Wgate, Wk, Wv, Wb, Wa, A_log, dt_bias, Wg, o_norm_weight, Wo):
        import jax, jax.numpy as jnp
        import numpy as np
        E, TOPK, H, DK, DV, D = (4, 2, 8, 64, 64, 128)
        B, L = (4, 256)
        VDIM = H * DV

        def _silu(x):
            return x * jax.nn.sigmoid(x)

        def _l2norm(x):
            return x * jax.lax.rsqrt(jnp.sum(x * x, axis=-1, keepdims=True) + 1e-06)

        def _forward(h, Wq, Wgate, Wk, Wv, Wb, Wa, A_log, dt_bias, Wg, o_norm_weight, Wo):
            Bs, Ls, _ = h.shape
            scores = jax.nn.softmax((h @ Wgate).astype(jnp.float32), axis=-1)
            rw, sel = jax.lax.top_k(scores, TOPK)
            rw = rw / jnp.sum(rw, axis=-1, keepdims=True)
            bi = jnp.arange(Bs)[:, None, None]
            li = jnp.arange(Ls)[None, :, None]
            w_full = jnp.zeros((Bs, Ls, E), jnp.float32).at[bi, li, sel].set(rw)
            m = jnp.transpose(w_full > 0, (2, 0, 1))
            q = _l2norm(_silu(h @ Wq).reshape(Bs, Ls, H, DK))
            k = _l2norm(_silu(h @ Wk).reshape(Bs, Ls, H, DK))
            v = _silu(h @ Wv).reshape(Bs, Ls, H, DV)
            beta = jax.nn.sigmoid(h @ Wb)
            g = -jnp.exp(A_log) * jax.nn.softplus((h @ Wa).astype(jnp.float32) + dt_bias)
            beta_e = beta[None] * m[..., None]
            g_e = jnp.where(m[..., None], g[None], 0.0)
            scale = DK ** (-0.5)
            xs = (jnp.moveaxis(q, 1, 0), jnp.moveaxis(k, 1, 0), jnp.moveaxis(v, 1, 0), jnp.moveaxis(beta_e, 2, 0), jnp.moveaxis(g_e, 2, 0))

            def step(S, x):
                qt, kt, vt, bt, gt = x
                S = S * jnp.exp(gt)[..., None, None]
                kv = jnp.einsum('bhk,ebhkv->ebhv', kt, S)
                delta = (vt[None] - kv) * bt[..., None]
                S = S + kt[None, :, :, :, None] * delta[..., None, :]
                ot = jnp.einsum('bhk,ebhkv->ebhv', qt * scale, S)
                return (S, ot)
            S0 = jnp.zeros((E, Bs, H, DK, DV), jnp.float32)
            _, o = jax.lax.scan(step, S0, xs)
            o = jnp.moveaxis(o, 0, 2)
            core = jnp.einsum('ble,eblhv->blhv', w_full, o)
            gate = _silu((h @ Wg).reshape(Bs, Ls, H, DV))
            core = core * jax.lax.rsqrt(jnp.mean(core * core, axis=-1, keepdims=True) + 1e-05)
            core = core * o_norm_weight * gate
            return core.reshape(Bs, Ls, VDIM) @ Wo
        return _forward(hidden_states, Wq, Wgate, Wk, Wv, Wb, Wa, A_log, dt_bias, Wg, o_norm_weight, Wo)

    def _L1_attn_ref(inputs, W0, U0, b0, W1, U1, b1):
        import jax, jax.numpy as jnp
        import numpy as np
        B, T, D = (64, 128, 128)
        H = 256
        I = 128
        MASK_VALUE = 0.0

        def _lstm_layer(x, mask, W, U, b):
            Hd = U.shape[0]
            xz = jnp.einsum('btd,dk->btk', x, W) + b
            xz_t = jnp.transpose(xz, (1, 0, 2))
            mask_t = jnp.transpose(mask, (1, 0))

            def step(carry, inp):
                h, c = carry
                z_in, m = inp
                z = z_in + h @ U
                i, f, g, o = jnp.split(z, 4, axis=-1)
                i = jax.nn.sigmoid(i)
                f = jax.nn.sigmoid(f)
                g = jnp.tanh(g)
                o = jax.nn.sigmoid(o)
                c_new = f * c + i * g
                h_new = o * jnp.tanh(c_new)
                m2 = m[:, None]
                h = jnp.where(m2, h_new, h)
                c = jnp.where(m2, c_new, c)
                return ((h, c), h)
            h0 = jnp.zeros((x.shape[0], Hd), dtype=x.dtype)
            c0 = jnp.zeros((x.shape[0], Hd), dtype=x.dtype)
            (_, _), hs = jax.lax.scan(step, (h0, c0), (xz_t, mask_t))
            return jnp.transpose(hs, (1, 0, 2))
        mask = jnp.any(inputs != MASK_VALUE, axis=-1)
        x = _lstm_layer(inputs, mask, W0, U0, b0)
        latent = _lstm_layer(x, mask, W1, U1, b1)
        return latent

    def _L1_ffn_ref(x, ln1_g, ln1_b, Wr, codebook, W1, b1, W2, b2, Ws1, bs1, Ws2, bs2, ffln_g, ffln_b, Wf1, bf1, Wf2, bf2):
        import jax, jax.numpy as jnp
        import numpy as np
        D, E, DR, K, DFF, DSH = (128, 64, 64, 2, 512, 256)
        TEMP = 0.7
        SHARED_SCALE = 0.25
        EPS = 1e-05

        def _ln(x, g, b):
            m = jnp.mean(x, axis=-1, keepdims=True)
            v = jnp.mean(jnp.square(x - m), axis=-1, keepdims=True)
            return (x - m) * jax.lax.rsqrt(v + EPS) * g + b
        B, S, _ = x.shape
        T = B * S
        h = _ln(x, ln1_g, ln1_b).reshape(T, D)
        r = h @ Wr
        logits = r @ codebook.T / TEMP
        probs = jax.nn.softmax(logits, axis=-1)
        vals, idx = jax.lax.top_k(probs, K)
        w = vals / jnp.sum(vals, axis=-1, keepdims=True)
        combine = jnp.zeros((T, E), x.dtype).at[jnp.arange(T)[:, None], idx].set(w)
        eh = jax.nn.silu(jnp.einsum('td,edf->tef', h, W1) + b1)
        eo = jnp.einsum('tef,efd->ted', eh, W2) + b2
        moe = jnp.einsum('te,ted->td', combine, eo)
        shared = (jax.nn.silu(h @ Ws1 + bs1) @ Ws2 + bs2) * SHARED_SCALE
        hmoe = (moe + shared).reshape(B, S, D)
        f = _ln(hmoe, ffln_g, ffln_b)
        f = jax.nn.silu(f @ Wf1 + bf1) @ Wf2 + bf2
        return x + hmoe + f

    def _L2_attn_ref(x, W_qf, b_qf, W_kf, b_kf, W_vf, b_vf, W_qt, b_qt, W_kt, b_kt, W_vt, b_vt):
        import jax, jax.numpy as jnp
        import numpy as np
        B, T, D = (8, 128, 128)
        lin = lambda h, W, b: jnp.einsum('bti,oi->bto', h, W) + b
        Q_f = lin(x, W_qf, b_qf)
        K_f = lin(x, W_kf, b_kf)
        V_f = lin(x, W_vf, b_vf)
        ctx_f = jax.nn.softmax(Q_f * K_f, axis=-1) * V_f
        Q_t = lin(x, W_qt, b_qt)
        K_t = lin(x, W_kt, b_kt)
        V_t = lin(x, W_vt, b_vt)
        scores_t = jnp.einsum('bti,btj->btij', Q_t, K_t)
        probs_t = jax.nn.softmax(scores_t, axis=-1)
        ctx_t = jnp.einsum('btij,btj->bti', probs_t, V_t)
        return ctx_f + ctx_t

    def _L2_ffn_ref(x, Wr, br, W1, W2, W3):
        import jax, jax.numpy as jnp
        import numpy as np
        import math
        B, T, D, H, E, TOPK = (8, 1024, 128, 512, 8, 2)
        CAP_FRAC = 1.0

        def _expert_ffn(x, w1, w2, w3):
            h = jax.nn.gelu(x @ w2 * (x @ w1), approximate=False)
            return h @ w3
        b, t, d = x.shape
        Bt = b * t
        x_flat = x.reshape(Bt, d)
        logits = x_flat.astype(jnp.float32) @ Wr + br
        vals, idx = jax.lax.top_k(logits, TOPK)
        scores = jax.nn.softmax(vals, axis=-1).astype(x.dtype).reshape(b, t, TOPK)
        onehot = jax.nn.one_hot(idx, E, dtype=jnp.float32)
        pos = jnp.cumsum(jnp.cumsum(onehot, axis=0), axis=1).astype(jnp.int32)
        capacity = math.floor(Bt * CAP_FRAC)
        mask3 = onehot * (pos < capacity)
        token_mask = mask3.sum(-1).reshape(b, t, TOPK)
        assign = jnp.einsum('tke,e->tk', mask3, jnp.arange(E, dtype=jnp.float32)).astype(jnp.int32)
        i_max = assign.reshape(b, t, TOPK).max(axis=-1)
        y = jnp.zeros_like(x)
        for i in range(E):
            yi = _expert_ffn(x, W1[i], W2[i], W3[i])
            y = jnp.where((i_max == i)[..., None], yi, y)
        expert_outputs = jnp.where(token_mask[..., None] > 0, y[:, :, None, :], x[:, :, None, :])
        return jnp.einsum('btkD,btk->btD', expert_outputs, scores)

    def _L3_attn_ref(input_tensor, in_proj_w, conv_w, conv_b, x_proj_w, dt_proj_w, dt_proj_b, A_log, D, out_proj_w, ln_gamma, ln_beta):
        import jax, jax.numpy as jnp
        import numpy as np
        D_MODEL = 128
        D_STATE = 16
        D_CONV = 4
        EXPAND = 2
        D_INNER = EXPAND * D_MODEL
        DT_RANK = (D_MODEL + 15) // 16
        BATCH, SEQ = (16, 512)
        LN_EPS = 1e-12

        def _selective_scan(u, dt, A, Bm, C, D):
            h0 = jnp.zeros((u.shape[0], u.shape[2], A.shape[1]), u.dtype)

            def step(h, inp):
                dt_t, B_t, u_t, C_t = inp
                dA = jnp.exp(dt_t[..., None] * A)
                h = dA * h + (dt_t * u_t)[..., None] * B_t[:, None, :]
                y = jnp.einsum('bdn,bn->bd', h, C_t)
                return (h, y)
            tswap = lambda x: jnp.swapaxes(x, 0, 1)
            _, ys = jax.lax.scan(step, h0, (tswap(dt), tswap(Bm), tswap(u), tswap(C)))
            return jnp.swapaxes(ys, 0, 1) + u * D

        def _mamba(x, in_proj_w, conv_w, conv_b, x_proj_w, dt_proj_w, dt_proj_b, A_log, D, out_proj_w):
            L = x.shape[1]
            xz = jnp.einsum('bld,ed->ble', x, in_proj_w)
            xc, z = jnp.split(xz, 2, axis=-1)
            P = D_CONV - 1
            xp = jnp.pad(xc, ((0, 0), (P, 0), (0, 0)))
            xconv = conv_b + sum((xp[:, k:k + L, :] * conv_w[:, k] for k in range(D_CONV)))
            xa = jax.nn.silu(xconv)
            dbl = jnp.einsum('bld,ed->ble', xa, x_proj_w)
            dt = jax.nn.softplus(jnp.einsum('blr,dr->bld', dbl[..., :DT_RANK], dt_proj_w) + dt_proj_b)
            Bm = dbl[..., DT_RANK:DT_RANK + D_STATE]
            C = dbl[..., DT_RANK + D_STATE:]
            A = -jnp.exp(A_log)
            y = _selective_scan(xa, dt, A, Bm, C, D)
            y = y * jax.nn.silu(z)
            return jnp.einsum('ble,de->bld', y, out_proj_w)
        h = _mamba(input_tensor, in_proj_w, conv_w, conv_b, x_proj_w, dt_proj_w, dt_proj_b, A_log, D, out_proj_w)
        r = h + input_tensor
        mu = jnp.mean(r, axis=-1, keepdims=True)
        var = jnp.mean(jnp.square(r - mu), axis=-1, keepdims=True)
        return (r - mu) * jax.lax.rsqrt(var + LN_EPS) * ln_gamma + ln_beta

    def _L3_ffn_ref(x, router_w1, router_b1, router_w2, router_b2, norm_s_w, norm_s_b, norm_t_w, norm_t_b, sp_in_w, sp_in_b, sp_out_w, sp_out_b, tq_w, tq_b, tk_w, tk_b, tv_w, tv_b, tp_w, tp_b, cross_in_w, cross_in_b, cross_out_w, cross_out_b, norm_mlp_w, norm_mlp_b, mlp_w1, mlp_b1, mlp_w2, mlp_b2):
        import jax, jax.numpy as jnp
        import numpy as np
        D = 128
        H = 8
        K = 4
        HD = D // H

        def _ln(x, w, b, eps=1e-05):
            m = x.mean(-1, keepdims=True)
            v = ((x - m) ** 2).mean(-1, keepdims=True)
            return (x - m) / jnp.sqrt(v + eps) * w + b

        def _spatial_experts(xn, idx, in_w, in_b, out_w, out_b):
            W = in_w[idx]
            qkv = jnp.einsum('btd,bed->bte', xn, W) + in_b[idx][:, None, :]
            q, k, v = jnp.split(qkv, 3, axis=-1)
            B, T, _ = xn.shape
            q = q.reshape(B, T, H, HD) * HD ** (-0.5)
            k = k.reshape(B, T, H, HD)
            v = v.reshape(B, T, H, HD)
            att = jax.nn.softmax(jnp.einsum('bthd,bshd->bhts', q, k), axis=-1)
            o = jnp.einsum('bhts,bshd->bthd', att, v).reshape(B, T, D)
            return jnp.einsum('btd,bod->bto', o, out_w[idx]) + out_b[idx][:, None, :]

        def _temporal_experts(xt, idx, qw, qb, kw, kb, vw, vb, pw, pb):
            B, T, _ = xt.shape
            q = (jnp.einsum('btd,bod->bto', xt, qw[idx]) + qb[idx][:, None, :]).reshape(B, T, H, HD)
            k = (jnp.einsum('btd,bod->bto', xt, kw[idx]) + kb[idx][:, None, :]).reshape(B, T, H, HD)
            v = (jnp.einsum('btd,bod->bto', xt, vw[idx]) + vb[idx][:, None, :]).reshape(B, T, H, HD)
            logits = jnp.einsum('bthd,bshd->bhts', q, k) * HD ** (-0.5)
            causal = jnp.tril(jnp.ones((T, T), dtype=bool))
            logits = jnp.where(causal, logits, -jnp.inf)
            att = jax.nn.softmax(logits, axis=-1)
            o = jnp.einsum('bhts,bshd->bthd', att, v).reshape(B, T, D)
            o = jnp.einsum('btd,bod->bto', o, pw[idx]) + pb[idx][:, None, :]
            return xt + o

        def _cross_mha(q_in, kv_in, in_w, in_b, out_w, out_b):
            B, T, _ = q_in.shape
            S = kv_in.shape[1]
            Wq, Wk, Wv = (in_w[:D], in_w[D:2 * D], in_w[2 * D:])
            bq, bk, bv = (in_b[:D], in_b[D:2 * D], in_b[2 * D:])
            q = (q_in @ Wq.T + bq).reshape(B, T, H, HD) * HD ** (-0.5)
            k = (kv_in @ Wk.T + bk).reshape(B, S, H, HD)
            v = (kv_in @ Wv.T + bv).reshape(B, S, H, HD)
            att = jax.nn.softmax(jnp.einsum('bthd,bshd->bhts', q, k), axis=-1)
            o = jnp.einsum('bhts,bshd->bthd', att, v).reshape(B, T, D)
            return o @ out_w.T + out_b
        pooled = x.mean(axis=1)
        h = jax.nn.gelu(pooled @ router_w1.T + router_b1, approximate=False)
        route = jax.nn.softmax(h @ router_w2.T + router_b2, axis=-1)
        idx_s = jnp.argmax(route[:, :K], axis=-1)
        idx_t = jnp.argmax(route[:, K:], axis=-1)
        xn = _ln(x, norm_s_w, norm_s_b)
        spatial_out = _spatial_experts(xn, idx_s, sp_in_w, sp_in_b, sp_out_w, sp_out_b)
        xt = _ln(x, norm_t_w, norm_t_b)
        temporal_out = _temporal_experts(xt, idx_t, tq_w, tq_b, tk_w, tk_b, tv_w, tv_b, tp_w, tp_b)
        fused = _cross_mha(spatial_out, temporal_out, cross_in_w, cross_in_b, cross_out_w, cross_out_b)
        x = x + fused
        h2 = _ln(x, norm_mlp_w, norm_mlp_b)
        x = x + (jax.nn.gelu(h2 @ mlp_w1.T + mlp_b1, approximate=False) @ mlp_w2.T + mlp_b2)
        return x
    h = _L0_tok_ref(x, L0_tok_emb_2, L0_tok_emb_3, L0_tok_emb_4, L0_tok_proj_w, L0_tok_proj_b)
    h = h + _L0_attn_ref(_layernorm(h, axis=-1), L0_attn_ln1_g, L0_attn_ln1_b, L0_attn_ln2_g, L0_attn_ln2_b, L0_attn_W_qkv, L0_attn_W_pos, L0_attn_W_out, L0_attn_b_out, L0_attn_pos_bias_u, L0_attn_pos_bias_v)
    h = h + _L0_ffn_ref(_layernorm(h, axis=-1), L0_ffn_Wq, L0_ffn_Wgate, L0_ffn_Wk, L0_ffn_Wv, L0_ffn_Wb, L0_ffn_Wa, L0_ffn_A_log, L0_ffn_dt_bias, L0_ffn_Wg, L0_ffn_o_norm_weight, L0_ffn_Wo)
    h = h + _L1_attn_ref(_layernorm(h, axis=-1), L1_attn_W0, L1_attn_U0, L1_attn_b0, L1_attn_W1, L1_attn_U1, L1_attn_b1)
    h = h + _L1_ffn_ref(_layernorm(h, axis=-1), L1_ffn_ln1_g, L1_ffn_ln1_b, L1_ffn_Wr, L1_ffn_codebook, L1_ffn_W1, L1_ffn_b1, L1_ffn_W2, L1_ffn_b2, L1_ffn_Ws1, L1_ffn_bs1, L1_ffn_Ws2, L1_ffn_bs2, L1_ffn_ffln_g, L1_ffn_ffln_b, L1_ffn_Wf1, L1_ffn_bf1, L1_ffn_Wf2, L1_ffn_bf2)
    h = h + _L2_attn_ref(_layernorm(h, axis=-1), L2_attn_W_qf, L2_attn_b_qf, L2_attn_W_kf, L2_attn_b_kf, L2_attn_W_vf, L2_attn_b_vf, L2_attn_W_qt, L2_attn_b_qt, L2_attn_W_kt, L2_attn_b_kt, L2_attn_W_vt, L2_attn_b_vt)
    h = h + _L2_ffn_ref(_layernorm(h, axis=-1), L2_ffn_Wr, L2_ffn_br, L2_ffn_W1, L2_ffn_W2, L2_ffn_W3)
    h = h + _L3_attn_ref(_layernorm(h, axis=-1), L3_attn_in_proj_w, L3_attn_conv_w, L3_attn_conv_b, L3_attn_x_proj_w, L3_attn_dt_proj_w, L3_attn_dt_proj_b, L3_attn_A_log, L3_attn_D, L3_attn_out_proj_w, L3_attn_ln_gamma, L3_attn_ln_beta)
    h = h + _L3_ffn_ref(_layernorm(h, axis=-1), L3_ffn_router_w1, L3_ffn_router_b1, L3_ffn_router_w2, L3_ffn_router_b2, L3_ffn_norm_s_w, L3_ffn_norm_s_b, L3_ffn_norm_t_w, L3_ffn_norm_t_b, L3_ffn_sp_in_w, L3_ffn_sp_in_b, L3_ffn_sp_out_w, L3_ffn_sp_out_b, L3_ffn_tq_w, L3_ffn_tq_b, L3_ffn_tk_w, L3_ffn_tk_b, L3_ffn_tv_w, L3_ffn_tv_b, L3_ffn_tp_w, L3_ffn_tp_b, L3_ffn_cross_in_w, L3_ffn_cross_in_b, L3_ffn_cross_out_w, L3_ffn_cross_out_b, L3_ffn_norm_mlp_w, L3_ffn_norm_mlp_b, L3_ffn_mlp_w1, L3_ffn_mlp_b1, L3_ffn_mlp_w2, L3_ffn_mlp_b2)
    return h

_drawn_inputs = setup_inputs


def setup_inputs(seed=0):
    import zlib

    import numpy as np

    out = dict(_drawn_inputs(seed))
    spreads = {'L0_attn_ln1_g': (1.0, 0.6),
     'L0_attn_ln1_b': (0.0, 0.492),
     'L0_attn_ln2_g': (1.0, 0.6),
     'L0_attn_ln2_b': (0.0, 0.402),
     'L0_attn_b_out': (0.0, 0.1),
     'L0_ffn_o_norm_weight': (1.0, 0.6),
     'L1_attn_b0': (0.0, 0.1),
     'L1_attn_b1': (0.0, 0.1),
     'L1_ffn_ln1_g': (1.0, 0.2),
     'L1_ffn_ln1_b': (0.0, 0.279),
     'L1_ffn_b1': (0.0, 0.529),
     'L1_ffn_b2': (0.0, 0.1),
     'L1_ffn_bs1': (0.0, 0.8),
     'L1_ffn_bs2': (0.0, 0.41),
     'L1_ffn_ffln_g': (1.0, 0.6),
     'L1_ffn_ffln_b': (0.0, 0.8),
     'L1_ffn_bf1': (0.0, 0.452),
     'L1_ffn_bf2': (0.0, 0.1),
     'L2_ffn_br': (0.0, 0.8),
     'L3_attn_conv_b': (0.0, 0.512),
     'L3_attn_dt_proj_b': (-4.600165843963623, 0.6),
     'L3_attn_D': (1.0, 0.6),
     'L3_attn_ln_gamma': (1.0, 0.2),
     'L3_attn_ln_beta': (0.0, 0.1),
     'L3_ffn_router_b1': (0.0, 0.1),
     'L3_ffn_router_b2': (0.0, 0.8),
     'L3_ffn_norm_s_w': (1.0, 0.6),
     'L3_ffn_norm_s_b': (0.0, 0.8),
     'L3_ffn_norm_t_w': (1.0, 0.6),
     'L3_ffn_norm_t_b': (0.0, 0.8),
     'L3_ffn_sp_in_b': (0.0, 0.8),
     'L3_ffn_sp_out_b': (0.0, 0.8),
     'L3_ffn_tq_b': (0.0, 0.8),
     'L3_ffn_tk_b': (0.0, 2.0),
     'L3_ffn_tv_b': (0.0, 0.8),
     'L3_ffn_tp_b': (0.0, 0.8),
     'L3_ffn_cross_in_b': (0.0, 0.8),
     'L3_ffn_cross_out_b': (0.0, 1.487),
     'L3_ffn_norm_mlp_w': (1.0, 0.6),
     'L3_ffn_norm_mlp_b': (0.0, 0.8),
     'L3_ffn_mlp_b1': (0.0, 0.8),
     'L3_ffn_mlp_b2': (0.0, 0.8)}
    factors = {'L0_attn_W_pos': 8.0,
     'L0_attn_pos_bias_u': 8.0,
     'L0_attn_pos_bias_v': 8.0,
     'L0_ffn_Wb': 6.537,
     'L0_ffn_Wa': 8.0,
     'L0_ffn_A_log': 3.487,
     'L1_ffn_Ws1': 7.48,
     'L1_ffn_Ws2': 7.044,
     'L2_attn_W_qf': 8.0,
     'L2_attn_b_qf': 8.0,
     'L2_attn_W_kf': 8.0,
     'L2_attn_b_kf': 8.0,
     'L2_attn_W_vf': 8.0,
     'L2_attn_b_vf': 8.0,
     'L2_attn_W_qt': 4.486,
     'L2_attn_b_qt': 8.0,
     'L2_attn_W_kt': 4.487,
     'L2_attn_b_kt': 8.0,
     'L2_attn_W_vt': 3.039,
     'L2_attn_b_vt': 8.0,
     'L2_ffn_Wr': 7.506,
     'L2_ffn_W1': 6.823,
     'L2_ffn_W2': 6.797,
     'L2_ffn_W3': 6.81,
     'L3_attn_x_proj_w': 3.921,
     'L3_attn_dt_proj_w': 8.0,
     'L3_attn_A_log': 3.982,
     'L3_ffn_sp_in_w': 8.0,
     'L3_ffn_sp_out_w': 8.0,
     'L3_ffn_tq_w': 8.0,
     'L3_ffn_tk_w': 8.0,
     'L3_ffn_tv_w': 8.0,
     'L3_ffn_tp_w': 8.0,
     'L3_ffn_cross_in_w': 8.0,
     'L3_ffn_cross_out_w': 6.962,
     'L3_ffn_mlp_w1': 3.354,
     'L3_ffn_mlp_w2': 3.117}
    for name, (base, spread) in spreads.items():
        noise = np.random.default_rng([zlib.crc32(name.encode()), seed]).standard_normal(out[name].shape)
        drawn = base * np.exp(spread * noise) if base else spread * noise
        out[name] = jnp.asarray(drawn.astype(out[name].dtype))
    for name, factor in factors.items():
        out[name] = (out[name] * factor).astype(out[name].dtype)
    return out
```

```python
from contextlib import ExitStack

import numpy as np

import concourse.bass as bass
from concourse import mybir

F32 = mybir.dt.float32
BF16 = mybir.dt.bfloat16
I32 = mybir.dt.int32
U32 = mybir.dt.uint32
ACT = mybir.ActivationFunctionType
ALU = mybir.AluOpType
AX = mybir.AxisListType

P = 128
B = 16
T = 128
D = 128
N = B * T
BANK = 512
NEVER = -1e30


class Stage:

    def __init__(self, nc, name):
        self.nc, self.name, self.stack, self.sems = nc, name, ExitStack(), []

    def __enter__(self):
        return self

    def sb(self, name, shape, dt=F32):
        return self.stack.enter_context(self.nc.sbuf_tensor(f"s_{self.name}_{name}", shape, dt))

    def ps(self, name, shape, dt=F32):
        return self.stack.enter_context(self.nc.psum_tensor(f"p_{self.name}_{name}", shape, dt))

    def sem(self, name):
        s = self.nc.alloc_semaphore(f"{self.name}_{name}")
        self.sems.append(s)
        return s

    def pair(self, name):
        return [self.sem(f"{name}{p}") for p in range(2)]

    def start_at_one(self, *sems):
        for sem in sems:
            self.nc.sync.sem_inc(sem, 1)

    def __exit__(self, kind, e, trace):
        if kind is None:
            self.stack.close()
            self.nc.clear_and_free_semaphores(self.sems)
            self.nc.all_engine_barrier()
        return False


class Link:

    def __init__(self, eng, sem, base=0):
        self.eng, self.sem, self.base, self.n = eng, sem, base, 0

    def __call__(self, ins):
        self.n += 1
        ins.then_inc(self.sem, 1)
        self.eng.wait_ge(self.sem, self.base + self.n)


def log1p(link, dve, x, ratio, square):
    link(dve.tensor_scalar(ratio, x, 2.0, None, ALU.add))
    link(dve.reciprocal(ratio, ratio))
    link(dve.tensor_tensor(ratio, x, ratio, ALU.mult))
    link(dve.tensor_tensor(square, ratio, ratio, ALU.mult))
    link(dve.tensor_scalar(x, square, 1.0 / 15, None, ALU.mult))
    for k in (13, 11, 9, 7, 5, 3):
        link(dve.scalar_tensor_tensor(x, x, 1.0 / k, square, ALU.add, ALU.mult))
    link(dve.scalar_tensor_tensor(x, x, 1.0, ratio, ALU.add, ALU.mult))
    link(dve.tensor_scalar(x, x, 2.0, None, ALU.mult))


def flat(x3):
    return x3.rearrange("p b d -> p (b d)")


def over_last(col, n):
    return col.unsqueeze(2).to_broadcast([col.shape[0], col.shape[1], n])


def over_mid(row, n):
    return row.unsqueeze(1).to_broadcast([row.shape[0], n, row.shape[1]])


def layer_norm(nc, name, src, dst, eps, rows=None):
    with Stage(nc, name) as s:
        total, mean, var, dev, inv = (s.sb(n, [P, B]) for n in ("total", "mean", "var", "dev", "inv"))
        square = s.sb("square", [P, B, D])
        affine = s.sb("affine", [P, 2, D])
        epscol = s.sb("epscol", [P, 1])
        centred, var_ready, dev_ready, dve_step, squared, rows_in = (
            s.sem(n) for n in ("centred", "var_ready", "dev_ready", "dve_step", "squared", "rows_in"))
        with nc.Block() as block:
            if rows is not None:
                @block.sync
                def _(sp):
                    sp.dma_start(affine[:], rows.partition_broadcast(P)).then_inc(rows_in, 16)

            @block.vector
            def _(dve):
                link = Link(dve, dve_step)
                link(dve.memset(epscol[:], eps))
                link(dve.tensor_reduce(total[:], src, AX.X, ALU.add))
                link(dve.tensor_scalar(mean[:], total[:], 1.0 / D, None, ALU.mult))
                dve.tensor_tensor(dst, src, over_last(mean[:], D), ALU.subtract).then_inc(centred, 1)
                dve.wait_ge(squared, 1)
                link(dve.tensor_reduce(total[:], square[:], AX.X, ALU.add))
                dve.tensor_scalar(var[:], total[:], 1.0 / D, None, ALU.mult).then_inc(var_ready, 1)
                dve.wait_ge(dev_ready, 1)
                link(dve.reciprocal(inv[:], dev[:]))
                link(dve.tensor_tensor(dst, dst, over_last(inv[:], D), ALU.mult))
                if rows is not None:
                    dve.wait_ge(rows_in, 16)
                    link(dve.tensor_tensor(dst, dst, over_mid(affine[:, 0, :], B), ALU.mult))
                    link(dve.tensor_tensor(dst, dst, over_mid(affine[:, 1, :], B), ALU.add))

            @block.scalar
            def _(act):
                act.wait_ge(centred, 1)
                act.activation(square[:], dst, ACT.Square).then_inc(squared, 1)
                act.wait_ge(var_ready, 1)
                act.activation(dev[:], var[:], ACT.Sqrt, bias=epscol[:]).then_inc(dev_ready, 1)


def to_features(nc, name, core, src, dst):
    with Stage(nc, name) as s:
        banks = [s.ps(f"turned{i}", [P, BANK]) for i in range(4)]
        turned, copied = s.sem("turned"), s.sem("copied")
        with nc.Block() as block:
            @block.tensor
            def _(pe):
                for g in range(4):
                    for k in range(4):
                        mm = pe.transpose(banks[g][:, k * P:(k + 1) * P], src[:, 4 * g + k, :], core.ident[:])
                    mm.then_inc(turned, 1)

            @block.vector
            def _(dve):
                for g in (0, 2):
                    dve.wait_ge(turned, g + 1)
                    dve.tensor_copy(dst[:, g * BANK:(g + 1) * BANK], banks[g][:]).then_inc(copied, 1)
                dve.wait_ge(copied, 4)

            @block.scalar
            def _(act):
                for g in (1, 3):
                    act.wait_ge(turned, g + 1)
                    act.activation(dst[:, g * BANK:(g + 1) * BANK], banks[g][:], ACT.Copy).then_inc(copied, 1)


def add_features(nc, name, core, srcT, dst):
    with Stage(nc, name) as s:
        banks = [s.ps(f"turned{i}", [P, BANK]) for i in range(4)]
        turned, added = s.sem("turned"), s.sem("added")
        with nc.Block() as block:
            @block.tensor
            def _(pe):
                for g in range(4):
                    for k in range(4):
                        b = 4 * g + k
                        mm = pe.transpose(banks[g][:, k * P:(k + 1) * P], srcT[:, b * T:(b + 1) * T], core.ident[:])
                    mm.then_inc(turned, 1)

            @block.vector
            def _(dve):
                for g in range(4):
                    dve.wait_ge(turned, g + 1)
                    part = flat(dst)[:, g * BANK:(g + 1) * BANK]
                    dve.tensor_tensor(part, part, banks[g][:], ALU.add).then_inc(added, 1)
                dve.wait_ge(added, 4)


class Core:
    pass


def tokens(nc, core, d):
    VOCAB, SHIFT = 25000, 64.0
    with Stage(nc, "tok") as s:
        raw = s.sb("raw", [P, 4, B], I32)
        byte = s.sb("byte", [P, 4, B])
        hashed = s.sb("hashed", [P, B])
        quotient = s.sb("quotient", [P, B])
        whole = s.sb("whole", [P, B], I32)
        over = s.sb("over", [P, B])
        ids = s.sb("ids", [P, 3, B], U32)
        inside = s.sb("inside", [P, 3])
        emb = s.sb("emb", [P, B, 3, D])
        stage = [s.sb(f"stage{p}", [P, 3, D]) for p in range(2)]
        embT = [s.sb(f"embT{p}", [P, 3, T]) for p in range(2)]
        w = s.sb("w", [P, 3, D])
        brow = s.sb("brow", [P, D])
        turn = [s.ps(f"turn{p}", [P, BANK]) for p in range(2)]
        proj = [s.ps(f"proj{p}", [P, BANK]) for p in range(2)]
        loaded, dve_step, ids_ready = s.sem("loaded"), s.sem("dve_step"), s.sem("ids_ready")
        gathered = [s.sem(f"gathered{b}") for b in range(B)]
        masked, turned, copied, projected, added = (s.pair(n) for n in (
            "masked", "turned", "copied", "projected", "added"))
        s.start_at_one(*turned, *copied, *added)
        with nc.Block() as block:
            @block.sync
            def _(sp):
                sp.dma_start(raw[:], d["x_windows"]).then_inc(loaded, 16)
                sp.dma_start(inside[:], d["inside"]).then_inc(loaded, 16)
                sp.dma_start(w[:], d["tok_w"]).then_inc(loaded, 16)
                sp.dma_start(brow[:], d["tok_b"].partition_broadcast(P)).then_inc(loaded, 16)
                sp.dma_start(core.ident[:], d["ident"]).then_inc(loaded, 16)

            @block.gpsimd
            def _(pool):
                pool.wait_ge(ids_ready, 3)
                for b in range(B):
                    for n in range(3):
                        pool.indirect_dma_start(emb[:, b, n, :], None, d[f"L0_tok_emb_{n + 2}"],
                                                bass.IndirectOffsetOnAxis(ap=ids[:, n, b:b + 1], axis=0))\
                            .then_inc(gathered[b], 16)

            @block.vector
            def _(dve):
                link = Link(dve, dve_step)
                dve.wait_ge(loaded, 80)
                link(dve.tensor_copy(byte[:], raw[:]))
                for n in range(3):
                    first = (1, 1, 0)[n]
                    link(dve.tensor_copy(hashed[:], byte[:, first, :]))
                    for k in range(1, n + 2):
                        link(dve.scalar_tensor_tensor(hashed[:], hashed[:], SHIFT, byte[:, first + k, :],
                                                      ALU.mult, ALU.add))
                        link(dve.tensor_scalar(quotient[:], hashed[:], 1.0 / VOCAB, None, ALU.mult))
                        link(dve.tensor_copy(whole[:], quotient[:]))
                        link(dve.tensor_copy(quotient[:], whole[:]))
                        link(dve.scalar_tensor_tensor(hashed[:], quotient[:], -float(VOCAB), hashed[:],
                                                      ALU.mult, ALU.add))
                        link(dve.tensor_scalar(over[:], hashed[:], 0.0, float(VOCAB), ALU.is_lt, ALU.mult))
                        link(dve.tensor_tensor(hashed[:], hashed[:], over[:], ALU.add))
                        link(dve.tensor_scalar(over[:], hashed[:], float(VOCAB), -float(VOCAB), ALU.is_ge, ALU.mult))
                        link(dve.tensor_tensor(hashed[:], hashed[:], over[:], ALU.add))
                    dve.tensor_copy(ids[:, n, :], hashed[:]).then_inc(ids_ready, 1)
                    dve.wait_ge(ids_ready, n + 1)
                with dve.Fori(0, B // 2) as j:
                    for p in range(2):
                        dve.wait_ge(turned[p], j + 2)
                        dve.tensor_copy(embT[p][:].rearrange("p a b -> p (a b)"), turn[p][:, 0:3 * T])\
                            .then_inc(copied[p], 1)
                    for p in range(2):
                        dve.wait_ge(projected[p], j + 1)
                        dve.tensor_tensor(flat(core.h[:])[:, bass.ds((2 * j + p) * D, D)], proj[p][:, 0:D], brow[:],
                                          ALU.add).then_inc(added[p], 1)
                for p in range(2):
                    dve.wait_ge(added[p], B // 2 + 1)

            @block.scalar
            def _(act):
                act.wait_ge(loaded, 80)
                for b in range(B):
                    act.wait_ge(gathered[b], 48)
                with act.Fori(0, B // 2) as j:
                    for p in range(2):
                        act.wait_ge(turned[p], j + 1)
                        for n in range(3):
                            ins = act.activation(
                                stage[p][:, n, :],
                                emb[:].rearrange("p b n d -> p (b n d)")[:, bass.ds((2 * j + p) * 3 * D + n * D, D)],
                                ACT.Copy, scale=inside[:, n:n + 1])
                        ins.then_inc(masked[p], 1)

            @block.tensor
            def _(pe):
                with pe.Fori(0, B // 2) as j:
                    for p in range(2):
                        pe.wait_ge(masked[p], j + 1)
                        pe.wait_ge(copied[p], j + 1)
                        for n in range(3):
                            mm = pe.transpose(turn[p][:, n * T:(n + 1) * T], stage[p][:, n, :], core.ident[:])
                        mm.then_inc(turned[p], 1)
                    for p in range(2):
                        pe.wait_ge(copied[p], j + 2)
                        pe.wait_ge(added[p], j + 1)
                        for n in range(3):
                            mm = pe.matmul(proj[p][:, 0:D], embT[p][:, n, :], w[:, n, :], start=(n == 0), stop=(n == 2))
                        mm.then_inc(projected[p], 1)


H, HD = 8, 16
HT = H * T


def attention(nc, name, core, xq, xkv, out, w_dram, b_dram, choice=None, causal=False, keep=False, shifted=None):
    routed = choice is not None
    with Stage(nc, name) as s:
        mask = s.sb("mask", [P, H])
        tri = s.sb("tri", [P, T])

        def two(n, shape, dt=F32):
            return [s.sb(f"{n}{p}", shape, dt) for p in range(2)]

        w, bias = two("w", [P, 4 * D]), two("bias", [P, 4])
        xq_s, xkv_s, qT, kT, v = (two(n, [P, T]) for n in ("xq_s", "xkv_s", "qT", "kT", "v"))
        keys, score, probs, probsT = (two(n, [P, H, T]) for n in ("keys", "score", "probs", "probsT"))
        top, mass, inv = (two(n, [P, H]) for n in ("top", "mass", "inv"))
        o, oT, pos = two("o", [P, D]), two("oT", [P, T]), two("pos", [P, H, T])
        small = [s.ps(f"small{p}", [P, BANK]) for p in range(2)]
        qkv = [s.ps(f"qkv{p}", [P, BANK]) for p in range(2)]
        wide = [s.ps(f"wide{p}", [P, HT]) for p in range(2)]
        const_in = s.sem("const_in")
        (x_in, w_in, projected, qk_ready, v_ready, keys_ready, scored, pos_in, lowered, exp_ready, inv_ready,
         turned, turned_a, turned_b, attended, o_ready, o_turned, oT_ready, y_ready, batch_done, dve_step) = (
            s.pair(n) for n in (
                "x_in", "w_in", "projected", "qk_ready", "v_ready", "keys_ready", "scored", "pos_in", "lowered",
                "exp_ready", "inv_ready", "turned", "turned_a", "turned_b", "attended", "o_ready", "o_turned",
                "oT_ready", "y_ready", "batch_done", "dve_step"))
        s.start_at_one(*batch_done)
        with nc.Block() as block:
            @block.sync
            def _(sp):
                sp.dma_start(mask[:], core.d["head_mask"]).then_inc(const_in, 16)
                sp.dma_start(tri[:], core.d["causal"]).then_inc(const_in, 16)
                if not routed:
                    for p in range(2):
                        sp.dma_start(w[p][:], w_dram).then_inc(w_in[p], 16)
                        sp.dma_start(bias[p][:], b_dram).then_inc(w_in[p], 16)
                if routed or shifted is not None:
                    with sp.Fori(0, B // 2) as j:
                        for p in range(2):
                            sp.wait_ge(batch_done[p], j + 1)
                            if routed:
                                e = sp.value_load(choice[0][0:1, bass.ds((2 * j + p) * 2 + choice[1], 1)], min_val=0, max_val=3)
                                sp.dma_start(w[p][:], w_dram[bass.ds(e, 1), :, :].rearrange("e p n -> p (e n)"))\
                                    .then_inc(w_in[p], 16)
                                sp.dma_start(bias[p][:], b_dram[bass.ds(e, 1), :, :].rearrange("e p n -> p (e n)"))\
                                    .then_inc(w_in[p], 16)
                            if shifted is not None:
                                sp.dma_start(pos[p][:], shifted[bass.ds(2 * j + p, 1), :, T:T + T * T].rearrange(
                                    "b h (q k) -> q (b h) k", k=T)).then_inc(pos_in[p], 16)

            @block.scalar
            def _(act):
                with act.Fori(0, B // 2) as j:
                    for p in range(2):
                        act.wait_ge(batch_done[p], j + 1)
                        act.activation(xq_s[p][:], xq[:, bass.ds((2 * j + p) * T, T)], ACT.Copy).then_inc(x_in[p], 1)
                        act.activation(xkv_s[p][:], xkv[:, bass.ds((2 * j + p) * T, T)], ACT.Copy).then_inc(x_in[p], 1)
                    for p in range(2):
                        act.wait_ge(projected[p], j + 1)
                        act.activation(qT[p][:], qkv[p][:, 0:T], ACT.Identity, bias=bias[p][:, 0:1]).then_inc(qk_ready[p], 1)
                        act.activation(kT[p][:], qkv[p][:, T:2 * T], ACT.Identity, bias=bias[p][:, 1:2])\
                            .then_inc(qk_ready[p], 1)
                        act.activation(v[p][:], qkv[p][:, 2 * T:3 * T], ACT.Copy).then_inc(v_ready[p], 1)
                    for p in range(2):
                        act.wait_ge(lowered[p], j + 1)
                        act.activation(probs[p][:], score[p][:], ACT.Exp, scale=HD ** -0.5).then_inc(exp_ready[p], 1)
                    for p in range(2):
                        act.wait_ge(turned[p], j + 1)
                        act.activation(probsT[p][:, 0:H // 2, :].rearrange("p h t -> p (h t)"), wide[p][:, 0:BANK],
                                       ACT.Copy).then_inc(turned_a[p], 1)
                    for p in range(2):
                        act.wait_ge(o_turned[p], j + 1)
                        act.activation(oT[p][:], small[p][:, T:2 * T], ACT.Identity, bias=bias[p][:, 2:3])\
                            .then_inc(oT_ready[p], 1)

            @block.vector
            def _(dve):
                dve.wait_ge(const_in, 32)
                per = 4 + (1 if (shifted is not None or causal) else 0)
                with dve.Fori(0, B // 2) as j:
                    links = [Link(dve, dve_step[p], j * per) for p in range(2)]
                    for p in range(2):
                        dve.wait_ge(qk_ready[p], 2 * j + 2)
                        dve.tensor_tensor(keys[p][:], over_mid(kT[p][:], H), over_last(mask[:], T), ALU.mult)\
                            .then_inc(keys_ready[p], 1)
                    for p in range(2):
                        dve.wait_ge(scored[p], j + 1)
                        w3 = wide[p][:].rearrange("p (h t) -> p h t", h=H)
                        if shifted is not None:
                            dve.wait_ge(pos_in[p], 16 * j + 16)
                            links[p](dve.tensor_tensor(score[p][:], w3, pos[p][:], ALU.add))
                            w3 = score[p][:]
                        if causal:
                            links[p](dve.tensor_tensor(score[p][:], w3, over_mid(tri[:], H), ALU.add))
                            w3 = score[p][:]
                        links[p](dve.tensor_reduce(top[p][:], w3, AX.X, ALU.max))
                        dve.tensor_tensor(score[p][:], w3, over_last(top[p][:], T), ALU.subtract).then_inc(lowered[p], 1)
                    for p in range(2):
                        dve.wait_ge(exp_ready[p], j + 1)
                        links[p](dve.tensor_reduce(mass[p][:], probs[p][:], AX.X, ALU.add))
                        links[p](dve.reciprocal(inv[p][:], mass[p][:]))
                    for p in range(2):
                        dve.wait_ge(turned[p], j + 1)
                        dve.tensor_copy(probsT[p][:, H // 2:, :].rearrange("p h t -> p (h t)"), wide[p][:, BANK:HT])\
                            .then_inc(turned_b[p], 1)
                    for p in range(2):
                        dve.wait_ge(attended[p], j + 1)
                        links[p](dve.tensor_tensor(o[p][:].rearrange("p (h e) -> p h e", h=H),
                                                   small[p][:, 0:D].rearrange("p (h e) -> p h e", h=H),
                                                   over_last(inv[p][:], HD), ALU.mult))
                        dve.sem_inc(o_ready[p], 1)
                    for p in range(2):
                        dve.wait_ge(y_ready[p], j + 1)
                        dst = out[:, bass.ds((2 * j + p) * T, T)]
                        if keep:
                            dve.scalar_tensor_tensor(dst, small[p][:, 2 * T:3 * T], bias[p][:, 3:4], xq_s[p][:],
                                                     ALU.add, ALU.add).then_inc(batch_done[p], 1)
                        else:
                            dve.tensor_scalar(dst, small[p][:, 2 * T:3 * T], bias[p][:, 3:4], None, ALU.add)\
                                .then_inc(batch_done[p], 1)
                for p in range(2):
                    dve.wait_ge(batch_done[p], B // 2 + 1)

            @block.tensor
            def _(pe):
                if not routed:
                    for p in range(2):
                        pe.wait_ge(w_in[p], 32)
                with pe.Fori(0, B // 2) as j:
                    for p in range(2):
                        pe.wait_ge(x_in[p], 2 * j + 2)
                        if routed:
                            pe.wait_ge(w_in[p], 32 * j + 32)
                        pe.matmul(qkv[p][:, 0:T], w[p][:, 0:D], xq_s[p][:], start=True, stop=True)
                        pe.matmul(qkv[p][:, T:2 * T], w[p][:, D:2 * D], xkv_s[p][:], start=True, stop=True)
                        pe.matmul(qkv[p][:, 2 * T:3 * T], xkv_s[p][:], w[p][:, 2 * D:3 * D], start=True, stop=True)\
                            .then_inc(projected[p], 1)
                    for p in range(2):
                        pe.wait_ge(keys_ready[p], j + 1)
                        k2 = keys[p][:].rearrange("p h t -> p (h t)")
                        for half in range(2):
                            mm = pe.matmul(wide[p][:, half * BANK:(half + 1) * BANK], qT[p][:],
                                           k2[:, half * BANK:(half + 1) * BANK], start=True, stop=True)
                        mm.then_inc(scored[p], 1)
                    for p in range(2):
                        pe.wait_ge(exp_ready[p], j + 1)
                        for h in range(H):
                            mm = pe.transpose(wide[p][:, h * T:(h + 1) * T], probs[p][:, h, :], core.ident[:])
                        mm.then_inc(turned[p], 1)
                    for p in range(2):
                        pe.wait_ge(turned_a[p], j + 1)
                        pe.wait_ge(turned_b[p], j + 1)
                        pe.wait_ge(v_ready[p], j + 1)
                        for h in range(H):
                            mm = pe.matmul(small[p][:, h * HD:(h + 1) * HD], probsT[p][:, h, :],
                                           v[p][:, h * HD:(h + 1) * HD], start=True, stop=True)
                        mm.then_inc(attended[p], 1)
                    for p in range(2):
                        pe.wait_ge(o_ready[p], j + 1)
                        pe.transpose(small[p][:, T:2 * T], o[p][:], core.ident[:]).then_inc(o_turned[p], 1)
                    for p in range(2):
                        pe.wait_ge(oT_ready[p], j + 1)
                        pe.matmul(small[p][:, 2 * T:3 * T], w[p][:, 3 * D:4 * D], oT[p][:], start=True, stop=True)\
                            .then_inc(y_ready[p], 1)


def position_scores(nc, core, u, xT, scratch):
    PI = float(np.pi)
    with Stage(nc, "pos") as s:
        freq, phase = s.sb("freq", [P, D]), s.sb("phase", [P, D])
        angle, turns, emb = s.sb("angle", [P, D]), s.sb("turns", [P, D]), s.sb("emb", [P, D])
        whole = s.sb("whole", [P, D], I32)
        embT, pT, wpos, wq, mask, bias = (s.sb("embT", [P, T]), s.sb("pT", [P, T]), s.sb("wpos", [P, D]),
                                          s.sb("wq", [P, D]), s.sb("mask", [P, H]), s.sb("bias", [P, 1]))
        places = s.sb("places", [P, H, T])
        xs = [s.sb(f"xs{p}", [P, T]) for p in range(2)]
        qT = [s.sb(f"qT{p}", [P, T]) for p in range(2)]
        padded = [s.sb(f"padded{p}", [P, H, T + 1]) for p in range(2)]
        small = [s.ps(f"small{p}", [P, BANK]) for p in range(2)]
        wide = [s.ps(f"wide{p}", [P, HT]) for p in range(2)]
        loaded, dve_step, angle_ready, sin_ready, embT_turned, p_ready, pT_ready, places_ready, embT_ready = (
            s.sem(n) for n in ("loaded", "dve_step", "angle_ready", "sin_ready", "embT_turned", "p_ready", "pT_ready",
                               "places_ready", "embT_ready"))
        x_in, q_made, q_ready, scored, copied, stored = (s.pair(n) for n in (
            "x_in", "q_made", "q_ready", "scored", "copied", "stored"))
        s.start_at_one(*stored, *copied, *scored, *q_made, *q_ready)
        with nc.Block() as block:
            @block.sync
            def _(sp):
                for dst, src in ((freq, "freq"), (phase, "phase"), (wpos, "L0_pos_w"), (mask, "head_mask"),
                                 (bias, "L0_bias_v")):
                    sp.dma_start(dst[:], core.d[src]).then_inc(loaded, 16)
                sp.dma_start(wq[:], core.d["L0_attn_w"][:, 0:D]).then_inc(loaded, 16)
                with sp.Fori(0, B // 2) as j:
                    for p in range(2):
                        sp.wait_ge(copied[p], 2 * j + 3)
                        sp.dma_start(scratch[bass.ds(2 * j + p, 1), :, :].rearrange("b h (q k) -> q (b h) k", k=T + 1),
                                     padded[p][:]).then_inc(stored[p], 16)
                for p in range(2):
                    sp.wait_ge(stored[p], 16 * (B // 2) + 1)

            @block.vector
            def _(dve):
                link = Link(dve, dve_step)
                for p in range(2):
                    link(dve.memset(padded[p][:, :, 0:1], 0.0))
                dve.wait_ge(loaded, 96)
                link(dve.scalar_tensor_tensor(angle[:], freq[:], u[:, 0, 0:1], phase[:], ALU.mult, ALU.add))
                link(dve.tensor_scalar(turns[:], angle[:], 1.0 / (2 * PI), None, ALU.mult))
                link(dve.tensor_copy(whole[:], turns[:]))
                link(dve.tensor_copy(turns[:], whole[:]))
                link(dve.scalar_tensor_tensor(angle[:], turns[:], -6.28125, angle[:], ALU.mult, ALU.add))
                link(dve.scalar_tensor_tensor(angle[:], turns[:], -(2 * PI - 6.28125), angle[:], ALU.mult, ALU.add))
                link(dve.tensor_scalar(turns[:], angle[:], PI, -2 * PI, ALU.is_gt, ALU.mult))
                link(dve.tensor_tensor(angle[:], angle[:], turns[:], ALU.add))
                link(dve.tensor_scalar(turns[:], angle[:], -PI, 2 * PI, ALU.is_lt, ALU.mult))
                link(dve.tensor_tensor(angle[:], angle[:], turns[:], ALU.add))
                dve.tensor_scalar(angle[:], angle[:], 3.1415925, -3.1415925, ALU.min, ALU.max).then_inc(angle_ready, 1)
                dve.wait_ge(embT_turned, 1)
                dve.tensor_copy(embT[:], small[0][:, 0:T]).then_inc(embT_ready, 1)
                dve.wait_ge(p_ready, 1)
                dve.tensor_copy(pT[:], small[1][:, 0:T]).then_inc(pT_ready, 1)
                dve.wait_ge(pT_ready, 1)
                dve.tensor_tensor(places[:], over_mid(pT[:], H), over_last(mask[:], T), ALU.mult)\
                    .then_inc(places_ready, 1)
                with dve.Fori(0, B // 2) as j:
                    for p in range(2):
                        dve.wait_ge(scored[p], j + 2)
                        dve.wait_ge(stored[p], 16 * j + 1)
                        dve.tensor_copy(padded[p][:, 0:4, 1:T + 1],
                                        wide[p][:, 0:BANK].rearrange("p (h t) -> p h t", t=T)).then_inc(copied[p], 1)

            @block.scalar
            def _(act):
                act.wait_ge(angle_ready, 1)
                act.activation(emb[:], angle[:], ACT.Sin).then_inc(sin_ready, 1)
                act.wait_ge(loaded, 96)
                with act.Fori(0, B // 2) as j:
                    for p in range(2):
                        act.wait_ge(q_made[p], j + 1)
                        act.activation(xs[p][:], xT[:, bass.ds((2 * j + p) * T, T)], ACT.Copy).then_inc(x_in[p], 1)
                    for p in range(2):
                        act.wait_ge(q_made[p], j + 2)
                        act.wait_ge(scored[p], j + 1)
                        act.activation(qT[p][:], small[p][:, 0:T], ACT.Identity, bias=bias[:]).then_inc(q_ready[p], 1)
                    for p in range(2):
                        act.wait_ge(scored[p], j + 2)
                        act.wait_ge(stored[p], 16 * j + 1)
                        act.activation(padded[p][:, 4:8, 1:T + 1],
                                       wide[p][:, BANK:HT].rearrange("p (h t) -> p h t", t=T), ACT.Copy)\
                            .then_inc(copied[p], 1)

            @block.tensor
            def _(pe):
                pe.wait_ge(sin_ready, 1)
                pe.transpose(small[0][:, 0:T], emb[:], core.ident[:]).then_inc(embT_turned, 1)
                pe.wait_ge(embT_ready, 1)
                pe.matmul(small[1][:, 0:T], wpos[:], embT[:], start=True, stop=True).then_inc(p_ready, 1)
                pe.wait_ge(places_ready, 1)
                flat_places = places[:].rearrange("p h t -> p (h t)")
                with pe.Fori(0, B // 2) as j:
                    for p in range(2):
                        pe.wait_ge(x_in[p], j + 1)
                        pe.wait_ge(q_ready[p], j + 1)
                        pe.matmul(small[p][:, 0:T], wq[:], xs[p][:], start=True, stop=True).then_inc(q_made[p], 1)
                    for p in range(2):
                        pe.wait_ge(q_ready[p], j + 2)
                        pe.wait_ge(copied[p], 2 * j + 1)
                        for half in range(2):
                            mm = pe.matmul(wide[p][:, half * BANK:(half + 1) * BANK], qT[p][:],
                                           flat_places[:, half * BANK:(half + 1) * BANK], start=True, stop=True)
                        mm.then_inc(scored[p], 1)


def l0_attention(nc, core, d):
    with ExitStack() as st:
        u = st.enter_context(nc.sbuf_tensor("l0a_u", [P, B, D], F32))
        xn = st.enter_context(nc.sbuf_tensor("l0a_xn", [P, B, D], F32))
        xT = st.enter_context(nc.sbuf_tensor("l0a_xT", [P, N], F32))
        yT = st.enter_context(nc.sbuf_tensor("l0a_yT", [P, N], F32))
        layer_norm(nc, "l0a_n0", core.h[:], u[:], 1e-5)
        layer_norm(nc, "l0a_n1", u[:], xn[:], 1e-5, d["L0_ln1"])
        layer_norm(nc, "l0a_n2", xn[:], xn[:], 1e-5, d["L0_ln2"])
        to_features(nc, "l0a_t", core, xn[:], xT[:])
        position_scores(nc, core, u[:], xT[:], core.rel_scratch)
        attention(nc, "l0a", core, xT[:], xT[:], yT[:], d["L0_attn_w"], d["L0_attn_b"], shifted=core.rel_scratch)
        add_features(nc, "l0a_r", core, yT[:], core.h[:])


E0, HV = 4, 64
BH = B * H


def delta_gates(nc, core, d, uT, weight, beta, decay_rows):
    G = E0 + 2 * H
    with Stage(nc, "dg") as s:
        w = s.sb("w", [P, G])
        dtb, alog, rate = s.sb("dtb", [P, H]), s.sb("alog", [P, H]), s.sb("rate", [P, H])
        logit = s.sb("logit", [P, B, G])
        prob, chosen, gt = s.sb("prob", [P, B, E0]), s.sb("chosen", [P, B, E0]), s.sb("gt", [P, B, E0])
        col = s.sb("col", [P, B])
        z, soft, mag, bt, square = (s.sb(n, [P, B, H]) for n in ("z", "soft", "mag", "bt", "square"))
        log_decay = s.sb("log_decay", [P, B, H, E0])
        rows = s.sb("rows", [P, 4, T])
        ps, psT = s.ps("ps", [P, BANK]), s.ps("psT", [P, BANK])
        loaded, logits_ready, dve_step, to_act, from_act, turned, rows_ready, stored = (
            s.sem(n) for n in ("loaded", "logits_ready", "dve_step", "to_act", "from_act", "turned", "rows_ready",
                               "stored"))
        with nc.Block() as block:
            @block.sync
            def _(sp):
                sp.dma_start(w[:], d["L0_gates_w"]).then_inc(loaded, 16)
                sp.dma_start(dtb[:], d["L0_dt_bias"].partition_broadcast(P)).then_inc(loaded, 16)
                sp.dma_start(alog[:], d["L0_A_log"].partition_broadcast(P)).then_inc(loaded, 16)
                sp.wait_ge(rows_ready, 1)
                sp.dma_start(decay_rows.rearrange("(g r) t -> r g t", g=4), rows[:]).then_inc(stored, 16)
                sp.wait_ge(stored, 16)

            @block.tensor
            def _(pe):
                pe.wait_ge(loaded, 48)
                for b in range(B):
                    mm = pe.matmul(ps[:, b * G:(b + 1) * G], uT[:, b * T:(b + 1) * T], w[:], start=True, stop=True)
                mm.then_inc(logits_ready, 1)
                pe.wait_ge(from_act, 5)
                flat_decay = log_decay[:].rearrange("p b h e -> p (b h e)")
                for g in range(4):
                    mm = pe.transpose(psT[:, g * P:(g + 1) * P], flat_decay[:, g * P:(g + 1) * P], core.ident[:])
                mm.then_inc(turned, 1)

            @block.scalar
            def _(act):
                act.wait_ge(loaded, 48)
                act.activation(rate[:], alog[:], ACT.Exp).then_inc(from_act, 1)
                act.wait_ge(to_act, 1)
                act.activation(prob[:], prob[:], ACT.Exp).then_inc(from_act, 1)
                act.wait_ge(to_act, 2)
                act.activation(bt[:], logit[:, :, E0:E0 + H], ACT.Exp, scale=-1.0).then_inc(from_act, 1)
                act.wait_ge(to_act, 3)
                act.activation(mag[:], mag[:], ACT.Exp, scale=-1.0).then_inc(from_act, 1)
                act.wait_ge(to_act, 4)
                act.activation(log_decay[:], log_decay[:], ACT.Exp).then_inc(from_act, 1)

            @block.vector
            def _(dve):
                link = Link(dve, dve_step)
                dve.wait_ge(logits_ready, 1)
                link(dve.tensor_copy(logit[:].rearrange("p b g -> p (b g)"), ps[:, 0:B * G]))
                gate = logit[:, :, 0:E0]
                link(dve.tensor_reduce(col[:], gate, AX.X, ALU.max))
                dve.tensor_tensor(prob[:], gate, over_last(col[:], E0), ALU.subtract).then_inc(to_act, 1)
                dve.wait_ge(from_act, 2)
                link(dve.tensor_reduce(col[:], prob[:], AX.X, ALU.add))
                link(dve.reciprocal(col[:], col[:]))
                link(dve.tensor_tensor(prob[:], prob[:], over_last(col[:], E0), ALU.mult))
                for e in range(E0):
                    link(dve.memset(gt[:], 0.0))
                    mine = prob[:, :, e:e + 1]
                    if e > 0:
                        link(dve.tensor_tensor(gt[:, :, 0:e], prob[:, :, 0:e], mine.to_broadcast([P, B, e]), ALU.is_ge))
                    if e < E0 - 1:
                        n = E0 - 1 - e
                        link(dve.tensor_tensor(gt[:, :, e + 1:], prob[:, :, e + 1:], mine.to_broadcast([P, B, n]),
                                               ALU.is_gt))
                    link(dve.tensor_reduce(col[:], gt[:], AX.X, ALU.add))
                    link(dve.tensor_scalar(chosen[:, :, e], col[:], 2.0, None, ALU.is_lt))
                link(dve.tensor_tensor(prob[:], prob[:], chosen[:], ALU.mult))
                link(dve.tensor_reduce(col[:], prob[:], AX.X, ALU.add))
                link(dve.reciprocal(col[:], col[:]))
                link(dve.tensor_tensor(weight, prob[:], over_last(col[:], E0), ALU.mult))
                dve.tensor_scalar(chosen[:], weight, 0.0, None, ALU.is_gt).then_inc(to_act, 1)
                dve.wait_ge(to_act, 2)
                dve.wait_ge(from_act, 3)
                link(dve.tensor_scalar(bt[:], bt[:], 1.0, None, ALU.add))
                link(dve.reciprocal(bt[:], bt[:]))
                shape = [P, B, H, E0]
                link(dve.tensor_tensor(beta, bt[:].unsqueeze(3).to_broadcast(shape),
                                       chosen[:].unsqueeze(2).to_broadcast(shape), ALU.mult))
                link(dve.tensor_tensor(z[:], logit[:, :, E0 + H:], over_mid(dtb[:], B), ALU.add))
                link(dve.tensor_scalar(soft[:], z[:], 0.0, None, ALU.max))
                dve.scalar_tensor_tensor(mag[:], z[:], -1.0, z[:], ALU.mult, ALU.max).then_inc(to_act, 1)
                dve.wait_ge(from_act, 4)
                log1p(link, dve, mag[:], z[:], square[:])
                link(dve.tensor_tensor(soft[:], soft[:], mag[:], ALU.add))
                link(dve.scalar_tensor_tensor(soft[:], soft[:], -1.0, over_mid(rate[:], B), ALU.mult, ALU.mult))
                dve.tensor_tensor(log_decay[:], soft[:].unsqueeze(3).to_broadcast(shape),
                                  chosen[:].unsqueeze(2).to_broadcast(shape), ALU.mult).then_inc(to_act, 1)
                dve.wait_ge(turned, 1)
                link(dve.tensor_copy(rows[:].rearrange("p g t -> p (g t)"), psT[:]))
                dve.memset(rows[:, :, 0:1], 0.0).then_inc(rows_ready, 1)


def delta_projections(nc, core, d, uT, qk, v):
    with Stage(nc, "dp") as s:
        w = s.sb("w", [P, 3, BANK])
        xs = [s.sb(f"xs{p}", [P, T]) for p in range(2)]
        square = s.sb("square", [P, 8, 2 * H * HV])
        length = s.sb("length", [P, 2 * BH])
        ps = [[s.ps(f"ps{p}{n}", [P, BANK]) for n in range(3)] for p in range(2)]
        loaded, dve_step, to_act, from_act = (s.sem(n) for n in ("loaded", "dve_step", "to_act", "from_act"))
        x_in, made, silu_done = s.pair("x_in"), s.pair("made"), s.pair("silu_done")
        W = 2 * HV
        s.start_at_one(*silu_done, *made)
        with nc.Block() as block:
            @block.sync
            def _(sp):
                sp.dma_start(w[:], d["L0_qkv_w"]).then_inc(loaded, 16)

            @block.tensor
            def _(pe):
                pe.wait_ge(loaded, 16)
                with pe.Fori(0, B // 2) as j:
                    for p in range(2):
                        pe.wait_ge(x_in[p], j + 1)
                        pe.wait_ge(silu_done[p], j + 1)
                        for n in range(3):
                            mm = pe.matmul(ps[p][n][:], xs[p][:], w[:, n, :], start=True, stop=True)
                        mm.then_inc(made[p], 1)

            @block.scalar
            def _(act):
                with act.Fori(0, B // 2) as j:
                    for p in range(2):
                        act.wait_ge(made[p], j + 1)
                        act.activation(xs[p][:], uT[:, bass.ds((2 * j + p) * T, T)], ACT.Copy).then_inc(x_in[p], 1)
                    for p in range(2):
                        act.wait_ge(made[p], j + 2)
                        here = qk[:, bass.ds((2 * j + p) * H * W, H * W)].rearrange("p (h w) -> p h w", h=H)
                        for n in range(2):
                            act.activation(here[:, :, n * HV:(n + 1) * HV],
                                           ps[p][n][:].rearrange("p (h w) -> p h w", h=H), ACT.Silu)
                        act.activation(v[:, bass.ds((2 * j + p) * BANK, BANK)], ps[p][2][:], ACT.Silu)\
                            .then_inc(silu_done[p], 1)
                act.wait_ge(to_act, 1)
                act.activation(length[:], length[:], ACT.Sqrt).then_inc(from_act, 1)

            @block.vector
            def _(dve):
                link = Link(dve, dve_step)
                for p in range(2):
                    dve.wait_ge(silu_done[p], B // 2 + 1)
                groups = qk.rearrange("p (g n) -> p g n", n=HV)
                for c in range(4):
                    part = slice(c * 64, (c + 1) * 64)
                    sq = square[:, 0:4, :].rearrange("p a n -> p (a n)").rearrange("p (g n) -> p g n", n=HV)
                    link(dve.tensor_tensor(sq, groups[:, part, :], groups[:, part, :], ALU.mult))
                    link(dve.tensor_reduce(length[:, part], sq, AX.X, ALU.add))
                dve.tensor_scalar(length[:], length[:], 1e-6, None, ALU.add).then_inc(to_act, 1)
                dve.wait_ge(from_act, 1)
                link(dve.reciprocal(length[:], length[:]))
                queries = length[:].rearrange("p (i n) -> p i n", n=2)[:, :, 0:1]
                link(dve.tensor_scalar(queries, queries, HV ** -0.5, None, ALU.mult))
                link(dve.tensor_tensor(groups, groups, over_last(length[:], HV), ALU.mult))


def delta_memories(nc, core, d, qk, v, weight, beta, decay_rows, mixed):
    W = 2 * HV
    LEVELS = 7
    with Stage(nc, "dm") as s:
        strict = s.sb("strict", [P, T])
        eye = s.sb("eye", [P, E0, T])
        levels = s.sb("levels", [P, LEVELS, T])

        def two(n, shape):
            return [s.sb(f"{n}{p}", shape) for p in range(2)]

        near, kq = two("near", [P, 3 * HV]), two("kq", [HV, 2, T])
        a, D_T, DB, NT, WT, off, Y, X, Z = (two(n, [P, E0, T]) for n in ("a", "D", "DB", "NT", "WT", "off", "Y", "X", "Z"))
        Gs, PT = two("Gs", [P, T]), two("PT", [P, T])
        delta, o = two("delta", [P, E0, HV]), two("o", [P, E0, HV])
        pA, pY, pX, pZ = ([s.ps(f"{n}{p}", [P, BANK]) for p in range(2)] for n in ("pA", "pY", "pX", "pZ"))
        const_in = s.sem("const_in")
        (a_in, near_in, kq_turned, kq_ready, products, gs_ready, pt_ready, scanned, weights_ready, z_ready, x_turned,
         off_ready, y_made, y_ready, xz_made, x_copied, z_copied, delta_made, delta_ready, o_made, turn_done,
         dve_step, decay_beta) = (s.pair(n) for n in (
            "a_in", "near_in", "kq_turned", "kq_ready", "products", "gs_ready", "pt_ready", "scanned", "weights_ready",
            "z_ready", "x_turned", "off_ready", "y_made", "y_ready", "xz_made", "x_copied", "z_copied", "delta_made",
            "delta_ready", "o_made", "turn_done", "dve_step", "decay_beta"))
        L = LEVELS - 1
        TURNS = BH // 2

        def cols(x3):
            return x3[:].rearrange("p e t -> p (e t)")

        s.start_at_one(*turn_done, *scanned, *o_made, *weights_ready)
        with nc.Block() as block:
            @block.sync
            def _(sp):
                sp.dma_start(strict[:], d["strict_upper"]).then_inc(const_in, 16)
                sp.dma_start(eye[:], d["ident"].unsqueeze(1).to_broadcast([P, E0, T])).then_inc(const_in, 16)
                sp.dma_start(levels[:], d["level_masks"]).then_inc(const_in, 16)
                with sp.Fori(0, TURNS) as j:
                    for p in range(2):
                        sp.wait_ge(scanned[p], j + 1)
                        sp.dma_start(cols(a[p]), decay_rows.rearrange("(i e) t -> i (e t)", e=E0)[
                            bass.ds(2 * j + p, 1), :].rearrange("i n -> (i n)").partition_broadcast(P)).then_inc(a_in[p], 16)

            @block.gpsimd
            def _(pool):
                with pool.Fori(0, TURNS) as j:
                    for p in range(2):
                        pool.wait_ge(scanned[p], j + 2)
                        pool.tensor_tensor(DB[p][:], D_T[p][:], over_last(beta[:, bass.ds((2 * j + p) * E0, E0)], T),
                                           ALU.mult).then_inc(decay_beta[p], 1)
                        pool.wait_ge(decay_beta[p], j + 1)
                        pool.wait_ge(pt_ready[p], j + 1)
                        pool.wait_ge(o_made[p], j + 1)
                        pool.tensor_tensor(WT[p][:], DB[p][:], over_mid(PT[p][:], E0), ALU.mult)\
                            .then_inc(weights_ready[p], 1)

            @block.scalar
            def _(act):
                with act.Fori(0, TURNS) as j:
                    for p in range(2):
                        act.wait_ge(turn_done[p], j + 1)
                        act.activation(near[p][:, HV:3 * HV], qk[:, bass.ds((2 * j + p) * W, W)], ACT.Copy)\
                            .then_inc(near_in[p], 1)
                        act.activation(near[p][:, 0:HV], qk[:, bass.ds((2 * j + p) * W + HV, HV)], ACT.Copy)\
                            .then_inc(near_in[p], 1)
                    for p in range(2):
                        act.wait_ge(kq_turned[p], j + 1)
                        act.activation(kq[p][:].rearrange("p a t -> p (a t)"), pA[p][0:HV, 0:2 * T], ACT.Copy)\
                            .then_inc(kq_ready[p], 1)
                    for p in range(2):
                        act.wait_ge(gs_ready[p], j + 1)
                        act.wait_ge(weights_ready[p], j + 1)
                        act.activation(PT[p][:], pA[p][:, 3 * T:4 * T], ACT.Copy).then_inc(pt_ready[p], 1)
                    for p in range(2):
                        act.wait_ge(x_turned[p], j + 1)
                        act.activation(cols(X[p]), pX[p][:], ACT.Copy).then_inc(x_copied[p], 1)
                    for l in range(L - 1):
                        for p in range(2):
                            act.wait_ge(xz_made[p], j * L + l + 1)
                            act.activation(cols(X[p]), pX[p][:], ACT.Copy).then_inc(x_copied[p], 1)
                    for p in range(2):
                        act.wait_ge(delta_made[p], j + 1)
                        act.activation(delta[p][:].rearrange("p e n -> p (e n)"), pA[p][:, 0:E0 * HV], ACT.Copy)\
                            .then_inc(delta_ready[p], 1)

            @block.vector
            def _(dve):
                dve.wait_ge(const_in, 48)
                per = 3
                with dve.Fori(0, TURNS) as j:
                    links = [Link(dve, dve_step[p], j * per) for p in range(2)]
                    for p in range(2):
                        dve.wait_ge(a_in[p], 16 * j + 16)
                        dve.wait_ge(weights_ready[p], j + 1)
                        dve.tensor_tensor_scan(cols(D_T[p]), cols(a[p]), cols(eye), 0.0, ALU.mult, ALU.add)\
                            .then_inc(scanned[p], 1)
                    for p in range(2):
                        dve.wait_ge(products[p], j + 1)
                        dve.tensor_tensor(Gs[p][:], pA[p][:, 2 * T:3 * T], strict[:], ALU.mult).then_inc(gs_ready[p], 1)
                        dve.wait_ge(gs_ready[p], j + 1)
                        links[p](dve.tensor_tensor(NT[p][:], over_mid(Gs[p][:], E0),
                                                   over_last(beta[:, bass.ds((2 * j + p) * E0, E0)], T), ALU.mult))
                        links[p](dve.tensor_tensor(off[p][:], NT[p][:], over_mid(levels[:, 0, :], E0), ALU.mult))
                        dve.tensor_tensor(Z[p][:], eye[:], off[p][:], ALU.subtract).then_inc(z_ready[p], 1)
                        dve.wait_ge(z_ready[p], j + 1)
                        dve.tensor_tensor(off[p][:], NT[p][:], over_mid(levels[:, 1, :], E0), ALU.mult)\
                            .then_inc(off_ready[p], 1)
                    for l in range(L):
                        for p in range(2):
                            dve.wait_ge(y_made[p], j * L + l + 1)
                            dve.tensor_tensor(cols(Y[p]), cols(eye), pY[p][:], ALU.subtract).then_inc(y_ready[p], 1)
                            if l < L - 1:
                                dve.tensor_tensor(off[p][:], NT[p][:], over_mid(levels[:, l + 2, :], E0), ALU.mult)\
                                    .then_inc(off_ready[p], 1)
                        for p in range(2):
                            dve.wait_ge(xz_made[p], j * L + l + 1)
                            if l < L - 1:
                                dve.tensor_copy(cols(Z[p]), pZ[p][:]).then_inc(z_copied[p], 1)
                            else:
                                dve.tensor_tensor(cols(Z[p]), pZ[p][:], cols(D_T[p]), ALU.mult).then_inc(z_copied[p], 1)
                    for p in range(2):
                        dve.wait_ge(o_made[p], j + 2)
                        seq = (2 * j + p) // H
                        links[p](dve.tensor_tensor(o[p][:], pY[p][:, 0:E0 * HV].rearrange("p (e n) -> p e n", e=E0),
                                                   over_last(weight[:, bass.ds(seq * E0, E0)], HV), ALU.mult))
                        dve.tensor_reduce(mixed[:, bass.ds((2 * j + p) * HV, HV)], o[p][:].rearrange("p e n -> p n e"),
                                          AX.X, ALU.add).then_inc(turn_done[p], 1)
                for p in range(2):
                    dve.wait_ge(turn_done[p], TURNS + 1)

            @block.tensor
            def _(pe):
                pe.wait_ge(const_in, 48)
                with pe.Fori(0, TURNS) as j:
                    for p in range(2):
                        pe.wait_ge(near_in[p], 2 * j + 2)
                        for n in range(2):
                            mm = pe.transpose(pA[p][:, n * T:(n + 1) * T], near[p][:, n * HV:(n + 2) * HV],
                                              core.ident[:])
                        mm.then_inc(kq_turned[p], 1)
                    for p in range(2):
                        pe.wait_ge(kq_ready[p], j + 1)
                        for n in range(2):
                            mm = pe.matmul(pA[p][:, (2 + n) * T:(3 + n) * T], kq[p][:, 0, :], kq[p][:, n, :],
                                           start=True, stop=True)
                        mm.then_inc(products[p], 1)
                    for p in range(2):
                        pe.wait_ge(z_ready[p], j + 1)
                        for e in range(E0):
                            mm = pe.transpose(pX[p][:, e * T:(e + 1) * T], Z[p][:, e, :], core.ident[:])
                        mm.then_inc(x_turned[p], 1)
                    for l in range(L):
                        for p in range(2):
                            pe.wait_ge(x_copied[p], j * L + l + 1)
                            pe.wait_ge(off_ready[p], j * L + l + 1)
                            if l > 0:
                                pe.wait_ge(z_copied[p], j * L + l)
                            for e in range(E0):
                                mm = pe.matmul(pY[p][:, e * T:(e + 1) * T], off[p][:, e, :], X[p][:, e, :],
                                               start=True, stop=True)
                            mm.then_inc(y_made[p], 1)
                        for p in range(2):
                            pe.wait_ge(y_ready[p], j * L + l + 1)
                            if l < L - 1:
                                for e in range(E0):
                                    pe.matmul(pX[p][:, e * T:(e + 1) * T], Z[p][:, e, :], Y[p][:, e, :],
                                              start=True, stop=True)
                            for e in range(E0):
                                mm = pe.matmul(pZ[p][:, e * T:(e + 1) * T], Y[p][:, e, :], Z[p][:, e, :],
                                               start=True, stop=True)
                            mm.then_inc(xz_made[p], 1)
                    for p in range(2):
                        pe.wait_ge(z_copied[p], j * L + L)
                        pe.wait_ge(pt_ready[p], j + 1)
                        for e in range(E0):
                            mm = pe.matmul(pA[p][:, e * HV:(e + 1) * HV], Z[p][:, e, :],
                                           v[:, bass.ds((2 * j + p) * HV, HV)], start=True, stop=True)
                        mm.then_inc(delta_made[p], 1)
                    for p in range(2):
                        pe.wait_ge(delta_ready[p], j + 1)
                        pe.wait_ge(weights_ready[p], j + 2)
                        for e in range(E0):
                            mm = pe.matmul(pY[p][:, e * HV:(e + 1) * HV], WT[p][:, e, :], delta[p][:, e, :],
                                           start=True, stop=True)
                        mm.then_inc(o_made[p], 1)


def delta_output(nc, core, d, uT, mixed):
    with Stage(nc, "do") as s:
        wg, wo, norm = s.sb("wg", [P, BANK]), s.sb("wo", [P, 4, D]), s.sb("norm", [P, HV])
        length = s.sb("length", [P, BH])
        square = s.sb("square", [P, 32, HV])

        def two(n, shape):
            return [s.sb(f"{n}{p}", shape) for p in range(2)]

        xs, gate, gated, gT = two("xs", [P, T]), two("gate", [P, BANK]), two("gated", [P, BANK]), two("gT", [P, 4, T])
        pg, pt, py = ([s.ps(f"{n}{p}", [P, BANK]) for p in range(2)] for n in ("pg", "pt", "py"))
        loaded, dve_step, to_act, from_act, scaled = (s.sem(n) for n in ("loaded", "dve_step", "to_act", "from_act",
                                                                        "scaled"))
        x_in, gate_made, gate_ready, gated_ready, turned, copied, made, added = (s.pair(n) for n in (
            "x_in", "gate_made", "gate_ready", "gated_ready", "turned", "copied", "made", "added"))
        s.start_at_one(*added, *gate_ready, *turned, *gate_made, *gated_ready, *copied)
        with nc.Block() as block:
            @block.sync
            def _(sp):
                sp.dma_start(wg[:], d["L0_gate_w"]).then_inc(loaded, 16)
                sp.dma_start(wo[:], d["L0_out_w"]).then_inc(loaded, 16)
                sp.dma_start(norm[:], d["L0_o_norm"].partition_broadcast(P)).then_inc(loaded, 16)

            @block.vector
            def _(dve):
                link = Link(dve, dve_step)
                groups = mixed.rearrange("p (g n) -> p g n", n=HV)
                for c in range(4):
                    part = slice(c * 32, (c + 1) * 32)
                    link(dve.tensor_tensor(square[:], groups[:, part, :], groups[:, part, :], ALU.mult))
                    link(dve.tensor_reduce(length[:, part], square[:], AX.X, ALU.add))
                dve.tensor_scalar(length[:], length[:], 1.0 / HV, 1e-5, ALU.mult, ALU.add).then_inc(to_act, 1)
                dve.wait_ge(from_act, 1)
                link(dve.reciprocal(length[:], length[:]))
                link(dve.tensor_tensor(groups, groups, over_last(length[:], HV), ALU.mult))
                dve.wait_ge(loaded, 48)
                dve.tensor_tensor(groups, groups, over_mid(norm[:], BH), ALU.mult).then_inc(scaled, 1)
                dve.wait_ge(scaled, 1)
                with dve.Fori(0, B // 2) as j:
                    for p in range(2):
                        dve.wait_ge(gate_ready[p], j + 2)
                        dve.wait_ge(turned[p], j + 1)
                        dve.tensor_tensor(gated[p][:], mixed[:, bass.ds((2 * j + p) * BANK, BANK)], gate[p][:], ALU.mult)\
                            .then_inc(gated_ready[p], 1)
                    for p in range(2):
                        dve.wait_ge(turned[p], j + 2)
                        dve.tensor_copy(gT[p][:].rearrange("p a t -> p (a t)"), pt[p][:]).then_inc(copied[p], 1)
                    for p in range(2):
                        dve.wait_ge(made[p], j + 1)
                        here = flat(core.h[:])[:, bass.ds((2 * j + p) * D, D)]
                        dve.tensor_tensor(here, here, py[p][:, 0:D], ALU.add).then_inc(added[p], 1)
                for p in range(2):
                    dve.wait_ge(added[p], B // 2 + 1)

            @block.scalar
            def _(act):
                act.wait_ge(to_act, 1)
                act.activation(length[:], length[:], ACT.Sqrt).then_inc(from_act, 1)
                with act.Fori(0, B // 2) as j:
                    for p in range(2):
                        act.wait_ge(gate_made[p], j + 1)
                        act.activation(xs[p][:], uT[:, bass.ds((2 * j + p) * T, T)], ACT.Copy).then_inc(x_in[p], 1)
                    for p in range(2):
                        act.wait_ge(gate_made[p], j + 2)
                        act.wait_ge(gated_ready[p], j + 1)
                        act.activation(gate[p][:], pg[p][:], ACT.Silu).then_inc(gate_ready[p], 1)

            @block.tensor
            def _(pe):
                pe.wait_ge(loaded, 48)
                with pe.Fori(0, B // 2) as j:
                    for p in range(2):
                        pe.wait_ge(x_in[p], j + 1)
                        pe.wait_ge(gate_ready[p], j + 1)
                        pe.matmul(pg[p][:], xs[p][:], wg[:], start=True, stop=True).then_inc(gate_made[p], 1)
                    for p in range(2):
                        pe.wait_ge(gated_ready[p], j + 2)
                        pe.wait_ge(copied[p], j + 1)
                        for k in range(4):
                            mm = pe.transpose(pt[p][:, k * T:(k + 1) * T], gated[p][:, k * P:(k + 1) * P], core.ident[:])
                        mm.then_inc(turned[p], 1)
                    for p in range(2):
                        pe.wait_ge(copied[p], j + 2)
                        pe.wait_ge(added[p], j + 1)
                        for k in range(4):
                            mm = pe.matmul(py[p][:, 0:D], gT[p][:, k, :], wo[:, k, :], start=(k == 0), stop=(k == 3))
                        mm.then_inc(made[p], 1)


def l0_ffn(nc, core, d):
    with ExitStack() as st:
        def sb(n, shape):
            return st.enter_context(nc.sbuf_tensor(f"l0f_{n}", shape, F32))

        uT = sb("uT", [P, N])
        with nc.sbuf_tensor("l0f_u", [P, B, D], F32) as u:
            layer_norm(nc, "l0f_n", core.h[:], u[:], 1e-5)
            to_features(nc, "l0f_t", core, u[:], uT[:])
        weight, beta = sb("weight", [P, B, E0]), sb("beta", [P, B, H, E0])
        decay_rows = core.decay_scratch
        delta_gates(nc, core, d, uT[:], weight[:], beta[:], decay_rows)
        qk, v, mixed = sb("qk", [P, BH * 2 * HV]), sb("v", [P, BH * HV]), sb("mixed", [P, BH * HV])
        delta_projections(nc, core, d, uT[:], qk[:], v[:])
        delta_memories(nc, core, d, qk[:], v[:], weight[:].rearrange("p b e -> p (b e)"),
                       beta[:].rearrange("p b h e -> p (b h e)"), decay_rows, mixed[:])
        delta_output(nc, core, d, uT[:], mixed[:])


H1, H2 = 256, 128
C1, C2 = 4 * H1 // P, 4 * H2 // P
K1 = H1 // P


def lstm_inputs(nc, core, d, u, uT, z1, z2, idle, mask_dram):
    with Stage(nc, "li") as s:
        w, b0, b1 = s.sb("w", [P, 4 * H1]), s.sb("b0", [P, C1]), s.sb("b1", [P, C2])
        ne, m = s.sb("ne", [P, B, D]), s.sb("m", [P, B])
        shut = s.sb("shut", [P, T, B])
        ps = [s.ps(f"ps{i}", [P, BANK]) for i in range(4)]
        loaded, m_ready, stored, idle_in, dve_step, made, z_ready = (
            s.sem(n) for n in ("loaded", "m_ready", "stored", "idle_in", "dve_step", "made", "z_ready"))
        TB = BANK // B
        with nc.Block() as block:
            @block.sync
            def _(sp):
                sp.dma_start(w[:], d["L1_W0"]).then_inc(loaded, 16)
                sp.dma_start(b0[:], d["L1_b0"]).then_inc(loaded, 16)
                sp.dma_start(b1[:], d["L1_b1"]).then_inc(loaded, 16)
                sp.wait_ge(m_ready, 1)
                sp.dma_start(mask_dram, m[:]).then_inc(stored, 16)
                sp.wait_ge(stored, 16)
                sp.dma_start(idle, mask_dram.rearrange("t b -> (t b)").partition_broadcast(P)).then_inc(idle_in, 16)

            @block.tensor
            def _(pe):
                pe.wait_ge(loaded, 48)
                xv = uT.rearrange("p (b t) -> p t b", t=T)
                for i in range(4 * C1):
                    c, g = i // 4, i % 4
                    if i >= 4:
                        pe.wait_ge(z_ready, i - 3)
                    pe.matmul(ps[i % 4][:], w[:, c * P:(c + 1) * P], xv[:, g * TB:(g + 1) * TB, :],
                              start=True, stop=True).then_inc(made, 1)

            @block.scalar
            def _(act):
                act.wait_ge(loaded, 48)
                for i in range(4 * C1):
                    c, g = i // 4, i % 4
                    act.wait_ge(made, i + 1)
                    act.activation(z1[:, g * TB:(g + 1) * TB, c, :],
                                   ps[i % 4][:].rearrange("p (t b) -> p t b", b=B), ACT.Identity,
                                   bias=b0[:, c:c + 1]).then_inc(z_ready, 1)

            @block.vector
            def _(dve):
                link = Link(dve, dve_step)
                link(dve.tensor_scalar(ne[:], u, 0.0, None, ALU.not_equal))
                link(dve.tensor_reduce(m[:], ne[:], AX.X, ALU.max))
                dve.tensor_scalar(m[:], m[:], -1.0, 1.0, ALU.mult, ALU.add).then_inc(m_ready, 1)
                dve.wait_ge(loaded, 48)
                link(dve.memset(z2, 0.0))
                for c in range(C2):
                    link(dve.tensor_scalar(z2[:, :, c, :], z2[:, :, c, :], b1[:, c:c + 1], None, ALU.add))
                dve.wait_ge(idle_in, 16)
                idle3 = idle.rearrange("p (t b) -> p t b", b=B)
                link(dve.tensor_scalar(shut[:], idle3, NEVER, None, ALU.mult))
                dve.wait_ge(z_ready, 4 * C1)
                for z, n in ((z1, C1 // 4), (z2, C2 // 4)):
                    for c in range(3 * n):
                        op = ALU.subtract if c // n == 1 else ALU.add
                        link(dve.tensor_tensor(z[:, :, c, :], z[:, :, c, :], shut[:], op))


def lstm_steps(nc, core, d, z1, z2, idle, yT):
    with Stage(nc, "ls") as s:
        raw = s.sb("raw", [P, K1, 4 * H1])
        U0, W1, U1 = (s.sb("U0", [P, 3, K1, 4 * H1], BF16), s.sb("W1", [P, 3, K1, 4 * H2], BF16),
                      s.sb("U1", [P, 3, 4 * H2], BF16))
        n = (C1 // 4 * B, C2 // 4 * B)
        chunks = (C1, C2)
        state = [[s.sb(f"state{l}{q}", [P, n[l]]) for q in range(2)] for l in range(2)]
        parts = [[s.sb(f"parts{l}{q}", [P, n[l] // B, 3, B], BF16) for q in range(2)] for l in range(2)]
        cell, bent, kept, fresh, left = ([s.sb(f"{name}{l}", [P, n[l]]) for l in range(2)] for name in (
            "cell", "bent", "kept", "fresh", "left"))
        sums, gates = ([s.sb(f"{name}{l}", [P, 4 * n[l]]) for l in range(2)] for name in ("sums", "gates"))
        pz = [[s.ps(f"pz{l}{q}", [P, BANK]) for q in range(2)] for l in range(2)]
        loaded, split, zeroed, copied = s.sem("loaded"), s.sem("split"), s.sem("zeroed"), s.sem("copied")
        z_made, summed, gates_ready, cell_ready, bent_ready, state_ready, parts_ready, dve_step = (
            [s.sem(f"{name}{l}") for l in range(2)] for name in (
                "z_made", "summed", "gates_ready", "cell_ready", "bent_ready", "state_ready", "parts_ready",
                "dve_step"))
        z = (z1.rearrange("p t c b -> p (t c b)"), z2.rearrange("p t c b -> p (t c b)"))
        weights = ((U0, "L1_U0", raw[:]), (W1, "L1_W1", raw[:, :, 0:4 * H2]), (U1, "L1_U1", raw[:, 0, 0:4 * H2]))

        def later(t, least):
            return not isinstance(t, int) or t >= least

        def wavefront(eng, first, both, last):
            first(0, 0)
            both(1, 1)
            both(2, 0)
            with eng.Fori(0, (T - 4) // 2) as j:
                both(2 * j + 3, 1)
                both(2 * j + 4, 0)
            both(T - 1, 1)
            last(T - 1, 1)

        with nc.Block() as block:
            @block.sync
            def _(sp):
                for i, (_, src, here) in enumerate(weights):
                    if i > 0:
                        sp.wait_ge(split, i)
                    sp.dma_start(here, d[src]).then_inc(loaded, 16)

            @block.tensor
            def _(pe):
                pe.wait_ge(split, len(weights))
                pe.wait_ge(zeroed, 6)

                def products(l, q, terms):
                    for c in range(chunks[l]):
                        for i, (w, x) in enumerate(terms):
                            mm = pe.matmul(pz[l][q][:, c * 3 * B:(c + 1) * 3 * B], w(c), x,
                                           start=False, stop=(i == len(terms) - 1), skip_group_check=True)
                    return mm

                def term(w, k, part, x):
                    x = x[:, k, :, :].rearrange("p s b -> p (s b)")
                    if w is U1:
                        return lambda c: U1[:, part, c * P:(c + 1) * P], x
                    return lambda c: w[:, part, k, c * P:(c + 1) * P], x

                def outer(l, t, q):
                    if later(t, 2):
                        pe.wait_ge(summed[l], t - 1)
                    pe.matmul(pz[l][q][:, 0:chunks[l] * 3 * B].rearrange("p (c s b) -> p s c b", s=3, b=B)[:, 0],
                              core.ident[:], z[l][:, bass.ds(t * 4 * n[l], 4 * n[l])], start=True, stop=False,
                              skip_group_check=True)

                def step1(t, q):
                    outer(0, t, q)
                    if later(t, 1):
                        pe.wait_ge(parts_ready[0], t)
                    products(0, q, [term(U0, k, part, parts[0][q]) for k in range(K1) for part in range(3)])\
                        .then_inc(z_made[0], 1)

                def step2(t, q):
                    outer(1, t, q)
                    pe.wait_ge(parts_ready[0], t + 1)
                    if later(t, 1):
                        pe.wait_ge(parts_ready[1], t)
                    products(1, q, [term(W1, k, part, parts[0][1 - q]) for k in range(K1) for part in range(3)]
                             + [term(U1, 0, part, parts[1][q]) for part in range(3)]).then_inc(z_made[1], 1)

                step1(0, 0)
                step1(1, 1)
                step2(0, 0)
                step1(2, 0)
                step2(1, 1)
                with pe.Fori(0, (T - 4) // 2) as j:
                    step1(2 * j + 3, 1)
                    step2(2 * j + 2, 0)
                    step1(2 * j + 4, 0)
                    step2(2 * j + 3, 1)
                step1(T - 1, 1)
                step2(T - 2, 0)
                step2(T - 1, 1)

            @block.scalar
            def _(act):
                def step(l, t):
                    act.wait_ge(summed[l], t + 1)
                    act.activation(gates[l][:, 0:3 * n[l]], sums[l][:, 0:3 * n[l]], ACT.Sigmoid)
                    act.activation(gates[l][:, 3 * n[l]:4 * n[l]], sums[l][:, 3 * n[l]:4 * n[l]], ACT.Tanh)\
                        .then_inc(gates_ready[l], 1)
                    act.wait_ge(cell_ready[l], t + 1)
                    act.activation(bent[l][:], cell[l][:], ACT.Tanh).then_inc(bent_ready[l], 1)

                def both(t, q):
                    step(0, t)
                    step(1, t - 1)

                wavefront(act, lambda t, q: step(0, t), both, lambda t, q: step(1, t))

            @block.gpsimd
            def _(pool):
                with pool.Fori(0, T // 2) as j:
                    for q in range(2):
                        pool.wait_ge(state_ready[1], 2 * j + q + 1)
                        pool.tensor_copy(yT.rearrange("p (b t) -> p t b", t=T)[:, bass.ds(2 * j + q, 1), :],
                                         state[1][1 - q][:].rearrange("p (t b) -> p t b", t=1)).then_inc(copied, 1)
                pool.wait_ge(copied, T)

            @block.vector
            def _(dve):
                for l in range(2):
                    dve.memset(state[l][0][:], 0.0).then_inc(zeroed, 1)
                    dve.memset(parts[l][0][:], 0.0).then_inc(zeroed, 1)
                    dve.memset(cell[l][:], 0.0).then_inc(zeroed, 1)
                dve.wait_ge(zeroed, 6)
                setup = Link(dve, dve_step[0])
                for i, (w, _, here) in enumerate(weights):
                    dve.wait_ge(loaded, 16 * i + 16)
                    for part in range(2):
                        setup(dve.tensor_copy(w[:, part], here))
                        setup(dve.tensor_tensor(here, here, w[:, part], ALU.subtract))
                    dve.tensor_copy(w[:, 2], here).then_inc(split, 1)
                base = (setup.n, 0)

                def step(l, t, q):
                    link = Link(dve, dve_step[l], base[l] + t * 3)
                    i, f, o, c = (gates[l][:, k * n[l]:(k + 1) * n[l]] for k in range(4))
                    if later(t, 1):
                        dve.wait_ge(state_ready[l], t)
                    dve.tensor_tensor(kept[l][:].rearrange("p (k b) -> p k b", b=B),
                                      state[l][q][:].rearrange("p (k b) -> p k b", b=B),
                                      over_mid(idle[:, bass.ds(t * B, B)], n[l] // B), ALU.mult)
                    dve.wait_ge(z_made[l], t + 1)
                    dve.tensor_reduce(sums[l][:].rearrange("p (c b) -> p c b", b=B),
                                      pz[l][q][:, 0:chunks[l] * 3 * B].rearrange("p (c s b) -> p c b s", s=3, b=B),
                                      AX.X, ALU.add).then_inc(summed[l], 1)
                    dve.wait_ge(gates_ready[l], t + 1)
                    dve.tensor_tensor(fresh[l][:], i, c, ALU.mult)
                    link(dve.tensor_tensor(cell[l][:], f, cell[l][:], ALU.mult))
                    dve.tensor_tensor(cell[l][:], cell[l][:], fresh[l][:], ALU.add).then_inc(cell_ready[l], 1)
                    dve.wait_ge(bent_ready[l], t + 1)
                    link(dve.tensor_tensor(fresh[l][:], o, bent[l][:], ALU.mult))
                    if l == 1 and later(t, 2):
                        dve.wait_ge(copied, t - 1)
                    new, rest, more, old = (x[:].rearrange("p (k b) -> p k b", b=B) for x in (
                        state[l][1 - q], left[l], fresh[l], kept[l]))
                    high, middle, low = (parts[l][1 - q][:, :, part, :] for part in range(3))
                    dve.tensor_tensor(high, more, old, ALU.add)
                    dve.tensor_tensor(new, more, old, ALU.add).then_inc(state_ready[l], 1)
                    dve.wait_ge(state_ready[l], t + 1)
                    dve.tensor_tensor(middle, new, high, ALU.subtract)
                    link(dve.tensor_tensor(rest, new, high, ALU.subtract))
                    dve.tensor_tensor(low, rest, middle, ALU.subtract).then_inc(parts_ready[l], 1)

                def both(t, q):
                    step(0, t, q)
                    step(1, t - 1, 1 - q)

                wavefront(dve, lambda t, q: step(0, t, q), both, lambda t, q: step(1, t, q))


def l1_attention(nc, core, d):
    with ExitStack() as st:
        def sb(n, shape):
            return st.enter_context(nc.sbuf_tensor(f"l1a_{n}", shape, F32))

        z1, z2, idle, yT = sb("z1", [P, T, C1, B]), sb("z2", [P, T, C2, B]), sb("idle", [P, T * B]), sb("yT", [P, N])
        with nc.sbuf_tensor("l1a_u", [P, B, D], F32) as u, nc.sbuf_tensor("l1a_uT", [P, N], F32) as uT:
            layer_norm(nc, "l1a_n", core.h[:], u[:], 1e-5)
            to_features(nc, "l1a_t", core, u[:], uT[:])
            lstm_inputs(nc, core, d, u[:], uT[:], z1[:], z2[:], idle[:], core.mask_scratch)
        lstm_steps(nc, core, d, z1[:], z2[:], idle[:], yT[:])
        add_features(nc, "l1a_r", core, yT[:], core.h[:])


GROUP = BANK // T
GROUPS = B // GROUP


def mlp(nc, name, core, xT, w1, b1, w2, b2, width, func, dst, scale=1.0):
    F = width // P
    with Stage(nc, name) as s:
        w1_s, b1_s, w2_s, b2_s = s.sb("w1", [P, width]), s.sb("b1", [P, F]), s.sb("w2", [P, F, D]), s.sb("b2", [P, D])
        mid, add = s.sb("mid", [P, F, BANK]), s.sb("add", [P, GROUP, D])
        up = [s.ps(f"up{i}", [P, BANK]) for i in range(F)]
        down = s.ps("down", [P, BANK])
        loaded, made, mid_ready, out_made, biased, added = (s.sem(n) for n in (
            "loaded", "made", "mid_ready", "out_made", "biased", "added"))
        s.start_at_one(added, mid_ready, biased, out_made)
        with nc.Block() as block:
            @block.sync
            def _(sp):
                sp.dma_start(w1_s[:], w1).then_inc(loaded, 16)
                sp.dma_start(b1_s[:], b1).then_inc(loaded, 16)
                sp.dma_start(w2_s[:], w2).then_inc(loaded, 16)
                sp.dma_start(b2_s[:], b2.partition_broadcast(P)).then_inc(loaded, 16)

            @block.tensor
            def _(pe):
                pe.wait_ge(loaded, 64)
                with pe.Fori(0, GROUPS) as g:
                    pe.wait_ge(mid_ready, g * F + 1)
                    for c in range(F):
                        pe.matmul(up[c][:], w1_s[:, c * P:(c + 1) * P], xT[:, bass.ds(g * BANK, BANK)],
                                  start=True, stop=True).then_inc(made, 1)
                    pe.wait_ge(mid_ready, g * F + F + 1)
                    pe.wait_ge(biased, g + 1)
                    for k in range(GROUP):
                        for c in range(F):
                            mm = pe.matmul(down[:, k * D:(k + 1) * D], mid[:, c, k * T:(k + 1) * T], w2_s[:, c, :],
                                           start=(c == 0), stop=(c == F - 1))
                    mm.then_inc(out_made, 1)

            @block.scalar
            def _(act):
                act.wait_ge(loaded, 64)
                with act.Fori(0, GROUPS) as g:
                    act.wait_ge(out_made, g + 1)
                    for c in range(F):
                        act.wait_ge(made, g * F + c + 1)
                        act.activation(mid[:, c, :], up[c][:], func, bias=b1_s[:, c:c + 1]).then_inc(mid_ready, 1)

            @block.vector
            def _(dve):
                dve.wait_ge(loaded, 64)
                with dve.Fori(0, GROUPS) as g:
                    dve.wait_ge(out_made, g + 2)
                    dve.wait_ge(added, g + 1)
                    dve.tensor_tensor(add[:], down[:].rearrange("p (b d) -> p b d", d=D), over_mid(b2_s[:], GROUP),
                                      ALU.add).then_inc(biased, 1)
                    dve.wait_ge(biased, g + 2)
                    here = flat(dst)[:, bass.ds(g * BANK, BANK)]
                    dve.scalar_tensor_tensor(here, flat(add[:]), scale, here, ALU.mult, ALU.add).then_inc(added, 1)
                dve.wait_ge(added, GROUPS + 1)


E1, R1, F1 = 64, 64, 4


def first_hot(link, dve, hot, best, value, order, key, keybest):
    n = value.shape[2]
    link(dve.tensor_reduce(best, value, AX.X, ALU.max))
    link(dve.tensor_tensor(key, value, over_last(best, n), ALU.is_ge))
    link(dve.tensor_tensor(key, key, over_mid(order, value.shape[1]), ALU.mult))
    link(dve.tensor_reduce(keybest, key, AX.X, ALU.max))
    link(dve.tensor_tensor(hot, key, over_last(keybest, n), ALU.is_equal))


def router64(nc, core, d, xT, combine, dst):
    with Stage(nc, "r1") as s:
        wr, cb, b2 = s.sb("wr", [P, R1]), s.sb("cb", [R1, E1]), s.sb("b2", [E1, D])
        rT = s.sb("rT", [R1, N])
        order = s.sb("order", [P, E1])
        prob, key, hot, rest = (s.sb(n, [P, B, E1]) for n in ("prob", "key", "hot", "rest"))
        top, best1, best2, kb, total = (s.sb(n, [P, B]) for n in ("top", "best1", "best2", "kb", "total"))
        cT = s.sb("cT", [E1, N])
        pr = [s.ps(f"pr{i}", [P, BANK]) for i in range(4)]
        pl = s.ps("pl", [P, B * E1])
        loaded, dve_step, r_made, r_ready, logits_made, lowered, exp_ready, combined, c_turned, c_ready, made, done = (
            s.sem(n) for n in ("loaded", "dve_step", "r_made", "r_ready", "logits_made", "lowered", "exp_ready",
                               "combined", "c_turned", "c_ready", "made", "done"))
        with nc.Block() as block:
            @block.sync
            def _(sp):
                sp.dma_start(wr[:], d["L1f_Wr"]).then_inc(loaded, 16)
                sp.dma_start(cb[:], d["L1f_codebook"]).then_inc(loaded, 16)
                sp.dma_start(b2[:], d["L1f_b2"]).then_inc(loaded, 16)
                sp.dma_start(order[:], d["order64"].partition_broadcast(P)).then_inc(loaded, 16)

            @block.tensor
            def _(pe):
                pe.wait_ge(loaded, 64)
                for g in range(GROUPS):
                    pe.matmul(pr[g][0:R1, :], wr[:], xT[:, g * BANK:(g + 1) * BANK], start=True, stop=True)\
                        .then_inc(r_made, 1)
                for b in range(B):
                    pe.wait_ge(r_ready, b // GROUP + 1)
                    mm = pe.matmul(pl[:, b * E1:(b + 1) * E1], rT[:, b * T:(b + 1) * T], cb[:], start=True, stop=True)
                mm.then_inc(logits_made, 1)
                pe.wait_ge(combined, 1)
                for b in range(B):
                    mm = pe.transpose(pr[b // GROUP][0:E1, (b % GROUP) * T:(b % GROUP + 1) * T], combine[:, :, b],
                                      core.ident[:])
                    if b % GROUP == GROUP - 1:
                        mm.then_inc(c_turned, 1)
                for g in range(GROUPS):
                    pe.wait_ge(c_ready, g + 1)
                    for k in range(GROUP):
                        b = g * GROUP + k
                        mm = pe.matmul(pr[g][:, k * D:(k + 1) * D], cT[:, b * T:(b + 1) * T], b2[:], start=True, stop=True)
                    mm.then_inc(made, 1)

            @block.scalar
            def _(act):
                for g in range(GROUPS):
                    act.wait_ge(r_made, g + 1)
                    act.activation(rT[:, g * BANK:(g + 1) * BANK], pr[g][0:R1, :], ACT.Copy).then_inc(r_ready, 1)
                act.wait_ge(lowered, 1)
                act.activation(prob[:], prob[:], ACT.Exp, scale=1.0 / 0.7).then_inc(exp_ready, 1)
                for g in range(GROUPS):
                    act.wait_ge(c_turned, g + 1)
                    act.activation(cT[:, g * BANK:(g + 1) * BANK], pr[g][0:E1, :], ACT.Copy).then_inc(c_ready, 1)

            @block.vector
            def _(dve):
                link = Link(dve, dve_step)
                dve.wait_ge(loaded, 64)
                dve.wait_ge(logits_made, 1)
                logits = pl[:].rearrange("p (b e) -> p b e", e=E1)
                link(dve.tensor_reduce(top[:], logits, AX.X, ALU.max))
                dve.tensor_tensor(prob[:], logits, over_last(top[:], E1), ALU.subtract).then_inc(lowered, 1)
                dve.wait_ge(exp_ready, 1)
                link(dve.tensor_reduce(top[:], prob[:], AX.X, ALU.add))
                link(dve.reciprocal(top[:], top[:]))
                link(dve.tensor_tensor(prob[:], prob[:], over_last(top[:], E1), ALU.mult))
                first_hot(link, dve, hot[:], best1[:], prob[:], order[:], key[:], kb[:])
                link(dve.scalar_tensor_tensor(rest[:], hot[:], -2.0, prob[:], ALU.mult, ALU.add))
                link(dve.tensor_reduce(best2[:], rest[:], AX.X, ALU.max))
                link(dve.tensor_tensor(total[:], best1[:], best2[:], ALU.add))
                link(dve.reciprocal(total[:], total[:]))
                link(dve.tensor_tensor(best1[:], best1[:], total[:], ALU.mult))
                link(dve.tensor_tensor(combine.rearrange("p e b -> p b e"), hot[:], over_last(best1[:], E1), ALU.mult))
                first_hot(link, dve, hot[:], best2[:], rest[:], order[:], key[:], kb[:])
                link(dve.tensor_tensor(best2[:], best2[:], total[:], ALU.mult))
                link(dve.tensor_tensor(hot[:], hot[:], over_last(best2[:], E1), ALU.mult))
                dve.tensor_tensor(combine.rearrange("p e b -> p b e"), combine.rearrange("p e b -> p b e"), hot[:],
                                  ALU.add).then_inc(combined, 1)
                for g in range(GROUPS):
                    dve.wait_ge(made, g + 1)
                    dve.tensor_copy(flat(dst)[:, g * BANK:(g + 1) * BANK], pr[g][:]).then_inc(done, 1)
                dve.wait_ge(done, GROUPS)


def experts64(nc, core, d, xT, combine, dst):
    with Stage(nc, "e1") as s:
        w1 = [s.sb(f"w1{p}", [P, F1 * P]) for p in range(2)]
        w2 = [s.sb(f"w2{p}", [P, F1, D]) for p in range(2)]
        b1 = s.sb("b1", [P, E1 * F1])
        b1_here = [s.sb(f"b1_here{p}", [P, F1]) for p in range(2)]
        mid = [s.sb(f"mid{q}", [P, F1, BANK]) for q in range(2)]
        part = s.sb("part", [P, GROUP, D])
        up = [s.ps(f"up{c}", [P, BANK]) for c in range(F1)]
        down = [s.ps(f"down{q}", [P, BANK]) for q in range(2)]
        b1_in, made, mid_ready, out_made, weighted, added = (s.sem(n) for n in (
            "b1_in", "made", "mid_ready", "out_made", "weighted", "added"))
        w_in, b1_ready = s.pair("w_in"), s.pair("b1_ready")
        s.start_at_one(added, out_made, mid_ready, weighted)
        with nc.Block() as block:
            @block.sync
            def _(sp):
                sp.dma_start(b1[:], d["L1f_b1"]).then_inc(b1_in, 16)

                def load(e, p):
                    sp.dma_start(w1[p][:], d["L1f_W1"][bass.ds(e, 1), :, :].rearrange("e k n -> k (e n)"))\
                        .then_inc(w_in[p], 16)
                    sp.dma_start(w2[p][:], d["L1f_W2"][bass.ds(e, 1), :, :].rearrange(
                        "e (c k) n -> k (e c) n", k=P)).then_inc(w_in[p], 16)

                for p in range(2):
                    load(p, p)
                with sp.Fori(1, E1 // 2) as j:
                    for p in range(2):
                        sp.wait_ge(out_made, (2 * j + p - 1) * GROUPS + 1)
                        load(2 * j + p, p)

            @block.tensor
            def _(pe):
                with pe.Fori(0, E1 // 2) as j:
                    def up_group(p, g):
                        i = (2 * j + p) * GROUPS + g
                        for c in range(F1):
                            pe.wait_ge(mid_ready, i * F1 - (F1 - c - 1) + 1 if (p or g) else i * F1 + 1)
                            pe.matmul(up[c][:], w1[p][:, c * P:(c + 1) * P], xT[:, g * BANK:(g + 1) * BANK],
                                      start=True, stop=True).then_inc(made, 1)

                    def down_group(p, g):
                        i = (2 * j + p) * GROUPS + g
                        pe.wait_ge(mid_ready, i * F1 + F1 + 1)
                        pe.wait_ge(weighted, i if (p or g >= 1) else i + 1)
                        for k in range(GROUP):
                            for c in range(F1):
                                mm = pe.matmul(down[g % 2][:, k * D:(k + 1) * D], mid[g % 2][:, c, k * T:(k + 1) * T],
                                               w2[p][:, c, :], start=(c == 0), stop=(c == F1 - 1))
                        mm.then_inc(out_made, 1)

                    for p in range(2):
                        pe.wait_ge(w_in[p], 32 * j + 32)
                        up_group(p, 0)
                        for g in range(1, GROUPS):
                            up_group(p, g)
                            down_group(p, g - 1)
                        down_group(p, GROUPS - 1)

            @block.scalar
            def _(act):
                act.wait_ge(b1_in, 16)
                with act.Fori(0, E1 // 2) as j:
                    for p in range(2):
                        act.activation(b1_here[p][:], b1[:, bass.ds((2 * j + p) * F1, F1)], ACT.Copy)\
                            .then_inc(b1_ready[p], 1)
                        act.wait_ge(b1_ready[p], j + 1)
                        for g in range(GROUPS):
                            i = (2 * j + p) * GROUPS + g
                            act.wait_ge(out_made, i if (p or g >= 1) else i + 1)
                            for c in range(F1):
                                act.wait_ge(made, i * F1 + c + 1)
                                act.activation(mid[g % 2][:, c, :], up[c][:], ACT.Silu, bias=b1_here[p][:, c:c + 1])\
                                    .then_inc(mid_ready, 1)

            @block.vector
            def _(dve):
                with dve.Fori(0, E1 // 2) as j:
                    for p in range(2):
                        for g in range(GROUPS):
                            i = (2 * j + p) * GROUPS + g
                            dve.wait_ge(out_made, i + 2)
                            dve.wait_ge(added, i + 1)
                            dve.tensor_tensor(part[:], down[g % 2][:].rearrange("p (b d) -> p b d", d=D),
                                              over_last(combine[:, bass.ds((2 * j + p) * B + g * GROUP, GROUP)], D),
                                              ALU.mult).then_inc(weighted, 1)
                            dve.wait_ge(weighted, i + 2)
                            here = flat(dst)[:, g * BANK:(g + 1) * BANK]
                            dve.tensor_tensor(here, here, flat(part[:]), ALU.add).then_inc(added, 1)
                dve.wait_ge(added, E1 * GROUPS + 1)


def add_all(nc, name, dst, terms):
    with Stage(nc, name) as s:
        added = s.sem("added")
        with nc.Block() as block:
            @block.vector
            def _(dve):
                link = Link(dve, added)
                for x in terms:
                    link(dve.tensor_tensor(dst, dst, x, ALU.add))


def l1_ffn(nc, core, d):
    with ExitStack() as st:
        def sb(n, shape):
            return st.enter_context(nc.sbuf_tensor(f"l1f_{n}", shape, F32))

        u, x, xT, hmoe, combine = (sb("u", [P, B, D]), sb("x", [P, B, D]), sb("xT", [P, N]), sb("hmoe", [P, B, D]),
                                   sb("combine", [P, E1, B]))
        layer_norm(nc, "l1f_n", core.h[:], u[:], 1e-5)
        layer_norm(nc, "l1f_n1", u[:], x[:], 1e-5, d["L1f_ln1"])
        to_features(nc, "l1f_t", core, x[:], xT[:])
        router64(nc, core, d, xT[:], combine[:], hmoe[:])
        experts64(nc, core, d, xT[:], combine[:].rearrange("p e b -> p (e b)"), hmoe[:])
        mlp(nc, "l1f_s", core, xT[:], d["L1f_Ws1"], d["L1f_bs1"], d["L1f_Ws2"], d["L1f_bs2"], 256, ACT.Silu, hmoe[:],
            scale=0.25)
        layer_norm(nc, "l1f_n2", hmoe[:], x[:], 1e-5, d["L1f_ffln"])
        to_features(nc, "l1f_t2", core, x[:], xT[:])
        add_all(nc, "l1f_a", core.h[:], (u[:], hmoe[:]))
        mlp(nc, "l1f_f", core, xT[:], d["L1f_Wf1"], d["L1f_bf1"], d["L1f_Wf2"], d["L1f_bf2"], 512, ACT.Silu, core.h[:])


QN = 8


def l2_attention(nc, core, d):
    W6 = 6 * D
    with ExitStack() as st:
        def sb(n, shape):
            return st.enter_context(nc.sbuf_tensor(f"l2a_{n}", shape, F32))

        u, uT = sb("u", [P, B, D]), sb("uT", [P, N])
        layer_norm(nc, "l2a_n", core.h[:], u[:], 1e-5)
        to_features(nc, "l2a_t", core, u[:], uT[:])
        with Stage(nc, "l2a") as s:
            w, bias = s.sb("w", [P, W6]), s.sb("bias", [P, W6])

            def two(n, shape):
                return [s.sb(f"{n}{p}", shape) for p in range(2)]

            xs, lin, low = two("xs", [P, T]), two("lin", [P, W6]), two("low", [P, D])
            f, fsum, fmax = two("f", [P, D]), two("fsum", [P, 1]), two("fmax", [P, 1])
            high_k, low_k, other = two("high_k", [P, 1]), two("low_k", [P, 1]), two("other", [P, D])
            e, ev = two("e", [P, QN, D]), two("ev", [P, QN, D])
            mass, ctx = two("mass", [P, D]), two("ctx", [P, D])
            ps = [s.ps(f"ps{p}", [P, 2 * BANK]) for p in range(2)]
            loaded = s.sem("loaded")
            x_in, made, lin_ready, f_low, f_exp, low_ready, batch_done, dve_step = (s.pair(n) for n in (
                "x_in", "made", "lin_ready", "f_low", "f_exp", "low_ready", "batch_done", "dve_step"))
            e_ready, e_used, ev_ready = s.sem("e_ready"), s.sem("e_used"), s.sem("ev_ready")
            NQ = D // QN
            s.start_at_one(*batch_done, *lin_ready, e_used)
            with nc.Block() as block:
                @block.sync
                def _(sp):
                    sp.dma_start(w[:], d["L2a_w"]).then_inc(loaded, 16)
                    sp.dma_start(bias[:], d["L2a_b"].partition_broadcast(P)).then_inc(loaded, 16)

                @block.tensor
                def _(pe):
                    pe.wait_ge(loaded, 32)
                    with pe.Fori(0, B // 2) as j:
                        for p in range(2):
                            pe.wait_ge(x_in[p], j + 1)
                            pe.wait_ge(lin_ready[p], j + 1)
                            pe.matmul(ps[p][:, 0:BANK], xs[p][:], w[:, 0:BANK], start=True, stop=True)
                            pe.matmul(ps[p][:, BANK:W6], xs[p][:], w[:, BANK:W6], start=True, stop=True)\
                                .then_inc(made[p], 1)

                @block.scalar
                def _(act):
                    with act.Fori(0, B // 2) as j:
                        for p in range(2):
                            act.wait_ge(batch_done[p], j + 1)
                            act.activation(xs[p][:], uT[:, bass.ds((2 * j + p) * T, T)], ACT.Copy).then_inc(x_in[p], 1)
                        for p in range(2):
                            act.wait_ge(f_low[p], j + 1)
                            act.activation(f[p][:], f[p][:], ACT.Exp).then_inc(f_exp[p], 1)
                        for p in range(2):
                            act.wait_ge(low_ready[p], j + 1)
                            for n in range(NQ):
                                act.wait_ge(e_used, (2 * j + p) * NQ + n if (p or n) else 2 * j * NQ + 1)
                                for q in range(QN):
                                    i = n * QN + q
                                    ins = act.activation(e[n % 2][:, q, :], lin[p][:, 4 * D:5 * D], ACT.Exp,
                                                         scale=lin[p][:, 3 * D + i:3 * D + i + 1], bias=low[p][:, i:i + 1])
                                ins.then_inc(e_ready, 1)

                @block.vector
                def _(dve):
                    dve.wait_ge(loaded, 32)
                    with dve.Fori(0, B // 2) as j:
                        links = [Link(dve, dve_step[p], j * 13) for p in range(2)]
                        for p in range(2):
                            link = links[p]
                            qf, kf, vf, qt, kt, vt = (lin[p][:, k * D:(k + 1) * D] for k in range(6))
                            dve.wait_ge(made[p], j + 1)
                            dve.tensor_tensor(lin[p][:], ps[p][:, 0:W6], bias[:], ALU.add).then_inc(lin_ready[p], 1)
                            dve.wait_ge(lin_ready[p], j + 2)
                            link(dve.tensor_reduce(high_k[p][:], kt, AX.X, ALU.max))
                            link(dve.tensor_reduce(low_k[p][:], kt, AX.X, ALU.min))
                            link(dve.tensor_scalar(other[p][:], qt, low_k[p][:], None, ALU.mult))
                            link(dve.scalar_tensor_tensor(low[p][:], qt, high_k[p][:], other[p][:], ALU.mult, ALU.max))
                            dve.tensor_scalar(low[p][:], low[p][:], -1.0, None, ALU.mult).then_inc(low_ready[p], 1)
                            link(dve.tensor_tensor(f[p][:], qf, kf, ALU.mult))
                            link(dve.tensor_reduce(fmax[p][:], f[p][:], AX.X, ALU.max))
                            dve.tensor_scalar(f[p][:], f[p][:], fmax[p][:], None, ALU.subtract).then_inc(f_low[p], 1)
                        for p in range(2):
                            link = links[p]
                            vf, vt = lin[p][:, 2 * D:3 * D], lin[p][:, 5 * D:6 * D]
                            dve.wait_ge(f_exp[p], j + 1)
                            link(dve.tensor_reduce(fsum[p][:], f[p][:], AX.X, ALU.add))
                            link(dve.reciprocal(fsum[p][:], fsum[p][:]))
                            link(dve.scalar_tensor_tensor(f[p][:], f[p][:], fsum[p][:], vf, ALU.mult, ALU.mult))
                            for n in range(NQ):
                                dve.wait_ge(e_ready, (2 * j + p) * NQ + n + 1)
                                dve.tensor_tensor(ev[n % 2][:], e[n % 2][:], over_mid(vt, QN), ALU.mult)\
                                    .then_inc(ev_ready, 1)
                                dve.tensor_reduce(mass[p][:, n * QN:(n + 1) * QN], e[n % 2][:], AX.X, ALU.add)\
                                    .then_inc(e_used, 1)
                                dve.wait_ge(ev_ready, (2 * j + p) * NQ + n + 1)
                                ins = dve.tensor_reduce(ctx[p][:, n * QN:(n + 1) * QN], ev[n % 2][:], AX.X, ALU.add)
                            dve.wait_ge(e_used, (2 * j + p + 1) * NQ + 1)
                            link(ins)
                            link(dve.reciprocal(mass[p][:], mass[p][:]))
                            link(dve.tensor_tensor(ctx[p][:], ctx[p][:], mass[p][:], ALU.mult))
                            here = flat(core.h[:])[:, bass.ds((2 * j + p) * D, D)]
                            link(dve.tensor_tensor(ctx[p][:], ctx[p][:], f[p][:], ALU.add))
                            dve.tensor_tensor(here, here, ctx[p][:], ALU.add).then_inc(batch_done[p], 1)
                    for p in range(2):
                        dve.wait_ge(batch_done[p], B // 2 + 1)


E2 = 8


def router8(nc, core, d, u, uT, combine, dst):
    with Stage(nc, "r2") as s:
        wr, br, order, index, last = (s.sb("wr", [P, E2]), s.sb("br", [P, E2]), s.sb("order", [P, E2]),
                                      s.sb("index", [P, E2]), s.sb("last", [P, B]))
        ones = s.sb("ones", [P, P])
        logit, rest, key, hot1, hot2, cut = (s.sb(n, [P, B, E2]) for n in ("logit", "rest", "key", "hot1", "hot2", "cut"))
        best1, best2, kb, e2, s1, s2, v1, v2, a1, a2, w1 = (s.sb(n, [P, B]) for n in (
            "best1", "best2", "kb", "e2", "s1", "s2", "v1", "v2", "a1", "a2", "w1"))
        count, full = s.sb("count", [P, 2, E2]), s.sb("full", [P, 2, E2])
        pl, pc = s.ps("pl", [P, BANK]), s.ps("pc", [P, BANK])
        loaded, dve_step, made, gap_ready, exp_ready, counted, total_ready = (s.sem(n) for n in (
            "loaded", "dve_step", "made", "gap_ready", "exp_ready", "counted", "total_ready"))
        with nc.Block() as block:
            @block.sync
            def _(sp):
                sp.dma_start(wr[:], d["L2f_Wr"]).then_inc(loaded, 16)
                for dst_, src in ((br, "L2f_br"), (order, "order8"), (index, "index8")):
                    sp.dma_start(dst_[:], d[src].partition_broadcast(P)).then_inc(loaded, 16)
                sp.dma_start(last[:], d["last_token"]).then_inc(loaded, 16)

            @block.tensor
            def _(pe):
                pe.wait_ge(loaded, 80)
                for b in range(B):
                    mm = pe.matmul(pl[:, b * E2:(b + 1) * E2], uT[:, b * T:(b + 1) * T], wr[:], start=True, stop=True)
                mm.then_inc(made, 1)
                pe.wait_ge(counted, 1)
                pe.matmul(pc[:, 0:2 * E2], ones[:], count[:].rearrange("p a e -> p (a e)"), start=True, stop=True)\
                    .then_inc(total_ready, 1)

            @block.scalar
            def _(act):
                act.wait_ge(gap_ready, 1)
                act.activation(e2[:], e2[:], ACT.Exp).then_inc(exp_ready, 1)

            @block.vector
            def _(dve):
                link = Link(dve, dve_step)
                dve.wait_ge(loaded, 80)
                link(dve.memset(ones[:], 1.0))
                dve.wait_ge(made, 1)
                link(dve.tensor_tensor(logit[:], pl[:, 0:B * E2].rearrange("p (b e) -> p b e", e=E2),
                                       over_mid(br[:], B), ALU.add))
                first_hot(link, dve, hot1[:], best1[:], logit[:], order[:], key[:], kb[:])
                link(dve.scalar_tensor_tensor(rest[:], hot1[:], NEVER, logit[:], ALU.mult, ALU.add))
                first_hot(link, dve, hot2[:], best2[:], rest[:], order[:], key[:], kb[:])
                dve.tensor_tensor(e2[:], best2[:], best1[:], ALU.subtract).then_inc(gap_ready, 1)
                dve.wait_ge(exp_ready, 1)
                link(dve.tensor_scalar(s1[:], e2[:], 1.0, None, ALU.add))
                link(dve.reciprocal(s1[:], s1[:]))
                link(dve.tensor_tensor(s2[:], s1[:], e2[:], ALU.mult))
                link(dve.tensor_reduce(count[:, 0, :], hot1[:].rearrange("p b e -> p e b"), AX.X, ALU.add))
                link(dve.tensor_reduce(count[:, 1, :], hot2[:].rearrange("p b e -> p e b"), AX.X, ALU.add))
                dve.tensor_tensor(count[:, 1, :], count[:, 1, :], count[:, 0, :], ALU.add).then_inc(counted, 1)
                dve.wait_ge(total_ready, 1)
                link(dve.tensor_scalar(full[:].rearrange("p a e -> p (a e)"), pc[:, 0:2 * E2], float(N), None, ALU.is_ge))
                for n, (hot, valid, expert) in enumerate(((hot1, v1, a1), (hot2, v2, a2))):
                    link(dve.tensor_tensor(cut[:], over_last(last[:], E2), over_mid(full[:, n, :], B), ALU.mult))
                    link(dve.tensor_scalar(cut[:], cut[:], -1.0, 1.0, ALU.mult, ALU.add))
                    link(dve.tensor_tensor(hot[:], hot[:], cut[:], ALU.mult))
                    link(dve.tensor_reduce(valid[:], hot[:], AX.X, ALU.add))
                    link(dve.tensor_tensor(cut[:], hot[:], over_mid(index[:], B), ALU.mult))
                    link(dve.tensor_reduce(expert[:], cut[:], AX.X, ALU.add))
                link(dve.tensor_tensor(a1[:], a1[:], a2[:], ALU.max))
                link(dve.tensor_tensor(cut[:], over_last(a1[:], E2), over_mid(index[:], B), ALU.is_equal))
                link(dve.tensor_tensor(v1[:], v1[:], s1[:], ALU.mult))
                link(dve.tensor_tensor(v2[:], v2[:], s2[:], ALU.mult))
                link(dve.tensor_tensor(w1[:], v1[:], v2[:], ALU.add))
                link(dve.tensor_tensor(combine.rearrange("p e b -> p b e"), cut[:], over_last(w1[:], E2), ALU.mult))
                link(dve.tensor_tensor(s1[:], s1[:], v1[:], ALU.subtract))
                link(dve.tensor_tensor(s2[:], s2[:], v2[:], ALU.subtract))
                link(dve.tensor_tensor(s1[:], s1[:], s2[:], ALU.add))
                link(dve.tensor_tensor(dst, u, over_last(s1[:], D), ALU.mult))


def experts8(nc, core, d, xT, combine, dst):
    with Stage(nc, "e2") as s:
        w12 = [s.sb(f"w12{p}", [P, 2, F1 * P]) for p in range(2)]
        w3 = [s.sb(f"w3{p}", [P, F1, D]) for p in range(2)]
        left, prod = ([s.sb(f"{n}{q}", [P, BANK]) for q in range(2)] for n in ("left", "prod"))
        mid = [s.sb(f"mid{q}", [P, F1, BANK]) for q in range(2)]
        part = s.sb("part", [P, GROUP, D])
        up1, up2 = ([s.ps(f"{n}{q}", [P, BANK]) for q in range(2)] for n in ("upa", "upb"))
        down = [s.ps(f"down{q}", [P, BANK]) for q in range(2)]
        made, left_ready, prod_ready, mid_ready, out_made, weighted, added = (s.sem(n) for n in (
            "made", "left_ready", "prod_ready", "mid_ready", "out_made", "weighted", "added"))
        w_in = s.pair("w_in")
        STEPS = GROUPS * F1
        s.start_at_one(added, out_made, mid_ready, weighted, prod_ready)
        with nc.Block() as block:
            @block.sync
            def _(sp):
                def load(e, p):
                    for n, src in enumerate(("L2f_W1", "L2f_W2")):
                        sp.dma_start(w12[p][:, n, :], d[src][bass.ds(e, 1), :, :].rearrange("e k n -> k (e n)"))\
                            .then_inc(w_in[p], 16)
                    sp.dma_start(w3[p][:], d["L2f_W3"][bass.ds(e, 1), :, :].rearrange("e (c k) n -> k (e c) n", k=P))\
                        .then_inc(w_in[p], 16)

                for p in range(2):
                    load(p, p)
                with sp.Fori(1, E2 // 2) as j:
                    for p in range(2):
                        sp.wait_ge(out_made, (2 * j + p - 1) * GROUPS + 1)
                        load(2 * j + p, p)

            @block.tensor
            def _(pe):
                with pe.Fori(0, E2 // 2) as j:
                    def down_group(p, g):
                        i = (2 * j + p) * GROUPS + g
                        pe.wait_ge(mid_ready, i * F1 + F1 + 1)
                        pe.wait_ge(weighted, i if (p or g >= 1) else i + 1)
                        for k in range(GROUP):
                            for c in range(F1):
                                mm = pe.matmul(down[g % 2][:, k * D:(k + 1) * D], mid[g % 2][:, c, k * T:(k + 1) * T],
                                               w3[p][:, c, :], start=(c == 0), stop=(c == F1 - 1))
                        mm.then_inc(out_made, 1)

                    for p in range(2):
                        pe.wait_ge(w_in[p], 48 * j + 48)
                        for g in range(GROUPS):
                            for c in range(F1):
                                k = (2 * j + p) * STEPS + g * F1 + c
                                pe.wait_ge(prod_ready, k if (p or g or c) else k + 1)
                                pe.matmul(up1[c % 2][:], w12[p][:, 0, c * P:(c + 1) * P],
                                          xT[:, g * BANK:(g + 1) * BANK], start=True, stop=True)
                                pe.matmul(up2[c % 2][:], w12[p][:, 1, c * P:(c + 1) * P],
                                          xT[:, g * BANK:(g + 1) * BANK], start=True, stop=True).then_inc(made, 1)
                            if g:
                                down_group(p, g - 1)
                        down_group(p, GROUPS - 1)

            @block.scalar
            def _(act):
                with act.Fori(0, E2 // 2) as j:
                    for p in range(2):
                        base = (2 * j + p) * STEPS

                        def take_left(k):
                            act.wait_ge(made, base + k + 1)
                            act.activation(left[k % 2][:], up1[k % 2][:], ACT.Copy).then_inc(left_ready, 1)

                        take_left(0)
                        for k in range(STEPS):
                            if k + 1 < STEPS:
                                take_left(k + 1)
                            if k % F1 == 0:
                                g = k // F1
                                i = (2 * j + p) * GROUPS + g
                                act.wait_ge(out_made, i if (p or g >= 1) else i + 1)
                            act.wait_ge(prod_ready, base + k + 2)
                            act.activation(mid[k // F1 % 2][:, k % F1, :], prod[k % 2][:], ACT.Gelu).then_inc(mid_ready, 1)

            @block.vector
            def _(dve):
                with dve.Fori(0, E2 // 2) as j:
                    for p in range(2):
                        def weigh(g):
                            i = (2 * j + p) * GROUPS + g
                            dve.wait_ge(out_made, i + 2)
                            dve.wait_ge(added, i + 1)
                            dve.tensor_tensor(part[:], down[g % 2][:].rearrange("p (b d) -> p b d", d=D),
                                              over_last(combine[:, bass.ds((2 * j + p) * B + g * GROUP, GROUP)], D),
                                              ALU.mult).then_inc(weighted, 1)
                            dve.wait_ge(weighted, i + 2)
                            here = flat(dst)[:, g * BANK:(g + 1) * BANK]
                            dve.tensor_tensor(here, here, flat(part[:]), ALU.add).then_inc(added, 1)

                        for k in range(STEPS):
                            n = (2 * j + p) * STEPS + k
                            dve.wait_ge(left_ready, n + 1)
                            dve.wait_ge(mid_ready, n if (p or k) else n + 1)
                            dve.tensor_tensor(prod[k % 2][:], left[k % 2][:], up2[k % 2][:], ALU.mult)\
                                .then_inc(prod_ready, 1)
                            if k % F1 == 2 and k > F1:
                                weigh(k // F1 - 1)
                        weigh(GROUPS - 1)
                dve.wait_ge(added, E2 * GROUPS + 1)


def l2_ffn(nc, core, d):
    with ExitStack() as st:
        def sb(n, shape):
            return st.enter_context(nc.sbuf_tensor(f"l2f_{n}", shape, F32))

        u, uT, y, combine = sb("u", [P, B, D]), sb("uT", [P, N]), sb("y", [P, B, D]), sb("combine", [P, E2, B])
        layer_norm(nc, "l2f_n", core.h[:], u[:], 1e-5)
        to_features(nc, "l2f_t", core, u[:], uT[:])
        router8(nc, core, d, u[:], uT[:], combine[:], y[:])
        experts8(nc, core, d, uT[:], combine[:].rearrange("p e b -> p (e b)"), y[:])
        add_all(nc, "l2f_a", core.h[:], (y[:],))


DI, DS, DR, DC = 256, 16, 8, 4
CI = DI // P


def mamba_inputs(nc, core, d, uT, xa, gate, dt, dtu, bc_dram):
    with Stage(nc, "mi") as s:
        w_in, w_x, w_dt = s.sb("w_in", [P, 2 * DI]), s.sb("w_x", [P, CI, DR + 2 * DS]), s.sb("w_dt", [DR, DI])
        conv_w, conv_b, dt_b = s.sb("conv_w", [P, CI, DC]), s.sb("conv_b", [P, CI]), s.sb("dt_b", [P, CI])
        pad = s.sb("pad", [P, CI, B, T + DC - 1])
        dbl = s.sb("dbl", [DR + 2 * DS, N])
        mag = s.sb("mag", [P, CI, N])
        ratio = pad[:].rearrange("p c b t -> p (c b t)")[:, 0:CI * N].rearrange("p (c n) -> p c n", c=CI)
        ps = [s.ps(f"ps{i}", [P, BANK]) for i in range(8)]
        loaded, dve_step, made, evacuated, conv_ready, xa_ready, dbl_made, dbl_ready, stored, dt_made, to_act, from_act = (
            s.sem(n) for n in ("loaded", "dve_step", "made", "evacuated", "conv_ready", "xa_ready", "dbl_made",
                               "dbl_ready", "stored", "dt_made", "to_act", "from_act"))
        with nc.Block() as block:
            @block.sync
            def _(sp):
                for dst, src in ((w_in, "L3a_in"), (w_x, "L3a_x"), (w_dt, "L3a_dt"), (conv_w, "L3a_conv_w"),
                                 (conv_b, "L3a_conv_b"), (dt_b, "L3a_dt_b")):
                    sp.dma_start(dst[:], d[src]).then_inc(loaded, 16)
                sp.wait_ge(dbl_ready, 4)
                sp.dma_start(bc_dram, dbl[DR:, :]).then_inc(stored, 16)
                sp.wait_ge(stored, 16)

            @block.tensor
            def _(pe):
                pe.wait_ge(loaded, 96)
                for i in range(16):
                    c, g = i // 4, i % 4
                    if i >= 8:
                        pe.wait_ge(evacuated, i - 7)
                    pe.matmul(ps[i % 8][:], w_in[:, c * P:(c + 1) * P], uT[:, g * BANK:(g + 1) * BANK],
                              start=True, stop=True).then_inc(made, 1)
                pe.wait_ge(xa_ready, CI)
                pe.wait_ge(evacuated, 16)
                for g in range(4):
                    for c in range(CI):
                        mm = pe.matmul(ps[g][0:DR + 2 * DS, :], w_x[:, c, :], xa[:, c, g * BANK:(g + 1) * BANK],
                                       start=(c == 0), stop=(c == CI - 1))
                    mm.then_inc(dbl_made, 1)
                pe.wait_ge(dbl_ready, 4)
                for i in range(4 * CI):
                    c, g = i // 4, i % 4
                    pe.matmul(ps[i][:], w_dt[:, c * P:(c + 1) * P], dbl[0:DR, g * BANK:(g + 1) * BANK],
                              start=True, stop=True).then_inc(dt_made, 1)

            @block.scalar
            def _(act):
                act.wait_ge(loaded, 96)
                for i in range(16):
                    c, g = i // 4, i % 4
                    act.wait_ge(made, i + 1)
                    if c < CI:
                        act.activation(pad[:, c, 4 * g:4 * g + 4, DC - 1:], ps[i % 8][:].rearrange(
                            "p (b t) -> p b t", t=T), ACT.Copy).then_inc(evacuated, 1)
                    else:
                        act.activation(gate[:, c - CI, g * BANK:(g + 1) * BANK], ps[i % 8][:], ACT.Silu)\
                            .then_inc(evacuated, 1)
                for c in range(CI):
                    act.wait_ge(conv_ready, c + 1)
                    act.activation(xa[:, c, :], xa[:, c, :], ACT.Silu).then_inc(xa_ready, 1)
                for g in range(4):
                    act.wait_ge(dbl_made, g + 1)
                    act.activation(dbl[:, g * BANK:(g + 1) * BANK], ps[g][0:DR + 2 * DS, :], ACT.Copy)\
                        .then_inc(dbl_ready, 1)
                for i in range(4 * CI):
                    c, g = i // 4, i % 4
                    act.wait_ge(dt_made, i + 1)
                    act.activation(dt[:, c, g * BANK:(g + 1) * BANK], ps[i][:], ACT.Identity, bias=dt_b[:, c:c + 1])\
                        .then_inc(from_act, 1)
                act.wait_ge(to_act, 1)
                act.activation(mag[:], mag[:], ACT.Exp, scale=-1.0).then_inc(from_act, 1)

            @block.vector
            def _(dve):
                link = Link(dve, dve_step)
                link(dve.memset(pad[:, :, :, 0:DC - 1], 0.0))
                dve.wait_ge(evacuated, 4 * CI)
                for c in range(CI):
                    out3 = xa[:, c, :].rearrange("p (b t) -> p b t", t=T)
                    link(dve.tensor_scalar(out3, pad[:, c, :, 0:T], conv_w[:, c, 0:1], conv_b[:, c:c + 1],
                                           ALU.mult, ALU.add))
                    for k in range(1, DC):
                        link(dve.scalar_tensor_tensor(out3, pad[:, c, :, k:k + T], conv_w[:, c, k:k + 1], out3,
                                                      ALU.mult, ALU.add))
                    dve.sem_inc(conv_ready, 1)
                dve.wait_ge(from_act, 4 * CI)
                dve.scalar_tensor_tensor(mag[:], dt, -1.0, dt, ALU.mult, ALU.max).then_inc(to_act, 1)
                dve.wait_ge(to_act, 1)
                link(dve.tensor_scalar(dt, dt, 0.0, None, ALU.max))
                dve.wait_ge(from_act, 4 * CI + 1)
                log1p(link, dve, mag[:], ratio, dtu)
                link(dve.tensor_tensor(dt, dt, mag[:], ALU.add))
                dve.wait_ge(xa_ready, CI)
                link(dve.tensor_tensor(dtu, dt, xa, ALU.mult))


def mamba_scan(nc, core, d, xa, gate, dt, dtu, bc_dram, yT):
    with Stage(nc, "ms") as s:
        a, skip, w_out = s.sb("a", [P, CI * DS]), s.sb("skip", [P, CI]), s.sb("w_out", [P, CI, D])
        a_here = [s.sb(f"a_here{p}", [P, CI]) for p in range(2)]
        bn, cn = ([s.sb(f"{n}{p}", [P, N]) for p in range(2)] for n in ("bn", "cn"))
        decay, fed, state = ([s.sb(f"{n}{c}", [P, N]) for c in range(CI)] for n in ("decay", "fed", "state"))
        py = [s.ps(f"py{c}", [P, N]) for c in range(CI)]
        loaded, a_ready, a_copied = s.sem("loaded"), s.sem("a_ready"), s.sem("a_copied")
        bc_in = s.pair("bc_in")
        decay_ready, fed_ready, scanned, read, summed, dve_step = ([s.sem(f"{n}{c}") for c in range(CI)] for n in (
            "decay_ready", "fed_ready", "scanned", "read", "summed", "dve_step"))
        mixed, projected, out_ready = s.sem("mixed"), s.sem("projected"), s.sem("out_ready")

        def over_states(eng, turn):
            turn(0, 0, True)
            turn(1, 1, False)
            with eng.Fori(1, DS // 2) as j:
                for p in range(2):
                    turn(2 * j + p, p, False)

        with nc.Block() as block:
            @block.sync
            def _(sp):
                sp.dma_start(a[:], d["L3a_A_log"]).then_inc(loaded, 16)
                sp.dma_start(skip[:], d["L3a_D"]).then_inc(loaded, 16)
                sp.dma_start(w_out[:], d["L3a_out"]).then_inc(loaded, 16)

                def turn(n, p, first):
                    if not isinstance(n, int):
                        sp.wait_ge(read[CI - 1], n - 1)
                        sp.wait_ge(fed_ready[CI - 1], n - 1)
                    for half, dst in ((0, bn), (1, cn)):
                        sp.dma_start(dst[p][:], bc_dram[bass.ds(n + half * DS, 1), :].rearrange("a n -> (a n)")
                                     .partition_broadcast(P)).then_inc(bc_in[p], 16)

                over_states(sp, turn)

            @block.gpsimd
            def _(pool):
                def turn(n, p, first):
                    turns = n // 2 if isinstance(n, int) else (n - p) // 2
                    pool.wait_ge(bc_in[p], 32 * turns + 32)
                    for c in range(CI):
                        if not first:
                            pool.wait_ge(scanned[c], n)
                        pool.tensor_tensor(fed[c][:], dtu[:, c, :], bn[p][:], ALU.mult).then_inc(fed_ready[c], 1)

                over_states(pool, turn)

            @block.scalar
            def _(act):
                act.wait_ge(loaded, 48)
                act.activation(a[:], a[:], ACT.Exp).then_inc(a_ready, 1)
                act.wait_ge(a_ready, 2)

                def turn(n, p, first):
                    act.activation(a_here[p][:], a[:, bass.ds(n * CI, CI)], ACT.Copy).then_inc(a_copied, 1)
                    act.wait_ge(a_copied, n + 1)
                    for c in range(CI):
                        if not first:
                            act.wait_ge(scanned[c], n)
                        act.activation(decay[c][:], dt[:, c, :], ACT.Exp, scale=a_here[p][:, c:c + 1])\
                            .then_inc(decay_ready[c], 1)

                over_states(act, turn)
                for g in range(4):
                    act.wait_ge(projected, g + 1)
                    act.activation(yT[:, g * BANK:(g + 1) * BANK], py[0][:, g * BANK:(g + 1) * BANK], ACT.Copy)\
                        .then_inc(out_ready, 1)
                act.wait_ge(out_ready, 4)

            @block.vector
            def _(dve):
                dve.wait_ge(a_ready, 1)
                dve.tensor_scalar(a[:], a[:], -1.0, None, ALU.mult).then_inc(a_ready, 1)

                def turn(n, p, first):
                    for c in range(CI):
                        link = Link(dve, dve_step[c], n)
                        dve.wait_ge(decay_ready[c], n + 1)
                        link(dve.memset(decay[c][:].rearrange("p (b t) -> p b t", t=T)[:, :, 0:1], 0.0))
                        dve.wait_ge(fed_ready[c], n + 1)
                        if not first:
                            dve.wait_ge(summed[c], n)
                        dve.tensor_tensor_scan(state[c][:], decay[c][:], fed[c][:], 0.0, ALU.mult, ALU.add)\
                            .then_inc(scanned[c], 1)
                        dve.wait_ge(scanned[c], n + 1)
                        dve.tensor_tensor(state[c][:], state[c][:], cn[p][:], ALU.mult).then_inc(read[c], 1)

                over_states(dve, turn)
                for c in range(CI):
                    dve.wait_ge(summed[c], DS)
                    for g in range(4):
                        part = slice(g * BANK, (g + 1) * BANK)
                        dve.scalar_tensor_tensor(state[c][:, part], xa[:, c, part], skip[:, c:c + 1], py[c][:, part],
                                                 ALU.mult, ALU.add).then_inc(read[c], 1)
                    dve.wait_ge(read[c], DS + 4)
                    dve.tensor_tensor(state[c][:], state[c][:], gate[:, c, :], ALU.mult).then_inc(mixed, 1)

            @block.tensor
            def _(pe):
                def turn(n, p, first):
                    for c in range(CI):
                        pe.wait_ge(read[c], n + 1)
                        for g in range(4):
                            part = slice(g * BANK, (g + 1) * BANK)
                            mm = pe.matmul(py[c][:, part], core.ident[:], state[c][:, part], start=first, stop=True,
                                           skip_group_check=True)
                        mm.then_inc(summed[c], 1)

                over_states(pe, turn)
                pe.wait_ge(mixed, CI)
                for g in range(4):
                    part = slice(g * BANK, (g + 1) * BANK)
                    for c in range(CI):
                        mm = pe.matmul(py[0][:, part], w_out[:, c, :], state[c][:, part], start=(c == 0),
                                       stop=(c == CI - 1))
                    mm.then_inc(projected, 1)


def l3_attention(nc, core, d):
    with ExitStack() as st:
        def sb(n, shape):
            return st.enter_context(nc.sbuf_tensor(f"l3a_{n}", shape, F32))

        u, yT = sb("u", [P, B, D]), sb("yT", [P, N])
        layer_norm(nc, "l3a_n", core.h[:], u[:], 1e-5)
        to_features(nc, "l3a_t", core, u[:], yT[:])
        xa, gate, dt, dtu = (sb(n, [P, CI, N]) for n in ("xa", "gate", "dt", "dtu"))
        mamba_inputs(nc, core, d, yT[:], xa[:], gate[:], dt[:], dtu[:], core.bc_scratch)
        mamba_scan(nc, core, d, xa[:], gate[:], dt[:], dtu[:], core.bc_scratch, yT[:])
        add_features(nc, "l3a_r", core, yT[:], u[:])
        layer_norm(nc, "l3a_n2", u[:], u[:], 1e-12, d["L3a_ln"])
        add_all(nc, "l3a_a", core.h[:], (u[:],))


def route_sequences(nc, core, d, uT, choice, choice_dram):
    K = 4
    with Stage(nc, "rs") as s:
        w1, b1, w2, b2 = s.sb("w1", [P, P]), s.sb("b1", [P, 1]), s.sb("w2", [P, 2 * K]), s.sb("b2", [B, 2 * K])
        order, index = s.sb("order", [B, K]), s.sb("index", [B, K])
        pooled, mid = s.sb("pooled", [P, B]), s.sb("mid", [P, B])
        route, top = s.sb("route", [B, 2, K]), s.sb("top", [B, 1])
        hot, key, best, kb = s.sb("hot", [B, 2, K]), s.sb("key", [B, 2, K]), s.sb("best", [B, 2]), s.sb("kb", [B, 2])
        whole = s.sb("whole", [B, 2], I32)
        ps = [s.ps(f"ps{i}", [P, BANK]) for i in range(2)]
        loaded, dve_step, pooled_ready, mid_made, mid_ready, made, lowered, exp_ready, chosen, stored, back = (
            s.sem(n) for n in ("loaded", "dve_step", "pooled_ready", "mid_made", "mid_ready", "made", "lowered",
                               "exp_ready", "chosen", "stored", "back"))
        with nc.Block() as block:
            @block.sync
            def _(sp):
                for dst, src in ((w1, "L3f_rw1"), (b1, "L3f_rb1"), (w2, "L3f_rw2")):
                    sp.dma_start(dst[:], d[src]).then_inc(loaded, 16)
                for dst, src in ((b2, "L3f_rb2"), (order, "order4"), (index, "index4")):
                    sp.dma_start(dst[:], d[src].partition_broadcast(B)).then_inc(loaded, 16)
                sp.wait_ge(chosen, 1)
                sp.dma_start(choice_dram, whole[:]).then_inc(stored, 16)
                sp.wait_ge(stored, 16)
                sp.dma_start(choice, choice_dram.rearrange("(a b) k -> a (b k)", a=1)).then_inc(back, 16)
                sp.wait_ge(back, 16)

            @block.tensor
            def _(pe):
                pe.wait_ge(loaded, 96)
                pe.wait_ge(pooled_ready, 1)
                pe.matmul(ps[0][:, 0:B], w1[:], pooled[:], start=True, stop=True).then_inc(mid_made, 1)
                pe.wait_ge(mid_ready, 1)
                pe.matmul(ps[1][0:B, 0:2 * K], mid[:], w2[:], start=True, stop=True).then_inc(made, 1)

            @block.scalar
            def _(act):
                act.wait_ge(mid_made, 1)
                act.activation(mid[:], ps[0][:, 0:B], ACT.Gelu, bias=b1[:]).then_inc(mid_ready, 1)
                act.wait_ge(lowered, 1)
                act.activation(route[:], route[:], ACT.Exp).then_inc(exp_ready, 1)

            @block.vector
            def _(dve):
                link = Link(dve, dve_step)
                link(dve.tensor_reduce(pooled[:], uT.rearrange("p (b t) -> p b t", t=T), AX.X, ALU.add))
                dve.tensor_scalar(pooled[:], pooled[:], 1.0 / T, None, ALU.mult).then_inc(pooled_ready, 1)
                dve.wait_ge(loaded, 96)
                dve.wait_ge(made, 1)
                flat_route = route[:].rearrange("p a k -> p (a k)")
                link(dve.tensor_tensor(flat_route, ps[1][0:B, 0:2 * K], b2[:], ALU.add))
                link(dve.tensor_reduce(top[:], flat_route, AX.X, ALU.max))
                dve.tensor_scalar(flat_route, flat_route, top[:], None, ALU.subtract).then_inc(lowered, 1)
                dve.wait_ge(exp_ready, 1)
                link(dve.tensor_reduce(top[:], flat_route, AX.X, ALU.add))
                link(dve.reciprocal(top[:], top[:]))
                link(dve.tensor_scalar(flat_route, flat_route, top[:], None, ALU.mult))
                first_hot(link, dve, hot[:], best[:], route[:], order[:], key[:], kb[:])
                link(dve.tensor_tensor(hot[:], hot[:], over_mid(index[:], 2), ALU.mult))
                link(dve.tensor_reduce(best[:], hot[:], AX.X, ALU.add))
                dve.tensor_copy(whole[:], best[:]).then_inc(chosen, 1)


def l3_ffn(nc, core, d):
    with ExitStack() as st:
        def sb(n, shape, dt=F32):
            return st.enter_context(nc.sbuf_tensor(f"l3f_{n}", shape, dt))

        u, x, xT, spatialT, temporalT = (sb("u", [P, B, D]), sb("x", [P, B, D]), sb("xT", [P, N]),
                                         sb("spatialT", [P, N]), sb("temporalT", [P, N]))
        choice = sb("choice", [1, 2 * B], I32)
        layer_norm(nc, "l3f_n", core.h[:], u[:], 1e-5)
        to_features(nc, "l3f_t", core, u[:], xT[:])
        route_sequences(nc, core, d, xT[:], choice[:], core.choice_scratch)
        layer_norm(nc, "l3f_n1", u[:], x[:], 1e-5, d["L3f_norm_s"])
        to_features(nc, "l3f_t1", core, x[:], xT[:])
        attention(nc, "l3s", core, xT[:], xT[:], spatialT[:], d["L3f_spatial_w"], d["L3f_spatial_b"],
                  choice=(choice[:], 0))
        layer_norm(nc, "l3f_n2", u[:], x[:], 1e-5, d["L3f_norm_t"])
        to_features(nc, "l3f_t2", core, x[:], xT[:])
        attention(nc, "l3t", core, xT[:], xT[:], temporalT[:], d["L3f_temporal_w"], d["L3f_temporal_b"],
                  choice=(choice[:], 1), causal=True, keep=True)
        attention(nc, "l3c", core, spatialT[:], temporalT[:], xT[:], d["L3f_cross_w"], d["L3f_cross_b"])
        add_features(nc, "l3f_r", core, xT[:], u[:])
        layer_norm(nc, "l3f_n3", u[:], x[:], 1e-5, d["L3f_norm_mlp"])
        to_features(nc, "l3f_t3", core, x[:], xT[:])
        mlp(nc, "l3f_m", core, xT[:], d["L3f_mw1"], d["L3f_mb1"], d["L3f_mw2"], d["L3f_mb2"], 512, ACT.Gelu, u[:])
        add_all(nc, "l3f_a", core.h[:], (u[:],))


def layout(i):
    i = {k: np.asarray(v) for k, v in i.items()}
    f = np.float32
    o = {}

    def put(name, a):
        o[name] = np.ascontiguousarray(a)

    x = i["x"]
    pad = np.concatenate([np.zeros((B, 2), x.dtype), x, np.zeros((B, 1), x.dtype)], 1)
    put("x_windows", np.stack([pad[:, k:k + T] for k in range(4)], 0).transpose(2, 0, 1))
    inside = np.zeros((P, 3), f)
    for n, c in ((0, 1), (1, 1), (2, 2)):
        inside[c:c + T - (n + 2) + 1, n] = 1
    put("inside", inside)
    put("tok_w", i["L0_tok_proj_w"].T.reshape(3, D, D).transpose(1, 0, 2))
    put("tok_b", i["L0_tok_proj_b"])
    for n in (2, 3, 4):
        put(f"L0_tok_emb_{n}", i[f"L0_tok_emb_{n}"])
    put("ident", np.eye(P, dtype=f))
    put("head_mask", np.repeat(np.eye(H, dtype=f), HD, 0))
    put("causal", np.where(np.arange(T)[:, None] >= np.arange(T)[None], 0, NEVER).astype(f))
    put("L0_attn_w", np.concatenate([i["L0_attn_W_qkv"].T, i["L0_attn_W_out"].T], 1))
    zero = np.zeros(D, f)
    put("L0_attn_b", np.stack([i["L0_attn_pos_bias_u"].reshape(D), zero, zero, i["L0_attn_b_out"]], 1))
    put("L0_bias_v", i["L0_attn_pos_bias_v"].reshape(D, 1))
    put("L0_ln1", np.stack([i["L0_attn_ln1_g"], i["L0_attn_ln1_b"]]))
    put("L0_ln2", np.stack([i["L0_attn_ln2_g"], i["L0_attn_ln2_b"]]))
    put("L0_pos_w", i["L0_attn_W_pos"].T)
    inv = (1.0 / 10000.0 ** (np.arange(0, D, 2, dtype=f) / D)).astype(f)
    put("freq", np.broadcast_to(np.concatenate([inv, inv]), (P, D)))
    put("phase", np.broadcast_to(np.repeat(np.array([0, np.pi / 2], f), D // 2), (P, D)))
    put("L0_gates_w", np.concatenate([i["L0_ffn_Wgate"], i["L0_ffn_Wb"], i["L0_ffn_Wa"]], 1))
    put("L0_dt_bias", i["L0_ffn_dt_bias"])
    put("L0_A_log", i["L0_ffn_A_log"])
    put("L0_qkv_w", np.stack([i["L0_ffn_Wq"], i["L0_ffn_Wk"], i["L0_ffn_Wv"]], 1))
    put("L0_gate_w", i["L0_ffn_Wg"])
    put("L0_out_w", i["L0_ffn_Wo"].reshape(4, D, D).transpose(1, 0, 2))
    put("L0_o_norm", i["L0_ffn_o_norm_weight"])
    s_, t_ = np.arange(T)[:, None], np.arange(T)[None]
    put("strict_upper", (s_ < t_).astype(f))
    put("level_masks", np.stack([((s_ >> (l + 1)) == (t_ >> (l + 1))) & ((s_ >> l) != (t_ >> l)) & (s_ < t_)
                                 for l in range(7)], 1).astype(f))

    def gate_order(a, n):
        return np.concatenate([a[..., 0:2 * n], a[..., 3 * n:4 * n], a[..., 2 * n:3 * n]], -1)

    put("L1_W0", gate_order(i["L1_attn_W0"], H1))
    put("L1_U0", gate_order(i["L1_attn_U0"], H1).reshape(K1, P, 4 * H1).transpose(1, 0, 2))
    put("L1_b0", gate_order(i["L1_attn_b0"], H1).reshape(C1, P).T)
    put("L1_W1", gate_order(i["L1_attn_W1"], H2).reshape(K1, P, 4 * H2).transpose(1, 0, 2))
    put("L1_U1", gate_order(i["L1_attn_U1"], H2))
    put("L1_b1", gate_order(i["L1_attn_b1"], H2).reshape(C2, P).T)

    def columns(a):
        return a.reshape(-1, P).T

    def chunks(a):
        return a.reshape(-1, P, a.shape[1]).transpose(1, 0, 2)

    put("L1f_ln1", np.stack([i["L1_ffn_ln1_g"], i["L1_ffn_ln1_b"]]))
    put("L1f_ffln", np.stack([i["L1_ffn_ffln_g"], i["L1_ffn_ffln_b"]]))
    put("L1f_Wr", i["L1_ffn_Wr"])
    put("L1f_codebook", i["L1_ffn_codebook"].T)
    put("order64", np.arange(E1, 0, -1).astype(f))
    put("L1f_W1", i["L1_ffn_W1"])
    put("L1f_W2", i["L1_ffn_W2"])
    put("L1f_b1", i["L1_ffn_b1"].reshape(E1 * F1, P).T)
    put("L1f_b2", i["L1_ffn_b2"])
    put("L1f_Ws1", i["L1_ffn_Ws1"])
    put("L1f_bs1", columns(i["L1_ffn_bs1"]))
    put("L1f_Ws2", chunks(i["L1_ffn_Ws2"]))
    put("L1f_bs2", i["L1_ffn_bs2"])
    put("L1f_Wf1", i["L1_ffn_Wf1"])
    put("L1f_bf1", columns(i["L1_ffn_bf1"]))
    put("L1f_Wf2", chunks(i["L1_ffn_Wf2"]))
    put("L1f_bf2", i["L1_ffn_bf2"])
    six = ("qf", "kf", "vf", "qt", "kt", "vt")
    put("L2a_w", np.concatenate([i[f"L2_attn_W_{n}"].T for n in six], 1))
    put("L2a_b", np.concatenate([i[f"L2_attn_b_{n}"] for n in six]))
    put("L2f_Wr", i["L2_ffn_Wr"])
    put("L2f_br", i["L2_ffn_br"])
    put("order8", np.arange(E2, 0, -1).astype(f))
    put("index8", np.arange(E2).astype(f))
    last = np.zeros((P, B), f)
    last[T - 1, B - 1] = 1
    put("last_token", last)
    for n in (1, 2, 3):
        put(f"L2f_W{n}", i[f"L2_ffn_W{n}"])
    put("L3a_in", i["L3_attn_in_proj_w"].T)
    put("L3a_x", chunks(i["L3_attn_x_proj_w"].T))
    put("L3a_dt", i["L3_attn_dt_proj_w"].T)
    put("L3a_conv_w", chunks(i["L3_attn_conv_w"]))
    put("L3a_conv_b", columns(i["L3_attn_conv_b"]))
    put("L3a_dt_b", columns(i["L3_attn_dt_proj_b"]))
    put("L3a_A_log", chunks(i["L3_attn_A_log"]).transpose(0, 2, 1).reshape(P, DS * CI))
    put("L3a_D", columns(i["L3_attn_D"]))
    put("L3a_out", chunks(i["L3_attn_out_proj_w"].T))
    put("L3a_ln", np.stack([i["L3_attn_ln_gamma"], i["L3_attn_ln_beta"]]))
    put("L3f_rw1", i["L3_ffn_router_w1"].T)
    put("L3f_rb1", i["L3_ffn_router_b1"].reshape(P, 1))
    put("L3f_rw2", i["L3_ffn_router_w2"].T)
    put("L3f_rb2", i["L3_ffn_router_b2"])
    put("order4", np.arange(4, 0, -1).astype(f))
    put("index4", np.arange(4).astype(f))
    for n in ("s", "t", "mlp"):
        put(f"L3f_norm_{n}", np.stack([i[f"L3_ffn_norm_{n}_w"], i[f"L3_ffn_norm_{n}_b"]]))
    put("L3f_spatial_w", np.concatenate([i["L3_ffn_sp_in_w"], i["L3_ffn_sp_out_w"]], 1).transpose(0, 2, 1))
    put("L3f_spatial_b", np.concatenate([i["L3_ffn_sp_in_b"], i["L3_ffn_sp_out_b"]], 1).reshape(4, 4, P)
        .transpose(0, 2, 1))
    put("L3f_temporal_w", np.concatenate([i[f"L3_ffn_t{n}_w"] for n in "qkvp"], 1).transpose(0, 2, 1))
    put("L3f_temporal_b", np.stack([i[f"L3_ffn_t{n}_b"] for n in "qkvp"], 2))
    put("L3f_cross_w", np.concatenate([i["L3_ffn_cross_in_w"], i["L3_ffn_cross_out_w"]], 0).T)
    put("L3f_cross_b", columns(np.concatenate([i["L3_ffn_cross_in_b"], i["L3_ffn_cross_out_b"]])))
    put("L3f_mw1", i["L3_ffn_mlp_w1"].T)
    put("L3f_mb1", columns(i["L3_ffn_mlp_b1"]))
    put("L3f_mw2", chunks(i["L3_ffn_mlp_w2"].T))
    put("L3f_mb2", i["L3_ffn_mlp_b2"])
    return o

STAGES = (tokens, l0_attention, l0_ffn, l1_attention, l1_ffn, l2_attention, l2_ffn, l3_attention, l3_ffn)


def build(nc, d, out):
    with ExitStack() as st:
        core = Core()
        core.d = d
        core.h = st.enter_context(nc.sbuf_tensor("resid", [P, B, D], F32))
        core.ident = st.enter_context(nc.sbuf_tensor("ident_sb", [P, P], F32))
        core.rel_scratch = nc.dram_tensor("rel_scratch", [B, H, T * (T + 1)], F32, kind="Internal").ap()
        core.decay_scratch = nc.dram_tensor("decay_scratch", [BH * E0, T], F32, kind="Internal").ap()
        core.mask_scratch = nc.dram_tensor("mask_scratch", [T, B], F32, kind="Internal").ap()
        core.bc_scratch = nc.dram_tensor("bc_scratch", [2 * DS, N], F32, kind="Internal").ap()
        core.choice_scratch = nc.dram_tensor("choice_scratch", [B, 2], I32, kind="Internal").ap()
        for stage in STAGES:
            stage(nc, core, d)
        with Stage(nc, "store") as s:
            stored = s.sem("stored")
            with nc.Block() as block:
                @block.sync
                def _(sp):
                    sp.dma_start(out.rearrange("b t d -> t b d"), core.h[:]).then_inc(stored, 16)
                    sp.wait_ge(stored, 16)


def kernel(**inputs):
    import concourse.bacc as bacc
    from concourse.bass_utils import run_bass_kernel_spmd

    nc = bacc.Bacc("TRN2", target_bir_lowering=False, num_devices=1)
    arrays = layout(inputs)
    d = {k: nc.dram_tensor(k, a.shape, mybir.dt.from_np(a.dtype), kind="ExternalInput").ap() for k, a in arrays.items()}
    out = nc.dram_tensor("out", (B, T, D), F32, kind="ExternalOutput").ap()
    build(nc, d, out)
    r = run_bass_kernel_spmd(nc, [arrays], core_ids=[0])
    return r.results[0]["out"]
```

```python
from contextlib import ExitStack

import numpy as np

import concourse.bass as bass
from concourse import mybir

F32 = mybir.dt.float32
BF16 = mybir.dt.bfloat16
I32 = mybir.dt.int32
U32 = mybir.dt.uint32
ACT = mybir.ActivationFunctionType
ALU = mybir.AluOpType
AX = mybir.AxisListType

P = 128
B = 16
T = 128
D = 128
N = B * T
BANK = 512
NEVER = -1e30


class Stage:

    def __init__(self, nc, name):
        self.nc, self.name, self.stack, self.sems = nc, name, ExitStack(), []

    def __enter__(self):
        return self

    def sb(self, name, shape, dt=F32):
        return self.stack.enter_context(self.nc.sbuf_tensor(f"s_{self.name}_{name}", shape, dt))

    def ps(self, name, shape, dt=F32):
        return self.stack.enter_context(self.nc.psum_tensor(f"p_{self.name}_{name}", shape, dt))

    def sem(self, name):
        s = self.nc.alloc_semaphore(f"{self.name}_{name}")
        self.sems.append(s)
        return s

    def pair(self, name):
        return [self.sem(f"{name}{p}") for p in range(2)]

    def start_at_one(self, *sems):
        for sem in sems:
            self.nc.sync.sem_inc(sem, 1)

    def __exit__(self, kind, e, trace):
        if kind is None:
            self.stack.close()
            self.nc.clear_and_free_semaphores(self.sems)
            self.nc.all_engine_barrier()
        return False


class Link:

    def __init__(self, eng, sem, base=0):
        self.eng, self.sem, self.base, self.n = eng, sem, base, 0

    def __call__(self, ins):
        self.n += 1
        ins.then_inc(self.sem, 1)
        self.eng.wait_ge(self.sem, self.base + self.n)


def log1p(link, dve, x, ratio, square):
    link(dve.tensor_scalar(ratio, x, 2.0, None, ALU.add))
    link(dve.reciprocal(ratio, ratio))
    link(dve.tensor_tensor(ratio, x, ratio, ALU.mult))
    link(dve.tensor_tensor(square, ratio, ratio, ALU.mult))
    link(dve.tensor_scalar(x, square, 1.0 / 15, None, ALU.mult))
    for k in (13, 11, 9, 7, 5, 3):
        link(dve.scalar_tensor_tensor(x, x, 1.0 / k, square, ALU.add, ALU.mult))
    link(dve.scalar_tensor_tensor(x, x, 1.0, ratio, ALU.add, ALU.mult))
    link(dve.tensor_scalar(x, x, 2.0, None, ALU.mult))


def flat(x3):
    return x3.rearrange("p b d -> p (b d)")


def over_last(col, n):
    return col.unsqueeze(2).to_broadcast([col.shape[0], col.shape[1], n])


def over_mid(row, n):
    return row.unsqueeze(1).to_broadcast([row.shape[0], n, row.shape[1]])


def layer_norm(nc, name, src, dst, eps, rows=None):
    with Stage(nc, name) as s:
        total, mean, var, dev, inv = (s.sb(n, [P, B]) for n in ("total", "mean", "var", "dev", "inv"))
        square = s.sb("square", [P, B, D])
        affine = s.sb("affine", [P, 2, D])
        epscol = s.sb("epscol", [P, 1])
        centred, var_ready, dev_ready, dve_step, squared, rows_in = (
            s.sem(n) for n in ("centred", "var_ready", "dev_ready", "dve_step", "squared", "rows_in"))
        with nc.Block() as block:
            if rows is not None:
                @block.sync
                def _(sp):
                    sp.dma_start(affine[:], rows.partition_broadcast(P)).then_inc(rows_in, 16)

            @block.vector
            def _(dve):
                link = Link(dve, dve_step)
                link(dve.memset(epscol[:], eps))
                link(dve.tensor_reduce(total[:], src, AX.X, ALU.add))
                link(dve.tensor_scalar(mean[:], total[:], 1.0 / D, None, ALU.mult))
                dve.tensor_tensor(dst, src, over_last(mean[:], D), ALU.subtract).then_inc(centred, 1)
                dve.wait_ge(squared, 1)
                link(dve.tensor_reduce(total[:], square[:], AX.X, ALU.add))
                dve.tensor_scalar(var[:], total[:], 1.0 / D, None, ALU.mult).then_inc(var_ready, 1)
                dve.wait_ge(dev_ready, 1)
                link(dve.reciprocal(inv[:], dev[:]))
                link(dve.tensor_tensor(dst, dst, over_last(inv[:], D), ALU.mult))
                if rows is not None:
                    dve.wait_ge(rows_in, 16)
                    link(dve.tensor_tensor(dst, dst, over_mid(affine[:, 0, :], B), ALU.mult))
                    link(dve.tensor_tensor(dst, dst, over_mid(affine[:, 1, :], B), ALU.add))

            @block.scalar
            def _(act):
                act.wait_ge(centred, 1)
                act.activation(square[:], dst, ACT.Square).then_inc(squared, 1)
                act.wait_ge(var_ready, 1)
                act.activation(dev[:], var[:], ACT.Sqrt, bias=epscol[:]).then_inc(dev_ready, 1)


def to_features(nc, name, core, src, dst):
    with Stage(nc, name) as s:
        banks = [s.ps(f"turned{i}", [P, BANK]) for i in range(4)]
        turned, copied = s.sem("turned"), s.sem("copied")
        with nc.Block() as block:
            @block.tensor
            def _(pe):
                for g in range(4):
                    for k in range(4):
                        mm = pe.transpose(banks[g][:, k * P:(k + 1) * P], src[:, 4 * g + k, :], core.ident[:])
                    mm.then_inc(turned, 1)

            @block.vector
            def _(dve):
                for g in (0, 2):
                    dve.wait_ge(turned, g + 1)
                    dve.tensor_copy(dst[:, g * BANK:(g + 1) * BANK], banks[g][:]).then_inc(copied, 1)
                dve.wait_ge(copied, 4)

            @block.scalar
            def _(act):
                for g in (1, 3):
                    act.wait_ge(turned, g + 1)
                    act.activation(dst[:, g * BANK:(g + 1) * BANK], banks[g][:], ACT.Copy).then_inc(copied, 1)


def add_features(nc, name, core, srcT, dst):
    with Stage(nc, name) as s:
        banks = [s.ps(f"turned{i}", [P, BANK]) for i in range(4)]
        turned, added = s.sem("turned"), s.sem("added")
        with nc.Block() as block:
            @block.tensor
            def _(pe):
                for g in range(4):
                    for k in range(4):
                        b = 4 * g + k
                        mm = pe.transpose(banks[g][:, k * P:(k + 1) * P], srcT[:, b * T:(b + 1) * T], core.ident[:])
                    mm.then_inc(turned, 1)

            @block.vector
            def _(dve):
                for g in range(4):
                    dve.wait_ge(turned, g + 1)
                    part = flat(dst)[:, g * BANK:(g + 1) * BANK]
                    dve.tensor_tensor(part, part, banks[g][:], ALU.add).then_inc(added, 1)
                dve.wait_ge(added, 4)


class Core:
    pass


def tokens(nc, core, d):
    VOCAB, SHIFT = 25000, 64.0
    with Stage(nc, "tok") as s:
        raw = s.sb("raw", [P, 4, B], I32)
        byte = s.sb("byte", [P, 4, B])
        hashed = s.sb("hashed", [P, B])
        quotient = s.sb("quotient", [P, B])
        whole = s.sb("whole", [P, B], I32)
        over = s.sb("over", [P, B])
        ids = s.sb("ids", [P, 3, B], U32)
        inside = s.sb("inside", [P, 3])
        emb = s.sb("emb", [P, B, 3, D])
        stage = [s.sb(f"stage{p}", [P, 3, D]) for p in range(2)]
        embT = [s.sb(f"embT{p}", [P, 3, T]) for p in range(2)]
        w = s.sb("w", [P, 3, D])
        brow = s.sb("brow", [P, D])
        turn = [s.ps(f"turn{p}", [P, BANK]) for p in range(2)]
        proj = [s.ps(f"proj{p}", [P, BANK]) for p in range(2)]
        loaded, dve_step, ids_ready = s.sem("loaded"), s.sem("dve_step"), s.sem("ids_ready")
        gathered = [s.sem(f"gathered{b}") for b in range(B)]
        masked, turned, copied, projected, added = (s.pair(n) for n in (
            "masked", "turned", "copied", "projected", "added"))
        s.start_at_one(*turned, *copied, *added)
        with nc.Block() as block:
            @block.sync
            def _(sp):
                sp.dma_start(raw[:], d["x_windows"]).then_inc(loaded, 16)
                sp.dma_start(inside[:], d["inside"]).then_inc(loaded, 16)
                sp.dma_start(w[:], d["tok_w"]).then_inc(loaded, 16)
                sp.dma_start(brow[:], d["tok_b"].partition_broadcast(P)).then_inc(loaded, 16)
                sp.dma_start(core.ident[:], d["ident"]).then_inc(loaded, 16)

            @block.gpsimd
            def _(pool):
                pool.wait_ge(ids_ready, 3)
                for b in range(B):
                    for n in range(3):
                        pool.indirect_dma_start(emb[:, b, n, :], None, d[f"L0_tok_emb_{n + 2}"],
                                                bass.IndirectOffsetOnAxis(ap=ids[:, n, b:b + 1], axis=0))\
                            .then_inc(gathered[b], 16)

            @block.vector
            def _(dve):
                link = Link(dve, dve_step)
                dve.wait_ge(loaded, 80)
                link(dve.tensor_copy(byte[:], raw[:]))
                for n in range(3):
                    first = (1, 1, 0)[n]
                    link(dve.tensor_copy(hashed[:], byte[:, first, :]))
                    for k in range(1, n + 2):
                        link(dve.scalar_tensor_tensor(hashed[:], hashed[:], SHIFT, byte[:, first + k, :],
                                                      ALU.mult, ALU.add))
                        link(dve.tensor_scalar(quotient[:], hashed[:], 1.0 / VOCAB, None, ALU.mult))
                        link(dve.tensor_copy(whole[:], quotient[:]))
                        link(dve.tensor_copy(quotient[:], whole[:]))
                        link(dve.scalar_tensor_tensor(hashed[:], quotient[:], -float(VOCAB), hashed[:],
                                                      ALU.mult, ALU.add))
                        link(dve.tensor_scalar(over[:], hashed[:], 0.0, float(VOCAB), ALU.is_lt, ALU.mult))
                        link(dve.tensor_tensor(hashed[:], hashed[:], over[:], ALU.add))
                        link(dve.tensor_scalar(over[:], hashed[:], float(VOCAB), -float(VOCAB), ALU.is_ge, ALU.mult))
                        link(dve.tensor_tensor(hashed[:], hashed[:], over[:], ALU.add))
                    dve.tensor_copy(ids[:, n, :], hashed[:]).then_inc(ids_ready, 1)
                    dve.wait_ge(ids_ready, n + 1)
                with dve.Fori(0, B // 2) as j:
                    for p in range(2):
                        dve.wait_ge(turned[p], j + 2)
                        dve.tensor_copy(embT[p][:].rearrange("p a b -> p (a b)"), turn[p][:, 0:3 * T])\
                            .then_inc(copied[p], 1)
                    for p in range(2):
                        dve.wait_ge(projected[p], j + 1)
                        dve.tensor_tensor(flat(core.h[:])[:, bass.ds((2 * j + p) * D, D)], proj[p][:, 0:D], brow[:],
                                          ALU.add).then_inc(added[p], 1)
                for p in range(2):
                    dve.wait_ge(added[p], B // 2 + 1)

            @block.scalar
            def _(act):
                act.wait_ge(loaded, 80)
                for b in range(B):
                    act.wait_ge(gathered[b], 48)
                with act.Fori(0, B // 2) as j:
                    for p in range(2):
                        act.wait_ge(turned[p], j + 1)
                        for n in range(3):
                            ins = act.activation(
                                stage[p][:, n, :],
                                emb[:].rearrange("p b n d -> p (b n d)")[:, bass.ds((2 * j + p) * 3 * D + n * D, D)],
                                ACT.Copy, scale=inside[:, n:n + 1])
                        ins.then_inc(masked[p], 1)

            @block.tensor
            def _(pe):
                with pe.Fori(0, B // 2) as j:
                    for p in range(2):
                        pe.wait_ge(masked[p], j + 1)
                        pe.wait_ge(copied[p], j + 1)
                        for n in range(3):
                            mm = pe.transpose(turn[p][:, n * T:(n + 1) * T], stage[p][:, n, :], core.ident[:])
                        mm.then_inc(turned[p], 1)
                    for p in range(2):
                        pe.wait_ge(copied[p], j + 2)
                        pe.wait_ge(added[p], j + 1)
                        for n in range(3):
                            mm = pe.matmul(proj[p][:, 0:D], embT[p][:, n, :], w[:, n, :], start=(n == 0), stop=(n == 2))
                        mm.then_inc(projected[p], 1)


H, HD = 8, 16
HT = H * T


def attention(nc, name, core, xq, xkv, out, w_dram, b_dram, choice=None, causal=False, keep=False, shifted=None):
    routed = choice is not None
    with Stage(nc, name) as s:
        mask = s.sb("mask", [P, H])
        tri = s.sb("tri", [P, T])

        def two(n, shape, dt=F32):
            return [s.sb(f"{n}{p}", shape, dt) for p in range(2)]

        w, bias = two("w", [P, 4 * D]), two("bias", [P, 4])
        xq_s, xkv_s, qT, kT = (two(n, [P, T]) for n in ("xq_s", "xkv_s", "qT", "kT"))
        v = two("v", [P, H, HD + 1])
        HW, AT_O, AT_Y = H * (HD + 1), 2 * T, 3 * T
        keys, score, probs, probsT = (two(n, [P, H, T]) for n in ("keys", "score", "probs", "probsT"))
        top, inv = (two(n, [P, H]) for n in ("top", "inv"))
        o, oT, pos = two("o", [P, D]), two("oT", [P, T]), two("pos", [P, H, T])
        small = [s.ps(f"small{p}", [P, BANK]) for p in range(2)]
        qkv = [s.ps(f"qkv{p}", [P, BANK]) for p in range(2)]
        wide = [s.ps(f"wide{p}", [P, HT]) for p in range(2)]
        const_in, ones_ready = s.sem("const_in"), s.sem("ones_ready")
        (x_in, w_in, projected, qk_ready, v_ready, keys_ready, scored, pos_in, lowered, exp_ready,
         turned, turned_a, turned_b, attended, o_ready, o_turned, oT_ready, y_ready, batch_done, dve_step) = (
            s.pair(n) for n in (
                "x_in", "w_in", "projected", "qk_ready", "v_ready", "keys_ready", "scored", "pos_in", "lowered",
                "exp_ready", "turned", "turned_a", "turned_b", "attended", "o_ready", "o_turned",
                "oT_ready", "y_ready", "batch_done", "dve_step"))
        s.start_at_one(*batch_done)
        with nc.Block() as block:
            @block.sync
            def _(sp):
                sp.dma_start(mask[:], core.d["head_mask"]).then_inc(const_in, 16)
                sp.dma_start(tri[:], core.d["causal"]).then_inc(const_in, 16)
                if not routed:
                    for p in range(2):
                        sp.dma_start(w[p][:], w_dram).then_inc(w_in[p], 16)
                        sp.dma_start(bias[p][:], b_dram).then_inc(w_in[p], 16)
                if routed or shifted is not None:
                    with sp.Fori(0, B // 2) as j:
                        for p in range(2):
                            sp.wait_ge(batch_done[p], j + 1)
                            if routed:
                                e = sp.value_load(choice[0][0:1, bass.ds((2 * j + p) * 2 + choice[1], 1)], min_val=0, max_val=3)
                                sp.dma_start(w[p][:], w_dram[bass.ds(e, 1), :, :].rearrange("e p n -> p (e n)"))\
                                    .then_inc(w_in[p], 16)
                                sp.dma_start(bias[p][:], b_dram[bass.ds(e, 1), :, :].rearrange("e p n -> p (e n)"))\
                                    .then_inc(w_in[p], 16)
                            if shifted is not None:
                                sp.dma_start(pos[p][:], shifted[bass.ds(2 * j + p, 1), :, T:T + T * T].rearrange(
                                    "b h (q k) -> q (b h) k", k=T)).then_inc(pos_in[p], 16)

            @block.scalar
            def _(act):
                with act.Fori(0, B // 2) as j:
                    for p in range(2):
                        act.wait_ge(batch_done[p], j + 1)
                        act.activation(xq_s[p][:], xq[:, bass.ds((2 * j + p) * T, T)], ACT.Copy).then_inc(x_in[p], 1)
                        act.activation(xkv_s[p][:], xkv[:, bass.ds((2 * j + p) * T, T)], ACT.Copy).then_inc(x_in[p], 1)
                    for p in range(2):
                        act.wait_ge(projected[p], j + 1)
                        act.activation(qT[p][:], qkv[p][:, 0:T], ACT.Identity, bias=bias[p][:, 0:1]).then_inc(qk_ready[p], 1)
                        act.activation(kT[p][:], qkv[p][:, T:2 * T], ACT.Identity, bias=bias[p][:, 1:2])\
                            .then_inc(qk_ready[p], 1)
                        act.activation(v[p][:, :, 0:HD], qkv[p][:, 2 * T:3 * T].rearrange("p (h e) -> p h e", h=H),
                                       ACT.Copy).then_inc(v_ready[p], 1)
                    for p in range(2):
                        act.wait_ge(lowered[p], j + 1)
                        act.activation(probs[p][:], score[p][:], ACT.Exp, scale=HD ** -0.5).then_inc(exp_ready[p], 1)
                    for p in range(2):
                        act.wait_ge(turned[p], j + 1)
                        act.activation(probsT[p][:, 0:H // 2, :].rearrange("p h t -> p (h t)"), wide[p][:, 0:BANK],
                                       ACT.Copy).then_inc(turned_a[p], 1)
                    for p in range(2):
                        act.wait_ge(o_turned[p], j + 1)
                        act.activation(oT[p][:], small[p][:, AT_O:AT_O + T], ACT.Identity, bias=bias[p][:, 2:3])\
                            .then_inc(oT_ready[p], 1)

            @block.vector
            def _(dve):
                dve.wait_ge(const_in, 32)
                for p in range(2):
                    dve.memset(v[p][:, :, HD:], 1.0).then_inc(ones_ready, 1)
                per = 3 + (1 if (shifted is not None or causal) else 0)
                with dve.Fori(0, B // 2) as j:
                    links = [Link(dve, dve_step[p], j * per) for p in range(2)]
                    for p in range(2):
                        dve.wait_ge(qk_ready[p], 2 * j + 2)
                        dve.tensor_tensor(keys[p][:], over_mid(kT[p][:], H), over_last(mask[:], T), ALU.mult)\
                            .then_inc(keys_ready[p], 1)
                    for p in range(2):
                        dve.wait_ge(scored[p], j + 1)
                        w3 = wide[p][:].rearrange("p (h t) -> p h t", h=H)
                        if shifted is not None:
                            dve.wait_ge(pos_in[p], 16 * j + 16)
                            links[p](dve.tensor_tensor(score[p][:], w3, pos[p][:], ALU.add))
                            w3 = score[p][:]
                        if causal:
                            links[p](dve.tensor_tensor(score[p][:], w3, over_mid(tri[:], H), ALU.add))
                            w3 = score[p][:]
                        links[p](dve.tensor_reduce(top[p][:], w3, AX.X, ALU.max))
                        dve.tensor_tensor(score[p][:], w3, over_last(top[p][:], T), ALU.subtract).then_inc(lowered[p], 1)
                    for p in range(2):
                        dve.wait_ge(turned[p], j + 1)
                        dve.tensor_copy(probsT[p][:, H // 2:, :].rearrange("p h t -> p (h t)"), wide[p][:, BANK:HT])\
                            .then_inc(turned_b[p], 1)
                    for p in range(2):
                        dve.wait_ge(attended[p], j + 1)
                        sums = small[p][:, 0:HW].rearrange("p (h e) -> p h e", h=H)
                        links[p](dve.reciprocal(inv[p][:].unsqueeze(2), sums[:, :, HD:]))
                        links[p](dve.tensor_tensor(o[p][:].rearrange("p (h e) -> p h e", h=H), sums[:, :, 0:HD],
                                                   over_last(inv[p][:], HD), ALU.mult))
                        dve.sem_inc(o_ready[p], 1)
                    for p in range(2):
                        dve.wait_ge(y_ready[p], j + 1)
                        dst = out[:, bass.ds((2 * j + p) * T, T)]
                        if keep:
                            dve.scalar_tensor_tensor(dst, small[p][:, AT_Y:AT_Y + T], bias[p][:, 3:4], xq_s[p][:],
                                                     ALU.add, ALU.add).then_inc(batch_done[p], 1)
                        else:
                            dve.tensor_scalar(dst, small[p][:, AT_Y:AT_Y + T], bias[p][:, 3:4], None, ALU.add)\
                                .then_inc(batch_done[p], 1)
                for p in range(2):
                    dve.wait_ge(batch_done[p], B // 2 + 1)

            @block.tensor
            def _(pe):
                pe.wait_ge(ones_ready, 2)
                if not routed:
                    for p in range(2):
                        pe.wait_ge(w_in[p], 32)
                with pe.Fori(0, B // 2) as j:
                    for p in range(2):
                        pe.wait_ge(x_in[p], 2 * j + 2)
                        if routed:
                            pe.wait_ge(w_in[p], 32 * j + 32)
                        pe.matmul(qkv[p][:, 0:T], w[p][:, 0:D], xq_s[p][:], start=True, stop=True)
                        pe.matmul(qkv[p][:, T:2 * T], w[p][:, D:2 * D], xkv_s[p][:], start=True, stop=True)
                        pe.matmul(qkv[p][:, 2 * T:3 * T], xkv_s[p][:], w[p][:, 2 * D:3 * D], start=True, stop=True)\
                            .then_inc(projected[p], 1)
                    for p in range(2):
                        pe.wait_ge(keys_ready[p], j + 1)
                        k2 = keys[p][:].rearrange("p h t -> p (h t)")
                        for half in range(2):
                            mm = pe.matmul(wide[p][:, half * BANK:(half + 1) * BANK], qT[p][:],
                                           k2[:, half * BANK:(half + 1) * BANK], start=True, stop=True)
                        mm.then_inc(scored[p], 1)
                    for p in range(2):
                        pe.wait_ge(exp_ready[p], j + 1)
                        for h in range(H):
                            mm = pe.transpose(wide[p][:, h * T:(h + 1) * T], probs[p][:, h, :], core.ident[:])
                        mm.then_inc(turned[p], 1)
                    for p in range(2):
                        pe.wait_ge(turned_a[p], j + 1)
                        pe.wait_ge(turned_b[p], j + 1)
                        pe.wait_ge(v_ready[p], j + 1)
                        for h in range(H):
                            mm = pe.matmul(small[p][:, h * (HD + 1):(h + 1) * (HD + 1)], probsT[p][:, h, :],
                                           v[p][:, h, :], start=True, stop=True)
                        mm.then_inc(attended[p], 1)
                    for p in range(2):
                        pe.wait_ge(o_ready[p], j + 1)
                        pe.transpose(small[p][:, AT_O:AT_O + T], o[p][:], core.ident[:]).then_inc(o_turned[p], 1)
                    for p in range(2):
                        pe.wait_ge(oT_ready[p], j + 1)
                        pe.matmul(small[p][:, AT_Y:AT_Y + T], w[p][:, 3 * D:4 * D], oT[p][:], start=True, stop=True)\
                            .then_inc(y_ready[p], 1)


def position_scores(nc, core, u, xT, scratch):
    PI = float(np.pi)
    with Stage(nc, "pos") as s:
        freq, phase = s.sb("freq", [P, D]), s.sb("phase", [P, D])
        angle, turns, emb = s.sb("angle", [P, D]), s.sb("turns", [P, D]), s.sb("emb", [P, D])
        whole = s.sb("whole", [P, D], I32)
        embT, pT, wpos, wq, mask, bias = (s.sb("embT", [P, T]), s.sb("pT", [P, T]), s.sb("wpos", [P, D]),
                                          s.sb("wq", [P, D]), s.sb("mask", [P, H]), s.sb("bias", [P, 1]))
        places = s.sb("places", [P, H, T])
        xs = [s.sb(f"xs{p}", [P, T]) for p in range(2)]
        qT = [s.sb(f"qT{p}", [P, T]) for p in range(2)]
        padded = [s.sb(f"padded{p}", [P, H, T + 1]) for p in range(2)]
        small = [s.ps(f"small{p}", [P, BANK]) for p in range(2)]
        wide = [s.ps(f"wide{p}", [P, HT]) for p in range(2)]
        loaded, dve_step, angle_ready, sin_ready, embT_turned, p_ready, pT_ready, places_ready, embT_ready = (
            s.sem(n) for n in ("loaded", "dve_step", "angle_ready", "sin_ready", "embT_turned", "p_ready", "pT_ready",
                               "places_ready", "embT_ready"))
        x_in, q_made, q_ready, scored, copied, stored = (s.pair(n) for n in (
            "x_in", "q_made", "q_ready", "scored", "copied", "stored"))
        s.start_at_one(*stored, *copied, *scored, *q_made, *q_ready)
        with nc.Block() as block:
            @block.sync
            def _(sp):
                for dst, src in ((freq, "freq"), (phase, "phase"), (wpos, "L0_pos_w"), (mask, "head_mask"),
                                 (bias, "L0_bias_v")):
                    sp.dma_start(dst[:], core.d[src]).then_inc(loaded, 16)
                sp.dma_start(wq[:], core.d["L0_attn_w"][:, 0:D]).then_inc(loaded, 16)
                with sp.Fori(0, B // 2) as j:
                    for p in range(2):
                        sp.wait_ge(copied[p], 2 * j + 3)
                        sp.dma_start(scratch[bass.ds(2 * j + p, 1), :, :].rearrange("b h (q k) -> q (b h) k", k=T + 1),
                                     padded[p][:]).then_inc(stored[p], 16)
                for p in range(2):
                    sp.wait_ge(stored[p], 16 * (B // 2) + 1)

            @block.vector
            def _(dve):
                link = Link(dve, dve_step)
                for p in range(2):
                    link(dve.memset(padded[p][:, :, 0:1], 0.0))
                dve.wait_ge(loaded, 96)
                link(dve.scalar_tensor_tensor(angle[:], freq[:], u[:, 0, 0:1], phase[:], ALU.mult, ALU.add))
                link(dve.tensor_scalar(turns[:], angle[:], 1.0 / (2 * PI), None, ALU.mult))
                link(dve.tensor_copy(whole[:], turns[:]))
                link(dve.tensor_copy(turns[:], whole[:]))
                link(dve.scalar_tensor_tensor(angle[:], turns[:], -6.28125, angle[:], ALU.mult, ALU.add))
                link(dve.scalar_tensor_tensor(angle[:], turns[:], -(2 * PI - 6.28125), angle[:], ALU.mult, ALU.add))
                link(dve.tensor_scalar(turns[:], angle[:], PI, -2 * PI, ALU.is_gt, ALU.mult))
                link(dve.tensor_tensor(angle[:], angle[:], turns[:], ALU.add))
                link(dve.tensor_scalar(turns[:], angle[:], -PI, 2 * PI, ALU.is_lt, ALU.mult))
                link(dve.tensor_tensor(angle[:], angle[:], turns[:], ALU.add))
                dve.tensor_scalar(angle[:], angle[:], 3.1415925, -3.1415925, ALU.min, ALU.max).then_inc(angle_ready, 1)
                dve.wait_ge(embT_turned, 1)
                dve.tensor_copy(embT[:], small[0][:, 0:T]).then_inc(embT_ready, 1)
                dve.wait_ge(p_ready, 1)
                dve.tensor_copy(pT[:], small[1][:, 0:T]).then_inc(pT_ready, 1)
                dve.wait_ge(pT_ready, 1)
                dve.tensor_tensor(places[:], over_mid(pT[:], H), over_last(mask[:], T), ALU.mult)\
                    .then_inc(places_ready, 1)
                with dve.Fori(0, B // 2) as j:
                    for p in range(2):
                        dve.wait_ge(scored[p], j + 2)
                        dve.wait_ge(stored[p], 16 * j + 1)
                        dve.tensor_copy(padded[p][:, 0:4, 1:T + 1],
                                        wide[p][:, 0:BANK].rearrange("p (h t) -> p h t", t=T)).then_inc(copied[p], 1)

            @block.scalar
            def _(act):
                act.wait_ge(angle_ready, 1)
                act.activation(emb[:], angle[:], ACT.Sin).then_inc(sin_ready, 1)
                act.wait_ge(loaded, 96)
                with act.Fori(0, B // 2) as j:
                    for p in range(2):
                        act.wait_ge(q_made[p], j + 1)
                        act.activation(xs[p][:], xT[:, bass.ds((2 * j + p) * T, T)], ACT.Copy).then_inc(x_in[p], 1)
                    for p in range(2):
                        act.wait_ge(q_made[p], j + 2)
                        act.wait_ge(scored[p], j + 1)
                        act.activation(qT[p][:], small[p][:, 0:T], ACT.Identity, bias=bias[:]).then_inc(q_ready[p], 1)
                    for p in range(2):
                        act.wait_ge(scored[p], j + 2)
                        act.wait_ge(stored[p], 16 * j + 1)
                        act.activation(padded[p][:, 4:8, 1:T + 1],
                                       wide[p][:, BANK:HT].rearrange("p (h t) -> p h t", t=T), ACT.Copy)\
                            .then_inc(copied[p], 1)

            @block.tensor
            def _(pe):
                pe.wait_ge(sin_ready, 1)
                pe.transpose(small[0][:, 0:T], emb[:], core.ident[:]).then_inc(embT_turned, 1)
                pe.wait_ge(embT_ready, 1)
                pe.matmul(small[1][:, 0:T], wpos[:], embT[:], start=True, stop=True).then_inc(p_ready, 1)
                pe.wait_ge(places_ready, 1)
                flat_places = places[:].rearrange("p h t -> p (h t)")
                with pe.Fori(0, B // 2) as j:
                    for p in range(2):
                        pe.wait_ge(x_in[p], j + 1)
                        pe.wait_ge(q_ready[p], j + 1)
                        pe.matmul(small[p][:, 0:T], wq[:], xs[p][:], start=True, stop=True).then_inc(q_made[p], 1)
                    for p in range(2):
                        pe.wait_ge(q_ready[p], j + 2)
                        pe.wait_ge(copied[p], 2 * j + 1)
                        for half in range(2):
                            mm = pe.matmul(wide[p][:, half * BANK:(half + 1) * BANK], qT[p][:],
                                           flat_places[:, half * BANK:(half + 1) * BANK], start=True, stop=True)
                        mm.then_inc(scored[p], 1)


def l0_attention(nc, core, d):
    with ExitStack() as st:
        u = st.enter_context(nc.sbuf_tensor("l0a_u", [P, B, D], F32))
        xn = st.enter_context(nc.sbuf_tensor("l0a_xn", [P, B, D], F32))
        xT = st.enter_context(nc.sbuf_tensor("l0a_xT", [P, N], F32))
        yT = st.enter_context(nc.sbuf_tensor("l0a_yT", [P, N], F32))
        layer_norm(nc, "l0a_n0", core.h[:], u[:], 1e-5)
        layer_norm(nc, "l0a_n1", u[:], xn[:], 1e-5, d["L0_ln1"])
        layer_norm(nc, "l0a_n2", xn[:], xn[:], 1e-5, d["L0_ln2"])
        to_features(nc, "l0a_t", core, xn[:], xT[:])
        position_scores(nc, core, u[:], xT[:], core.rel_scratch)
        attention(nc, "l0a", core, xT[:], xT[:], yT[:], d["L0_attn_w"], d["L0_attn_b"], shifted=core.rel_scratch)
        add_features(nc, "l0a_r", core, yT[:], core.h[:])


E0, HV = 4, 64
BH = B * H


def delta_gates(nc, core, d, uT, weight, chosen, scal):
    G = E0 + 2 * H
    with Stage(nc, "dg") as s:
        w = s.sb("w", [P, G])
        dtb, alog, rate = s.sb("dtb", [P, H]), s.sb("alog", [P, H]), s.sb("rate", [P, H])
        logit = s.sb("logit", [P, B, G])
        prob, gt = s.sb("prob", [P, B, E0]), s.sb("gt", [P, B, E0])
        col = s.sb("col", [P, B])
        z, soft, mag, bt, square = (s.sb(n, [P, B, H]) for n in ("z", "soft", "mag", "bt", "square"))
        ps = s.ps("ps", [P, BANK])
        loaded, logits_ready, dve_step, to_act, from_act = (
            s.sem(n) for n in ("loaded", "logits_ready", "dve_step", "to_act", "from_act"))
        with nc.Block() as block:
            @block.sync
            def _(sp):
                sp.dma_start(w[:], d["L0_gates_w"]).then_inc(loaded, 16)
                sp.dma_start(dtb[:], d["L0_dt_bias"].partition_broadcast(P)).then_inc(loaded, 16)
                sp.dma_start(alog[:], d["L0_A_log"].partition_broadcast(P)).then_inc(loaded, 16)

            @block.tensor
            def _(pe):
                pe.wait_ge(loaded, 48)
                for b in range(B):
                    mm = pe.matmul(ps[:, b * G:(b + 1) * G], uT[:, b * T:(b + 1) * T], w[:], start=True, stop=True)
                mm.then_inc(logits_ready, 1)

            @block.scalar
            def _(act):
                act.wait_ge(loaded, 48)
                act.activation(rate[:], alog[:], ACT.Exp).then_inc(from_act, 1)
                act.wait_ge(to_act, 1)
                act.activation(prob[:], prob[:], ACT.Exp).then_inc(from_act, 1)
                act.wait_ge(to_act, 2)
                act.activation(bt[:], logit[:, :, E0:E0 + H], ACT.Exp, scale=-1.0).then_inc(from_act, 1)
                act.wait_ge(to_act, 3)
                act.activation(mag[:], mag[:], ACT.Exp, scale=-1.0).then_inc(from_act, 1)
                act.wait_ge(to_act, 4)
                act.activation(scal[:, :, H:], scal[:, :, H:], ACT.Exp).then_inc(from_act, 1)

            @block.vector
            def _(dve):
                link = Link(dve, dve_step)
                dve.wait_ge(logits_ready, 1)
                link(dve.tensor_copy(logit[:].rearrange("p b g -> p (b g)"), ps[:, 0:B * G]))
                gate = logit[:, :, 0:E0]
                link(dve.tensor_reduce(col[:], gate, AX.X, ALU.max))
                dve.tensor_tensor(prob[:], gate, over_last(col[:], E0), ALU.subtract).then_inc(to_act, 1)
                dve.wait_ge(from_act, 2)
                link(dve.tensor_reduce(col[:], prob[:], AX.X, ALU.add))
                link(dve.reciprocal(col[:], col[:]))
                link(dve.tensor_tensor(prob[:], prob[:], over_last(col[:], E0), ALU.mult))
                for e in range(E0):
                    link(dve.memset(gt[:], 0.0))
                    mine = prob[:, :, e:e + 1]
                    if e > 0:
                        link(dve.tensor_tensor(gt[:, :, 0:e], prob[:, :, 0:e], mine.to_broadcast([P, B, e]), ALU.is_ge))
                    if e < E0 - 1:
                        n = E0 - 1 - e
                        link(dve.tensor_tensor(gt[:, :, e + 1:], prob[:, :, e + 1:], mine.to_broadcast([P, B, n]),
                                               ALU.is_gt))
                    link(dve.tensor_reduce(col[:], gt[:], AX.X, ALU.add))
                    link(dve.tensor_scalar(chosen[:, :, e], col[:], 2.0, None, ALU.is_lt))
                link(dve.tensor_tensor(prob[:], prob[:], chosen, ALU.mult))
                link(dve.tensor_reduce(col[:], prob[:], AX.X, ALU.add))
                link(dve.reciprocal(col[:], col[:]))
                link(dve.tensor_tensor(weight, prob[:], over_last(col[:], E0), ALU.mult))
                dve.tensor_scalar(chosen, weight, 0.0, None, ALU.is_gt).then_inc(to_act, 1)
                dve.wait_ge(to_act, 2)
                dve.wait_ge(from_act, 3)
                link(dve.tensor_scalar(bt[:], bt[:], 1.0, None, ALU.add))
                link(dve.reciprocal(scal[:, :, 0:H], bt[:]))
                link(dve.tensor_tensor(z[:], logit[:, :, E0 + H:], over_mid(dtb[:], B), ALU.add))
                link(dve.tensor_scalar(soft[:], z[:], 0.0, None, ALU.max))
                dve.scalar_tensor_tensor(mag[:], z[:], -1.0, z[:], ALU.mult, ALU.max).then_inc(to_act, 1)
                dve.wait_ge(from_act, 4)
                log1p(link, dve, mag[:], z[:], square[:])
                link(dve.tensor_tensor(soft[:], soft[:], mag[:], ALU.add))
                dve.scalar_tensor_tensor(scal[:, :, H:], soft[:], -1.0, over_mid(rate[:], B), ALU.mult, ALU.mult)\
                    .then_inc(to_act, 1)
                dve.wait_ge(from_act, 5)


SLOTS = 2 * T


def delta_slots(nc, core, d, weight, chosen, scal, beta2, beta3):
    with Stage(nc, "dz") as s:
        upto, ones, places, number = (s.sb("upto", [P, T]), s.sb("ones", [P, P]), s.sb("places", [P, SLOTS]),
                                      s.sb("number", [P, 2]))
        total, first, slot = (s.sb(n, [P, B, E0]) for n in ("total", "first", "slot"))
        hot = s.sb("hot", [P, E0, SLOTS])
        inside, back, backT = s.sb("inside", [P, B, SLOTS]), s.sb("back", [P, B, SLOTS]), s.sb("backT", [P, B, 2, T])
        there, begins = s.sb("there", [P, B, 2, 2 * H]), s.sb("begins", [P, B, E0])
        fresh, decay, rows = s.sb("fresh", [P, 2, B]), s.sb("decay", [P, 2, BH]), s.sb("rows", [P, SLOTS])
        pc, ps, pr = s.ps("pc", [P, BANK]), s.ps("ps", [P, BANK]), s.ps("pr", [P, BANK])
        pt = [s.ps(f"pt{i}", [P, BANK]) for i in range(4)]
        loaded, dve_step, counted, hot_ready, moved, decay_ready, rows_turned, rows_ready, stored, turned, copied = (
            s.sem(n) for n in ("loaded", "dve_step", "counted", "hot_ready", "moved", "decay_ready", "rows_turned",
                               "rows_ready", "stored", "turned", "copied"))
        with nc.Block() as block:
            @block.sync
            def _(sp):
                sp.dma_start(upto[:], d["up_to"]).then_inc(loaded, 16)
                sp.dma_start(places[:], d["places"].partition_broadcast(P)).then_inc(loaded, 16)
                sp.dma_start(number[:], d["number"]).then_inc(loaded, 16)
                sp.wait_ge(hot_ready, B)
                sp.dma_start(core.slot_scratch.rearrange("b t s -> t b s"), inside[:]).then_inc(stored, 16)
                sp.wait_ge(rows_ready, 1)
                sp.dma_start(core.decay_scratch, rows[:]).then_inc(stored, 16)
                sp.wait_ge(copied, B // 2)
                sp.dma_start(core.back_scratch.rearrange("b s k t -> s b k t"), backT[:]).then_inc(stored, 16)
                sp.wait_ge(stored, 48)

            @block.tensor
            def _(pe):
                pe.wait_ge(loaded, 48)
                pe.wait_ge(dve_step, 1)
                flat_chosen = chosen.rearrange("p b e -> p (b e)")
                pe.matmul(pc[:, 0:B * E0], upto[:], flat_chosen, start=True, stop=True)
                pe.matmul(pc[:, B * E0:2 * B * E0], ones[:], flat_chosen, start=True, stop=True).then_inc(counted, 1)
                for b in range(B):
                    pe.wait_ge(hot_ready, b + 1)
                    for k in range(2):
                        mm = pe.matmul(ps[:, (2 * b + k) * 2 * H:(2 * b + k + 1) * 2 * H],
                                       inside[:, b, k * T:(k + 1) * T], scal[:, b, :], start=True, stop=True)
                    if b == B - 1:
                        mm.then_inc(moved, 1)
                    i = b // 2
                    if i >= 4 and b % 2 == 0:
                        pe.wait_ge(copied, i - 3)
                    for k in range(2):
                        mm = pe.transpose(pt[i % 4][:, (b % 2 * 2 + k) * T:(b % 2 * 2 + k + 1) * T],
                                          back[:, b, k * T:(k + 1) * T], core.ident[:])
                    if b % 2:
                        mm.then_inc(turned, 1)
                pe.wait_ge(decay_ready, 1)
                for k in range(2):
                    mm = pe.transpose(pr[:, k * T:(k + 1) * T], decay[:, k, :], core.ident[:])
                mm.then_inc(rows_turned, 1)

            @block.scalar
            def _(act):
                for i in range(B // 2):
                    act.wait_ge(turned, i + 1)
                    act.activation(backT[:, 2 * i:2 * i + 2, :, :].rearrange("p b k t -> p (b k t)"), pt[i % 4][:],
                                   ACT.Copy).then_inc(copied, 1)

            @block.vector
            def _(dve):
                link = Link(dve, dve_step)
                link(dve.memset(ones[:], 1.0))
                dve.wait_ge(loaded, 48)
                link(dve.memset(first[:], 0.0))
                dve.wait_ge(counted, 1)
                count = pc[:, 0:B * E0].rearrange("p (b e) -> p b e", e=E0)
                link(dve.tensor_copy(total[:].rearrange("p b e -> p (b e)"), pc[:, B * E0:2 * B * E0]))
                for e in range(1, E0):
                    link(dve.tensor_tensor(first[:, :, e], first[:, :, e - 1], total[:, :, e - 1], ALU.add))
                link(dve.tensor_tensor(slot[:], count, first[:], ALU.add))
                link(dve.tensor_tensor(slot[:], slot[:], chosen, ALU.mult))
                link(dve.tensor_scalar(slot[:], slot[:], -1.0, None, ALU.add))
                for b in range(B):
                    link(dve.tensor_tensor(hot[:], over_mid(places[:], E0), over_last(slot[:, b, :], SLOTS), ALU.is_equal))
                    link(dve.tensor_reduce(inside[:, b, :], hot[:].rearrange("p e s -> p s e"), AX.X, ALU.add))
                    link(dve.tensor_tensor(hot[:], hot[:], over_last(weight[:, b, :], SLOTS), ALU.mult))
                    dve.tensor_reduce(back[:, b, :], hot[:].rearrange("p e s -> p s e"), AX.X, ALU.add)\
                        .then_inc(hot_ready, 1)
                    dve.wait_ge(hot_ready, b + 1)
                dve.wait_ge(moved, 1)
                link(dve.tensor_copy(there[:].rearrange("p b k h -> p (b k h)"), ps[:]))
                for k in range(2):
                    link(dve.tensor_scalar(begins[:], first[:], number[:, k:k + 1], None, ALU.is_equal))
                    link(dve.tensor_reduce(fresh[:, k, :], begins[:], AX.X, ALU.max))
                    link(dve.tensor_scalar(fresh[:, k, :], fresh[:, k, :], -1.0, 1.0, ALU.mult, ALU.add))
                    link(dve.tensor_tensor(decay[:, k, :].rearrange("p (b h) -> p b h", h=H), there[:, :, k, H:],
                                           over_last(fresh[:, k, :], H), ALU.mult))
                    link(dve.tensor_copy(beta2[:, :, k].rearrange("p (b h) -> p b h", h=H), there[:, :, k, 0:H]))
                for k, c in ((0, 0), (0, 1), (1, 2)):
                    link(dve.tensor_copy(beta3[:, :, c].rearrange("p (b h) -> p b h", h=H), there[:, :, k, 0:H]))
                dve.sem_inc(decay_ready, 1)
                dve.wait_ge(rows_turned, 1)
                dve.tensor_copy(rows[:], pr[:, 0:SLOTS]).then_inc(rows_ready, 1)


def delta_projections(nc, core, d, uT, qk, v):
    with Stage(nc, "dp") as s:
        w = s.sb("w", [P, 3, BANK])
        xs = [s.sb(f"xs{p}", [P, T]) for p in range(2)]
        square = s.sb("square", [P, 8, 2 * H * HV])
        length = s.sb("length", [P, 2 * BH])
        ps = [[s.ps(f"ps{p}{n}", [P, BANK]) for n in range(3)] for p in range(2)]
        loaded, dve_step, to_act, from_act = (s.sem(n) for n in ("loaded", "dve_step", "to_act", "from_act"))
        x_in, made, silu_done = s.pair("x_in"), s.pair("made"), s.pair("silu_done")
        W = 2 * HV
        s.start_at_one(*silu_done, *made)
        with nc.Block() as block:
            @block.sync
            def _(sp):
                sp.dma_start(w[:], d["L0_qkv_w"]).then_inc(loaded, 16)

            @block.tensor
            def _(pe):
                pe.wait_ge(loaded, 16)
                with pe.Fori(0, B // 2) as j:
                    for p in range(2):
                        pe.wait_ge(x_in[p], j + 1)
                        pe.wait_ge(silu_done[p], j + 1)
                        for n in range(3):
                            mm = pe.matmul(ps[p][n][:], xs[p][:], w[:, n, :], start=True, stop=True)
                        mm.then_inc(made[p], 1)

            @block.scalar
            def _(act):
                with act.Fori(0, B // 2) as j:
                    for p in range(2):
                        act.wait_ge(made[p], j + 1)
                        act.activation(xs[p][:], uT[:, bass.ds((2 * j + p) * T, T)], ACT.Copy).then_inc(x_in[p], 1)
                    for p in range(2):
                        act.wait_ge(made[p], j + 2)
                        here = qk[:, bass.ds((2 * j + p) * H * W, H * W)].rearrange("p (h w) -> p h w", h=H)
                        for n in range(2):
                            act.activation(here[:, :, n * HV:(n + 1) * HV],
                                           ps[p][n][:].rearrange("p (h w) -> p h w", h=H), ACT.Silu)
                        act.activation(v[:, bass.ds((2 * j + p) * BANK, BANK)], ps[p][2][:], ACT.Silu)\
                            .then_inc(silu_done[p], 1)
                act.wait_ge(to_act, 1)
                act.activation(length[:], length[:], ACT.Sqrt).then_inc(from_act, 1)

            @block.vector
            def _(dve):
                link = Link(dve, dve_step)
                for p in range(2):
                    dve.wait_ge(silu_done[p], B // 2 + 1)
                groups = qk.rearrange("p (g n) -> p g n", n=HV)
                for c in range(4):
                    part = slice(c * 64, (c + 1) * 64)
                    sq = square[:, 0:4, :].rearrange("p a n -> p (a n)").rearrange("p (g n) -> p g n", n=HV)
                    link(dve.tensor_tensor(sq, groups[:, part, :], groups[:, part, :], ALU.mult))
                    link(dve.tensor_reduce(length[:, part], sq, AX.X, ALU.add))
                dve.tensor_scalar(length[:], length[:], 1e-6, None, ALU.add).then_inc(to_act, 1)
                dve.wait_ge(from_act, 1)
                link(dve.reciprocal(length[:], length[:]))
                queries = length[:].rearrange("p (i n) -> p i n", n=2)[:, :, 0:1]
                link(dve.tensor_scalar(queries, queries, HV ** -0.5, None, ALU.mult))
                link(dve.tensor_tensor(groups, groups, over_last(length[:], HV), ALU.mult))


def delta_memories(nc, core, d, qk, v, beta2, beta3):
    W = 2 * HV
    LEVELS = 7
    E = 4
    with Stage(nc, "dm") as s:
        strict, eye = s.sb("strict", [P, T]), s.sb("eye", [P, E, T])
        eye_wide = s.sb("eye_wide", [P, SLOTS])
        levels = s.sb("levels", [P, LEVELS, T])

        def two(n, shape):
            return [s.sb(f"{n}{p}", shape) for p in range(2)]

        inside, back = two("inside", [P, SLOTS]), two("back", [P, 2, T])
        near, kq = two("near", [P, 2 * W]), two("kq", [HV, 2, 2, SLOTS])
        a, D_T, weights, PT = two("a", [P, 2, SLOTS]), two("D", [P, 2, 3, T]), two("weights", [P, 2, 3, T]), \
            two("PT", [P, 2, 3, T])
        NT, off, Y, X, Z = (two(n, [P, E, T]) for n in ("NT", "off", "Y", "X", "Z"))
        across = two("across", [P, 2, T])
        values, second, delta, o = (two("values", [P, 2, 2, HV]), two("second", [P, 2, HV]),
                                    two("delta", [P, 2, 2, HV]), two("o", [P, 2, 2 * HV]))
        pA, pY, pX, pZ = ([s.ps(f"{n}{p}", [P, BANK]) for p in range(2)] for n in ("pA", "pY", "pX", "pZ"))
        const_in = s.sem("const_in")
        (a_in, near_in, gathered, copied, products, strict_ready, across_ready, pt_ready, scanned, weights_ready,
         z_ready, x_turned, off_ready, y_made, y_ready, xz_made, x_copied, z_copied, delta_made, delta_ready, r_made,
         second_ready, o_made, o_ready, out_made, dve_step, decay_beta, slots_in) = (s.pair(n) for n in (
            "a_in", "near_in", "gathered", "copied", "products", "strict_ready", "across_ready", "pt_ready", "scanned",
            "weights_ready", "z_ready", "x_turned", "off_ready", "y_made", "y_ready", "xz_made", "x_copied", "z_copied",
            "delta_made", "delta_ready", "r_made", "second_ready", "o_made", "o_ready", "out_made", "dve_step",
            "decay_beta", "slots_in"))
        turn_done = [s.pair(f"turn_done{q}_") for q in range(2)]
        L = LEVELS - 1

        def cols(x3):
            return x3[:].rearrange("p e t -> p (e t)")

        def turns(jj):
            for q in range(2):
                for half in range(2):
                    yield 4 * jj + 2 * q + half, q, half

        def wait_last_turn(eng, p, jj, q, half):
            if half:
                eng.wait_ge(turn_done[q][p], 2 * jj + 2)
            elif q:
                eng.wait_ge(turn_done[0][p], 2 * jj + 3)
            else:
                eng.wait_ge(turn_done[1][p], 2 * jj + 1)

        s.start_at_one(*turn_done[0], *turn_done[1], *scanned, *o_made, *weights_ready)
        with nc.Block() as block:
            @block.sync
            def _(sp):
                sp.dma_start(strict[:], d["strict_upper"]).then_inc(const_in, 16)
                sp.dma_start(eye[:], d["ident"].unsqueeze(1).to_broadcast([P, E, T])).then_inc(const_in, 16)
                sp.dma_start(eye_wide[:], d["eye_wide"]).then_inc(const_in, 16)
                sp.dma_start(levels[:], d["level_masks"]).then_inc(const_in, 16)
                with sp.Fori(0, B // 2) as jj:
                    for j, q, half in turns(jj):
                        if half == 0:
                            for p in range(2):
                                sp.wait_ge(turn_done[q][p], 2 * jj + 1)
                            sp.dma_start(inside[q][:], core.slot_scratch[bass.ds(2 * jj + q, 1), :, :].rearrange(
                                "b t s -> t (b s)")).then_inc(slots_in[q], 16)
                            sp.dma_start(back[q][:], core.back_scratch[bass.ds(2 * jj + q, 1), :, :, :].rearrange(
                                "b s k t -> s (b k) t")).then_inc(slots_in[q], 16)
                        for p in range(2):
                            sp.wait_ge(scanned[p], 4 * j + 1)
                            sp.dma_start(a[p][:].rearrange("p h s -> p (h s)"), core.decay_scratch.rearrange(
                                "(i h) s -> i (h s)", h=2)[bass.ds(2 * j + p, 1), :].rearrange("i n -> (i n)")
                                .partition_broadcast(P)).then_inc(a_in[p], 16)

            @block.gpsimd
            def _(pool):
                with pool.Fori(0, B // 2) as jj:
                    for j, q, half in turns(jj):
                        for p in range(2):
                            pool.wait_ge(scanned[p], 4 * j + 5)
                            pool.wait_ge(o_made[p], j + 1)
                            w6 = weights[p][:].rearrange("p h c t -> p (h c) t")
                            pool.tensor_tensor(w6, D_T[p][:].rearrange("p h c t -> p (h c) t"),
                                               over_last(beta3[:, bass.ds((2 * j + p) * 6, 6)], T), ALU.mult)\
                                .then_inc(decay_beta[p], 1)
                        for p in range(2):
                            w6 = weights[p][:].rearrange("p h c t -> p (h c) t")
                            pool.wait_ge(across_ready[p], 2 * j + 2)
                            pool.wait_ge(pt_ready[p], 3 * j + 3)
                            pool.tensor_tensor(w6, w6, PT[p][:].rearrange("p h c t -> p (h c) t"), ALU.mult)\
                                .then_inc(weights_ready[p], 1)

            @block.scalar
            def _(act):
                with act.Fori(0, B // 2) as jj:
                    for j, q, half in turns(jj):
                        for p in range(2):
                            wait_last_turn(act, p, jj, q, half)
                            act.activation(near[p][:], qk[:, bass.ds((2 * j + p) * 2 * W, 2 * W)], ACT.Copy)\
                                .then_inc(near_in[p], 1)
                        for p in range(2):
                            act.wait_ge(gathered[p], j + 1)
                            for h, bank in ((0, pY[p]), (1, pZ[p])):
                                act.activation(kq[p][:, h].rearrange("p n s -> p (n s)"), bank[0:HV, :], ACT.Copy)\
                                    .then_inc(copied[p], 1)
                            act.activation(values[p][:].rearrange("p k h n -> p (k h n)"), pX[p][:, 0:4 * HV], ACT.Copy)\
                                .then_inc(copied[p], 1)
                        for p in range(2):
                            act.wait_ge(strict_ready[p], 3 * j + 3)
                            act.wait_ge(across_ready[p], 2 * j + 2)
                            act.wait_ge(weights_ready[p], j + 1)
                            for h, bank in ((0, pY[p]), (1, pZ[p])):
                                act.activation(PT[p][:, h, 0:2, :].rearrange("p c t -> p (c t)"), bank[:, SLOTS:BANK],
                                               ACT.Copy).then_inc(pt_ready[p], 1)
                            act.activation(PT[p][:, :, 2, :], pA[p][:].rearrange("p (h n t) -> p h n t", h=2, n=2)[:, :, 1],
                                           ACT.Copy).then_inc(pt_ready[p], 1)
                        for p in range(2):
                            act.wait_ge(x_turned[p], j + 1)
                            act.activation(cols(X[p]), pX[p][:], ACT.Copy).then_inc(x_copied[p], 1)
                        for l in range(L - 1):
                            for p in range(2):
                                act.wait_ge(xz_made[p], j * L + l + 1)
                                act.activation(cols(X[p]), pX[p][:], ACT.Copy).then_inc(x_copied[p], 1)
                        for k in range(2):
                            for p in range(2):
                                act.wait_ge(delta_made[p], 2 * j + k + 1)
                                act.activation(delta[p][:, :, k, :], pA[p][:, k * SLOTS:k * SLOTS + 2 * HV].rearrange(
                                    "p (h n) -> p h n", h=2), ACT.Copy).then_inc(delta_ready[p], 1)
                        for p in range(2):
                            act.wait_ge(o_made[p], j + 2)
                            act.activation(o[p][:].rearrange("p k n -> p (k n)"), pY[p][:, 0:4 * HV], ACT.Copy)\
                                .then_inc(o_ready[p], 1)

            @block.vector
            def _(dve):
                dve.wait_ge(const_in, 64)
                with dve.Fori(0, B // 2) as jj:
                    for j, q, half in turns(jj):
                        links = [Link(dve, dve_step[p], j * 2) for p in range(2)]
                        for p in range(2):
                            dve.wait_ge(a_in[p], 16 * j + 16)
                            dve.wait_ge(weights_ready[p], j + 1)
                            wait_last_turn(dve, p, jj, q, half)
                            for h in range(2):
                                dve.tensor_tensor_scan(D_T[p][:, h, 0:2, :].rearrange("p c t -> p (c t)"), a[p][:, h, :],
                                                       eye_wide[:], 0.0, ALU.mult, ALU.add).then_inc(scanned[p], 1)
                                dve.tensor_tensor_scan(D_T[p][:, h, 2, :], a[p][:, h, T:], eye_wide[:, 0:T], 0.0,
                                                       ALU.mult, ALU.add).then_inc(scanned[p], 1)
                        for p in range(2):
                            dve.wait_ge(products[p], j + 1)
                            blocks = NT[p][:].rearrange("p (h k) t -> p h k t", h=2)
                            for h, bank in ((0, pY[p]), (1, pZ[p])):
                                dve.tensor_tensor(blocks[:, h, 0, :], bank[:, 0:T], strict[:], ALU.mult)\
                                    .then_inc(strict_ready[p], 1)
                            dve.tensor_tensor(blocks[:, :, 1, :], pA[p][:].rearrange("p (h n t) -> p h n t", h=2, n=2)
                                              [:, :, 0], over_mid(strict[:], 2), ALU.mult).then_inc(strict_ready[p], 1)
                            dve.wait_ge(decay_beta[p], j + 1)
                            for h, bank in ((0, pY[p]), (1, pZ[p])):
                                dve.tensor_tensor(across[p][:, h, :], bank[:, T:SLOTS], weights[p][:, h, 1, :], ALU.mult)\
                                    .then_inc(across_ready[p], 1)
                            dve.wait_ge(strict_ready[p], 3 * j + 3)
                            links[p](dve.tensor_tensor(NT[p][:], NT[p][:],
                                                       over_last(beta2[:, bass.ds((2 * j + p) * E, E)], T), ALU.mult))
                            links[p](dve.tensor_tensor(off[p][:], NT[p][:], over_mid(levels[:, 0, :], E), ALU.mult))
                            dve.tensor_tensor(Z[p][:], eye[:], off[p][:], ALU.subtract).then_inc(z_ready[p], 1)
                            dve.wait_ge(z_ready[p], j + 1)
                            dve.tensor_tensor(off[p][:], NT[p][:], over_mid(levels[:, 1, :], E), ALU.mult)\
                                .then_inc(off_ready[p], 1)
                        for l in range(L):
                            for p in range(2):
                                dve.wait_ge(y_made[p], j * L + l + 1)
                                dve.tensor_tensor(cols(Y[p]), cols(eye), pY[p][:], ALU.subtract).then_inc(y_ready[p], 1)
                                if l < L - 1:
                                    dve.tensor_tensor(off[p][:], NT[p][:], over_mid(levels[:, l + 2, :], E), ALU.mult)\
                                        .then_inc(off_ready[p], 1)
                            for p in range(2):
                                dve.wait_ge(xz_made[p], j * L + l + 1)
                                if l < L - 1:
                                    dve.tensor_copy(cols(Z[p]), pZ[p][:]).then_inc(z_copied[p], 1)
                                else:
                                    dve.tensor_tensor(Z[p][:].rearrange("p (h k) t -> p h k t", h=2),
                                                      pZ[p][:].rearrange("p (h k t) -> p h k t", h=2, k=2),
                                                      D_T[p][:, :, 0:3:2, :], ALU.mult).then_inc(z_copied[p], 1)
                        for p in range(2):
                            dve.wait_ge(r_made[p], j + 1)
                            dve.tensor_tensor(second[p][:], values[p][:, 1], pA[p][:, T:T + 2 * HV].rearrange(
                                "p (h n) -> p h n", h=2), ALU.subtract).then_inc(second_ready[p], 1)
                        for p in range(2):
                            dve.wait_ge(out_made[p], j + 1)
                            dve.tensor_copy(v[:, bass.ds((2 * j + p) * 2 * HV, 2 * HV)],
                                            pY[p][:, SLOTS:SLOTS + 2 * HV]).then_inc(turn_done[q][p], 1)
                for p in range(2):
                    for q in range(2):
                        dve.wait_ge(turn_done[q][p], B + 1)

            @block.tensor
            def _(pe):
                pe.wait_ge(const_in, 64)
                with pe.Fori(0, B // 2) as jj:
                    for j, q, half in turns(jj):
                        if half == 0:
                            pe.wait_ge(slots_in[q], 32 * jj + 32)
                        for p in range(2):
                            pe.wait_ge(near_in[p], j + 1)
                            for h, bank in ((0, pY[p]), (1, pZ[p])):
                                for n in range(2):
                                    start = h * W + (1 - n) * HV
                                    pe.matmul(bank[0:HV, n * SLOTS:(n + 1) * SLOTS], near[p][:, start:start + HV],
                                              inside[q][:], start=True, stop=True)
                            for k in range(2):
                                mm = pe.matmul(pX[p][:, k * 2 * HV:(k + 1) * 2 * HV], inside[q][:, k * T:(k + 1) * T],
                                               v[:, bass.ds((2 * j + p) * 2 * HV, 2 * HV)], start=True, stop=True)
                            mm.then_inc(gathered[p], 1)
                        for p in range(2):
                            pe.wait_ge(copied[p], 3 * j + 3)
                            for h, bank in ((0, pY[p]), (1, pZ[p])):
                                pe.matmul(bank[:], kq[p][:, h, 0, 0:T], kq[p][:, h].rearrange("p n s -> p (n s)"),
                                          start=True, stop=True)
                                mm = pe.matmul(pA[p][:, h * SLOTS:(h + 1) * SLOTS], kq[p][:, h, 0, T:], kq[p][:, h, :, T:],
                                               start=True, stop=True)
                            mm.then_inc(products[p], 1)
                        for p in range(2):
                            pe.wait_ge(z_ready[p], j + 1)
                            for e in range(E):
                                mm = pe.transpose(pX[p][:, e * T:(e + 1) * T], Z[p][:, e, :], core.ident[:])
                            mm.then_inc(x_turned[p], 1)
                        for l in range(L):
                            for p in range(2):
                                if l == 0:
                                    pe.wait_ge(pt_ready[p], 3 * j + 3)
                                pe.wait_ge(x_copied[p], j * L + l + 1)
                                pe.wait_ge(off_ready[p], j * L + l + 1)
                                if l > 0:
                                    pe.wait_ge(z_copied[p], j * L + l)
                                for e in range(E):
                                    mm = pe.matmul(pY[p][:, e * T:(e + 1) * T], off[p][:, e, :], X[p][:, e, :],
                                                   start=True, stop=True)
                                mm.then_inc(y_made[p], 1)
                            for p in range(2):
                                pe.wait_ge(y_ready[p], j * L + l + 1)
                                if l < L - 1:
                                    for e in range(E):
                                        pe.matmul(pX[p][:, e * T:(e + 1) * T], Z[p][:, e, :], Y[p][:, e, :],
                                                  start=True, stop=True)
                                for e in range(E):
                                    mm = pe.matmul(pZ[p][:, e * T:(e + 1) * T], Y[p][:, e, :], Z[p][:, e, :],
                                                   start=True, stop=True)
                                mm.then_inc(xz_made[p], 1)
                        for p in range(2):
                            pe.wait_ge(z_copied[p], j * L + L)
                            for h in range(2):
                                mm = pe.matmul(pA[p][:, h * HV:(h + 1) * HV], Z[p][:, 2 * h, :], values[p][:, 0, h, :],
                                               start=True, stop=True)
                            mm.then_inc(delta_made[p], 1)
                        for p in range(2):
                            pe.wait_ge(delta_ready[p], 2 * j + 1)
                            pe.wait_ge(across_ready[p], 2 * j + 2)
                            for h in range(2):
                                mm = pe.matmul(pA[p][:, T + h * HV:T + (h + 1) * HV], across[p][:, h, :],
                                               delta[p][:, h, 0, :], start=True, stop=True)
                            mm.then_inc(r_made[p], 1)
                        for p in range(2):
                            pe.wait_ge(second_ready[p], j + 1)
                            for h in range(2):
                                mm = pe.matmul(pA[p][:, SLOTS + h * HV:SLOTS + (h + 1) * HV], Z[p][:, 2 * h + 1, :],
                                               second[p][:, h, :], start=True, stop=True)
                            mm.then_inc(delta_made[p], 1)
                        for p in range(2):
                            pe.wait_ge(delta_ready[p], 2 * j + 2)
                            pe.wait_ge(weights_ready[p], j + 2)
                            for h in range(2):
                                pe.matmul(pY[p][:, h * HV:(h + 1) * HV], weights[p][:, h, 0, :], delta[p][:, h, 0, :],
                                          start=True, stop=True)
                                there = pY[p][:, T + h * HV:T + (h + 1) * HV]
                                pe.matmul(there, weights[p][:, h, 1, :], delta[p][:, h, 0, :], start=True, stop=False)
                                mm = pe.matmul(there, weights[p][:, h, 2, :], delta[p][:, h, 1, :], start=False, stop=True)
                            mm.then_inc(o_made[p], 1)
                        for p in range(2):
                            pe.wait_ge(o_ready[p], j + 1)
                            for k in range(2):
                                mm = pe.matmul(pY[p][:, SLOTS:SLOTS + 2 * HV], back[q][:, k, :], o[p][:, k, :],
                                               start=(k == 0), stop=(k == 1))
                            mm.then_inc(out_made[p], 1)


def delta_output(nc, core, d, uT, mixed):
    with Stage(nc, "do") as s:
        wg, wo, norm = s.sb("wg", [P, BANK]), s.sb("wo", [P, 4, D]), s.sb("norm", [P, HV])
        length = s.sb("length", [P, BH])
        square = s.sb("square", [P, 32, HV])

        def two(n, shape):
            return [s.sb(f"{n}{p}", shape) for p in range(2)]

        xs, gate, gated, gT = two("xs", [P, T]), two("gate", [P, BANK]), two("gated", [P, BANK]), two("gT", [P, 4, T])
        pg, pt, py = ([s.ps(f"{n}{p}", [P, BANK]) for p in range(2)] for n in ("pg", "pt", "py"))
        loaded, dve_step, to_act, from_act, scaled = (s.sem(n) for n in ("loaded", "dve_step", "to_act", "from_act",
                                                                        "scaled"))
        x_in, gate_made, gate_ready, gated_ready, turned, copied, made, added = (s.pair(n) for n in (
            "x_in", "gate_made", "gate_ready", "gated_ready", "turned", "copied", "made", "added"))
        s.start_at_one(*added, *gate_ready, *turned, *gate_made, *gated_ready, *copied)
        with nc.Block() as block:
            @block.sync
            def _(sp):
                sp.dma_start(wg[:], d["L0_gate_w"]).then_inc(loaded, 16)
                sp.dma_start(wo[:], d["L0_out_w"]).then_inc(loaded, 16)
                sp.dma_start(norm[:], d["L0_o_norm"].partition_broadcast(P)).then_inc(loaded, 16)

            @block.vector
            def _(dve):
                link = Link(dve, dve_step)
                groups = mixed.rearrange("p (g n) -> p g n", n=HV)
                for c in range(4):
                    part = slice(c * 32, (c + 1) * 32)
                    link(dve.tensor_tensor(square[:], groups[:, part, :], groups[:, part, :], ALU.mult))
                    link(dve.tensor_reduce(length[:, part], square[:], AX.X, ALU.add))
                dve.tensor_scalar(length[:], length[:], 1.0 / HV, 1e-5, ALU.mult, ALU.add).then_inc(to_act, 1)
                dve.wait_ge(from_act, 1)
                link(dve.reciprocal(length[:], length[:]))
                link(dve.tensor_tensor(groups, groups, over_last(length[:], HV), ALU.mult))
                dve.wait_ge(loaded, 48)
                dve.tensor_tensor(groups, groups, over_mid(norm[:], BH), ALU.mult).then_inc(scaled, 1)
                dve.wait_ge(scaled, 1)
                with dve.Fori(0, B // 2) as j:
                    for p in range(2):
                        dve.wait_ge(gate_ready[p], j + 2)
                        dve.wait_ge(turned[p], j + 1)
                        dve.tensor_tensor(gated[p][:], mixed[:, bass.ds((2 * j + p) * BANK, BANK)], gate[p][:], ALU.mult)\
                            .then_inc(gated_ready[p], 1)
                    for p in range(2):
                        dve.wait_ge(turned[p], j + 2)
                        dve.tensor_copy(gT[p][:].rearrange("p a t -> p (a t)"), pt[p][:]).then_inc(copied[p], 1)
                    for p in range(2):
                        dve.wait_ge(made[p], j + 1)
                        here = flat(core.h[:])[:, bass.ds((2 * j + p) * D, D)]
                        dve.tensor_tensor(here, here, py[p][:, 0:D], ALU.add).then_inc(added[p], 1)
                for p in range(2):
                    dve.wait_ge(added[p], B // 2 + 1)

            @block.scalar
            def _(act):
                act.wait_ge(to_act, 1)
                act.activation(length[:], length[:], ACT.Sqrt).then_inc(from_act, 1)
                with act.Fori(0, B // 2) as j:
                    for p in range(2):
                        act.wait_ge(gate_made[p], j + 1)
                        act.activation(xs[p][:], uT[:, bass.ds((2 * j + p) * T, T)], ACT.Copy).then_inc(x_in[p], 1)
                    for p in range(2):
                        act.wait_ge(gate_made[p], j + 2)
                        act.wait_ge(gated_ready[p], j + 1)
                        act.activation(gate[p][:], pg[p][:], ACT.Silu).then_inc(gate_ready[p], 1)

            @block.tensor
            def _(pe):
                pe.wait_ge(loaded, 48)
                with pe.Fori(0, B // 2) as j:
                    for p in range(2):
                        pe.wait_ge(x_in[p], j + 1)
                        pe.wait_ge(gate_ready[p], j + 1)
                        pe.matmul(pg[p][:], xs[p][:], wg[:], start=True, stop=True).then_inc(gate_made[p], 1)
                    for p in range(2):
                        pe.wait_ge(gated_ready[p], j + 2)
                        pe.wait_ge(copied[p], j + 1)
                        for k in range(4):
                            mm = pe.transpose(pt[p][:, k * T:(k + 1) * T], gated[p][:, k * P:(k + 1) * P], core.ident[:])
                        mm.then_inc(turned[p], 1)
                    for p in range(2):
                        pe.wait_ge(copied[p], j + 2)
                        pe.wait_ge(added[p], j + 1)
                        for k in range(4):
                            mm = pe.matmul(py[p][:, 0:D], gT[p][:, k, :], wo[:, k, :], start=(k == 0), stop=(k == 3))
                        mm.then_inc(made[p], 1)


def l0_ffn(nc, core, d):
    with ExitStack() as st:
        def sb(n, shape):
            return st.enter_context(nc.sbuf_tensor(f"l0f_{n}", shape, F32))

        uT = sb("uT", [P, N])
        with nc.sbuf_tensor("l0f_u", [P, B, D], F32) as u:
            layer_norm(nc, "l0f_n", core.h[:], u[:], 1e-5)
            to_features(nc, "l0f_t", core, u[:], uT[:])
        beta2, beta3 = sb("beta2", [P, BH, 2]), sb("beta3", [P, BH, 3])
        with ExitStack() as before:
            weight, chosen, scal = (before.enter_context(nc.sbuf_tensor(f"l0f_{n}", [P, B, k], F32)) for n, k in (
                ("weight", E0), ("chosen", E0), ("scal", 2 * H)))
            delta_gates(nc, core, d, uT[:], weight[:], chosen[:], scal[:])
            delta_slots(nc, core, d, weight[:], chosen[:], scal[:], beta2[:], beta3[:])
        qk, v = sb("qk", [P, BH * 2 * HV]), sb("v", [P, BH * HV])
        delta_projections(nc, core, d, uT[:], qk[:], v[:])
        delta_memories(nc, core, d, qk[:], v[:], beta2[:].rearrange("p g k -> p (g k)"),
                       beta3[:].rearrange("p g k -> p (g k)"))
        delta_output(nc, core, d, uT[:], v[:])


H1, H2 = 256, 128
C1, C2 = 4 * H1 // P, 4 * H2 // P
K1 = H1 // P


def lstm_inputs(nc, core, d, u, uT, z1, z2, idle, mask_dram):
    with Stage(nc, "li") as s:
        w, b0, b1 = s.sb("w", [P, 4 * H1]), s.sb("b0", [P, C1]), s.sb("b1", [P, C2])
        ne, m = s.sb("ne", [P, B, D]), s.sb("m", [P, B])
        shut = s.sb("shut", [P, T, B])
        ps = [s.ps(f"ps{i}", [P, BANK]) for i in range(4)]
        loaded, m_ready, stored, idle_in, dve_step, made, z_ready = (
            s.sem(n) for n in ("loaded", "m_ready", "stored", "idle_in", "dve_step", "made", "z_ready"))
        TB = BANK // B
        with nc.Block() as block:
            @block.sync
            def _(sp):
                sp.dma_start(w[:], d["L1_W0"]).then_inc(loaded, 16)
                sp.dma_start(b0[:], d["L1_b0"]).then_inc(loaded, 16)
                sp.dma_start(b1[:], d["L1_b1"]).then_inc(loaded, 16)
                sp.wait_ge(m_ready, 1)
                sp.dma_start(mask_dram, m[:]).then_inc(stored, 16)
                sp.wait_ge(stored, 16)
                sp.dma_start(idle, mask_dram.rearrange("t b -> (t b)").partition_broadcast(P)).then_inc(idle_in, 16)

            @block.tensor
            def _(pe):
                pe.wait_ge(loaded, 48)
                xv = uT.rearrange("p (b t) -> p t b", t=T)
                for i in range(4 * C1):
                    c, g = i // 4, i % 4
                    if i >= 4:
                        pe.wait_ge(z_ready, i - 3)
                    pe.matmul(ps[i % 4][:], w[:, c * P:(c + 1) * P], xv[:, g * TB:(g + 1) * TB, :],
                              start=True, stop=True).then_inc(made, 1)

            @block.scalar
            def _(act):
                act.wait_ge(loaded, 48)
                for i in range(4 * C1):
                    c, g = i // 4, i % 4
                    act.wait_ge(made, i + 1)
                    act.activation(z1[:, g * TB:(g + 1) * TB, c, :],
                                   ps[i % 4][:].rearrange("p (t b) -> p t b", b=B), ACT.Identity,
                                   bias=b0[:, c:c + 1]).then_inc(z_ready, 1)

            @block.vector
            def _(dve):
                link = Link(dve, dve_step)
                link(dve.tensor_scalar(ne[:], u, 0.0, None, ALU.not_equal))
                link(dve.tensor_reduce(m[:], ne[:], AX.X, ALU.max))
                dve.tensor_scalar(m[:], m[:], -1.0, 1.0, ALU.mult, ALU.add).then_inc(m_ready, 1)
                dve.wait_ge(loaded, 48)
                link(dve.memset(z2, 0.0))
                for c in range(C2):
                    link(dve.tensor_scalar(z2[:, :, c, :], z2[:, :, c, :], b1[:, c:c + 1], None, ALU.add))
                dve.wait_ge(idle_in, 16)
                idle3 = idle.rearrange("p (t b) -> p t b", b=B)
                link(dve.tensor_scalar(shut[:], idle3, NEVER, None, ALU.mult))
                dve.wait_ge(z_ready, 4 * C1)
                for z, n in ((z1, C1 // 4), (z2, C2 // 4)):
                    for c in range(3 * n):
                        op = ALU.subtract if c // n == 1 else ALU.add
                        link(dve.tensor_tensor(z[:, :, c, :], z[:, :, c, :], shut[:], op))


def lstm_steps(nc, core, d, z1, z2, idle, yT):
    with Stage(nc, "ls") as s:
        raw = s.sb("raw", [P, K1, 4 * H1])
        U0, W1, U1 = (s.sb("U0", [P, 3, K1, 4 * H1], BF16), s.sb("W1", [P, 3, K1, 4 * H2], BF16),
                      s.sb("U1", [P, 3, 4 * H2], BF16))
        n = (C1 // 4 * B, C2 // 4 * B)
        chunks = (C1, C2)
        state = [[s.sb(f"state{l}{q}", [P, n[l]]) for q in range(2)] for l in range(2)]
        parts = [[s.sb(f"parts{l}{q}", [P, n[l] // B, 3, B], BF16) for q in range(2)] for l in range(2)]
        cell, bent, kept, fresh, left = ([s.sb(f"{name}{l}", [P, n[l]]) for l in range(2)] for name in (
            "cell", "bent", "kept", "fresh", "left"))
        sums, gates = ([s.sb(f"{name}{l}", [P, 4 * n[l]]) for l in range(2)] for name in ("sums", "gates"))
        pz = [[s.ps(f"pz{l}{q}", [P, BANK]) for q in range(2)] for l in range(2)]
        loaded, split, zeroed, copied = s.sem("loaded"), s.sem("split"), s.sem("zeroed"), s.sem("copied")
        z_made, summed, gates_ready, cell_ready, bent_ready, state_ready, parts_ready, dve_step = (
            [s.sem(f"{name}{l}") for l in range(2)] for name in (
                "z_made", "summed", "gates_ready", "cell_ready", "bent_ready", "state_ready", "parts_ready",
                "dve_step"))
        z = (z1.rearrange("p t c b -> p (t c b)"), z2.rearrange("p t c b -> p (t c b)"))
        weights = ((U0, "L1_U0", raw[:]), (W1, "L1_W1", raw[:, :, 0:4 * H2]), (U1, "L1_U1", raw[:, 0, 0:4 * H2]))

        def later(t, least):
            return not isinstance(t, int) or t >= least

        def wavefront(eng, first, both, last):
            first(0, 0)
            both(1, 1)
            both(2, 0)
            with eng.Fori(0, (T - 4) // 2) as j:
                both(2 * j + 3, 1)
                both(2 * j + 4, 0)
            both(T - 1, 1)
            last(T - 1, 1)

        with nc.Block() as block:
            @block.sync
            def _(sp):
                for i, (_, src, here) in enumerate(weights):
                    if i > 0:
                        sp.wait_ge(split, i)
                    sp.dma_start(here, d[src]).then_inc(loaded, 16)

            @block.tensor
            def _(pe):
                pe.wait_ge(split, len(weights))
                pe.wait_ge(zeroed, 6)

                def products(l, q, terms):
                    for c in range(chunks[l]):
                        for i, (w, x) in enumerate(terms):
                            mm = pe.matmul(pz[l][q][:, c * 3 * B:(c + 1) * 3 * B], w(c), x,
                                           start=False, stop=(i == len(terms) - 1), skip_group_check=True)
                    return mm

                def term(w, k, part, x):
                    x = x[:, k, :, :].rearrange("p s b -> p (s b)")
                    if w is U1:
                        return lambda c: U1[:, part, c * P:(c + 1) * P], x
                    return lambda c: w[:, part, k, c * P:(c + 1) * P], x

                def outer(l, t, q):
                    if later(t, 2):
                        pe.wait_ge(summed[l], t - 1)
                    pe.matmul(pz[l][q][:, 0:chunks[l] * 3 * B].rearrange("p (c s b) -> p s c b", s=3, b=B)[:, 0],
                              core.ident[:], z[l][:, bass.ds(t * 4 * n[l], 4 * n[l])], start=True, stop=False,
                              skip_group_check=True)

                def step1(t, q):
                    outer(0, t, q)
                    if later(t, 1):
                        pe.wait_ge(parts_ready[0], t)
                    products(0, q, [term(U0, k, part, parts[0][q]) for k in range(K1) for part in range(3)])\
                        .then_inc(z_made[0], 1)

                def step2(t, q):
                    outer(1, t, q)
                    pe.wait_ge(parts_ready[0], t + 1)
                    if later(t, 1):
                        pe.wait_ge(parts_ready[1], t)
                    products(1, q, [term(W1, k, part, parts[0][1 - q]) for k in range(K1) for part in range(3)]
                             + [term(U1, 0, part, parts[1][q]) for part in range(3)]).then_inc(z_made[1], 1)

                step1(0, 0)
                step1(1, 1)
                step2(0, 0)
                step1(2, 0)
                step2(1, 1)
                with pe.Fori(0, (T - 4) // 2) as j:
                    step1(2 * j + 3, 1)
                    step2(2 * j + 2, 0)
                    step1(2 * j + 4, 0)
                    step2(2 * j + 3, 1)
                step1(T - 1, 1)
                step2(T - 2, 0)
                step2(T - 1, 1)

            @block.scalar
            def _(act):
                def step(l, t):
                    act.wait_ge(summed[l], t + 1)
                    act.activation(gates[l][:, 0:3 * n[l]], sums[l][:, 0:3 * n[l]], ACT.Sigmoid)
                    act.activation(gates[l][:, 3 * n[l]:4 * n[l]], sums[l][:, 3 * n[l]:4 * n[l]], ACT.Tanh)\
                        .then_inc(gates_ready[l], 1)
                    act.wait_ge(cell_ready[l], t + 1)
                    act.activation(bent[l][:], cell[l][:], ACT.Tanh).then_inc(bent_ready[l], 1)

                def both(t, q):
                    step(0, t)
                    step(1, t - 1)

                wavefront(act, lambda t, q: step(0, t), both, lambda t, q: step(1, t))

            @block.gpsimd
            def _(pool):
                with pool.Fori(0, T // 2) as j:
                    for q in range(2):
                        pool.wait_ge(state_ready[1], 2 * j + q + 1)
                        pool.tensor_copy(yT.rearrange("p (b t) -> p t b", t=T)[:, bass.ds(2 * j + q, 1), :],
                                         state[1][1 - q][:].rearrange("p (t b) -> p t b", t=1)).then_inc(copied, 1)
                pool.wait_ge(copied, T)

            @block.vector
            def _(dve):
                for l in range(2):
                    dve.memset(state[l][0][:], 0.0).then_inc(zeroed, 1)
                    dve.memset(parts[l][0][:], 0.0).then_inc(zeroed, 1)
                    dve.memset(cell[l][:], 0.0).then_inc(zeroed, 1)
                dve.wait_ge(zeroed, 6)
                setup = Link(dve, dve_step[0])
                for i, (w, _, here) in enumerate(weights):
                    dve.wait_ge(loaded, 16 * i + 16)
                    for part in range(2):
                        setup(dve.tensor_copy(w[:, part], here))
                        setup(dve.tensor_tensor(here, here, w[:, part], ALU.subtract))
                    dve.tensor_copy(w[:, 2], here).then_inc(split, 1)
                base = (setup.n, 0)

                def step(l, t, q):
                    link = Link(dve, dve_step[l], base[l] + t * 3)
                    i, f, o, c = (gates[l][:, k * n[l]:(k + 1) * n[l]] for k in range(4))
                    if later(t, 1):
                        dve.wait_ge(state_ready[l], t)
                    dve.tensor_tensor(kept[l][:].rearrange("p (k b) -> p k b", b=B),
                                      state[l][q][:].rearrange("p (k b) -> p k b", b=B),
                                      over_mid(idle[:, bass.ds(t * B, B)], n[l] // B), ALU.mult)
                    dve.wait_ge(z_made[l], t + 1)
                    dve.tensor_reduce(sums[l][:].rearrange("p (c b) -> p c b", b=B),
                                      pz[l][q][:, 0:chunks[l] * 3 * B].rearrange("p (c s b) -> p c b s", s=3, b=B),
                                      AX.X, ALU.add).then_inc(summed[l], 1)
                    dve.wait_ge(gates_ready[l], t + 1)
                    dve.tensor_tensor(fresh[l][:], i, c, ALU.mult)
                    link(dve.tensor_tensor(cell[l][:], f, cell[l][:], ALU.mult))
                    dve.tensor_tensor(cell[l][:], cell[l][:], fresh[l][:], ALU.add).then_inc(cell_ready[l], 1)
                    dve.wait_ge(bent_ready[l], t + 1)
                    link(dve.tensor_tensor(fresh[l][:], o, bent[l][:], ALU.mult))
                    if l == 1 and later(t, 2):
                        dve.wait_ge(copied, t - 1)
                    new, rest, more, old = (x[:].rearrange("p (k b) -> p k b", b=B) for x in (
                        state[l][1 - q], left[l], fresh[l], kept[l]))
                    high, middle, low = (parts[l][1 - q][:, :, part, :] for part in range(3))
                    dve.tensor_tensor(high, more, old, ALU.add)
                    dve.tensor_tensor(new, more, old, ALU.add).then_inc(state_ready[l], 1)
                    dve.wait_ge(state_ready[l], t + 1)
                    dve.tensor_tensor(middle, new, high, ALU.subtract)
                    link(dve.tensor_tensor(rest, new, high, ALU.subtract))
                    dve.tensor_tensor(low, rest, middle, ALU.subtract).then_inc(parts_ready[l], 1)

                def both(t, q):
                    step(0, t, q)
                    step(1, t - 1, 1 - q)

                wavefront(dve, lambda t, q: step(0, t, q), both, lambda t, q: step(1, t, q))


def l1_attention(nc, core, d):
    with ExitStack() as st:
        def sb(n, shape):
            return st.enter_context(nc.sbuf_tensor(f"l1a_{n}", shape, F32))

        z1, z2, idle, yT = sb("z1", [P, T, C1, B]), sb("z2", [P, T, C2, B]), sb("idle", [P, T * B]), sb("yT", [P, N])
        with nc.sbuf_tensor("l1a_u", [P, B, D], F32) as u, nc.sbuf_tensor("l1a_uT", [P, N], F32) as uT:
            layer_norm(nc, "l1a_n", core.h[:], u[:], 1e-5)
            to_features(nc, "l1a_t", core, u[:], uT[:])
            lstm_inputs(nc, core, d, u[:], uT[:], z1[:], z2[:], idle[:], core.mask_scratch)
        lstm_steps(nc, core, d, z1[:], z2[:], idle[:], yT[:])
        add_features(nc, "l1a_r", core, yT[:], core.h[:])


GROUP = BANK // T
GROUPS = B // GROUP


def mlp(nc, name, core, xT, w1, b1, w2, b2, width, func, dst, scale=1.0):
    F = width // P
    with Stage(nc, name) as s:
        w1_s, b1_s, w2_s, b2_s = s.sb("w1", [P, width]), s.sb("b1", [P, F]), s.sb("w2", [P, F, D]), s.sb("b2", [P, D])
        mid, add = s.sb("mid", [P, F, BANK]), s.sb("add", [P, GROUP, D])
        up = [s.ps(f"up{i}", [P, BANK]) for i in range(F)]
        down = s.ps("down", [P, BANK])
        loaded, made, mid_ready, out_made, biased, added = (s.sem(n) for n in (
            "loaded", "made", "mid_ready", "out_made", "biased", "added"))
        s.start_at_one(added, mid_ready, biased, out_made)
        with nc.Block() as block:
            @block.sync
            def _(sp):
                sp.dma_start(w1_s[:], w1).then_inc(loaded, 16)
                sp.dma_start(b1_s[:], b1).then_inc(loaded, 16)
                sp.dma_start(w2_s[:], w2).then_inc(loaded, 16)
                sp.dma_start(b2_s[:], b2.partition_broadcast(P)).then_inc(loaded, 16)

            @block.tensor
            def _(pe):
                pe.wait_ge(loaded, 64)
                with pe.Fori(0, GROUPS) as g:
                    pe.wait_ge(mid_ready, g * F + 1)
                    for c in range(F):
                        pe.matmul(up[c][:], w1_s[:, c * P:(c + 1) * P], xT[:, bass.ds(g * BANK, BANK)],
                                  start=True, stop=True).then_inc(made, 1)
                    pe.wait_ge(mid_ready, g * F + F + 1)
                    pe.wait_ge(biased, g + 1)
                    for k in range(GROUP):
                        for c in range(F):
                            mm = pe.matmul(down[:, k * D:(k + 1) * D], mid[:, c, k * T:(k + 1) * T], w2_s[:, c, :],
                                           start=(c == 0), stop=(c == F - 1))
                    mm.then_inc(out_made, 1)

            @block.scalar
            def _(act):
                act.wait_ge(loaded, 64)
                with act.Fori(0, GROUPS) as g:
                    act.wait_ge(out_made, g + 1)
                    for c in range(F):
                        act.wait_ge(made, g * F + c + 1)
                        act.activation(mid[:, c, :], up[c][:], func, bias=b1_s[:, c:c + 1]).then_inc(mid_ready, 1)

            @block.vector
            def _(dve):
                dve.wait_ge(loaded, 64)
                with dve.Fori(0, GROUPS) as g:
                    dve.wait_ge(out_made, g + 2)
                    dve.wait_ge(added, g + 1)
                    dve.tensor_tensor(add[:], down[:].rearrange("p (b d) -> p b d", d=D), over_mid(b2_s[:], GROUP),
                                      ALU.add).then_inc(biased, 1)
                    dve.wait_ge(biased, g + 2)
                    here = flat(dst)[:, bass.ds(g * BANK, BANK)]
                    dve.scalar_tensor_tensor(here, flat(add[:]), scale, here, ALU.mult, ALU.add).then_inc(added, 1)
                dve.wait_ge(added, GROUPS + 1)


E1, R1, F1 = 64, 64, 4
TILES = 2 * N // P + E1


def first_hot(link, dve, hot, best, value, order, key, keybest):
    n = value.shape[2]
    link(dve.tensor_reduce(best, value, AX.X, ALU.max))
    link(dve.tensor_tensor(key, value, over_last(best, n), ALU.is_ge))
    link(dve.tensor_tensor(key, key, over_mid(order, value.shape[1]), ALU.mult))
    link(dve.tensor_reduce(keybest, key, AX.X, ALU.max))
    link(dve.tensor_tensor(hot, key, over_last(keybest, n), ALU.is_equal))


def router64(nc, core, d, xT, slot, share, owner, dst):
    with Stage(nc, "r1") as s:
        wr, cb, b2 = s.sb("wr", [P, R1]), s.sb("cb", [R1, E1]), s.sb("b2", [E1, D])
        rT = s.sb("rT", [R1, N])
        order = s.sb("order", [P, E1])
        prob, key, hot, rest, hot2, place, before = (s.sb(n, [P, B, E1]) for n in (
            "prob", "key", "hot", "rest", "hot2", "place", "before"))
        combine = s.sb("combine", [P, E1, B])
        upto, ones, starts = s.sb("upto", [P, T]), s.sb("ones", [P, P]), s.sb("starts", [P, B])
        count, tiles, until, one_row = (s.sb(n, [P, E1]) for n in ("count", "tiles", "until", "one_row"))
        over = s.sb("over", [P, E1, B])
        number, past, owner_f = s.sb("number", [1, TILES]), s.sb("past", [1, TILES, E1]), s.sb("owner_f", [1, TILES])
        slot_f = s.sb("slot_f", [P, 2, B])
        top, best1, best2, kb, total = (s.sb(n, [P, B]) for n in ("top", "best1", "best2", "kb", "total"))
        cT = s.sb("cT", [E1, N])
        pr = [s.ps(f"pr{i}", [P, BANK]) for i in range(4)]
        pl, pn = s.ps("pl", [P, B * E1]), s.ps("pn", [P, B * E1])
        chosen, prefixed = s.sem("chosen"), s.sem("prefixed")
        loaded, dve_step, r_made, r_ready, logits_made, lowered, exp_ready, combined, c_turned, c_ready, made, done = (
            s.sem(n) for n in ("loaded", "dve_step", "r_made", "r_ready", "logits_made", "lowered", "exp_ready",
                               "combined", "c_turned", "c_ready", "made", "done"))
        with nc.Block() as block:
            @block.sync
            def _(sp):
                sp.dma_start(wr[:], d["L1f_Wr"]).then_inc(loaded, 16)
                sp.dma_start(cb[:], d["L1f_codebook"]).then_inc(loaded, 16)
                sp.dma_start(b2[:], d["L1f_b2"]).then_inc(loaded, 16)
                sp.dma_start(order[:], d["order64"].partition_broadcast(P)).then_inc(loaded, 16)
                sp.dma_start(upto[:], d["up_to"]).then_inc(loaded, 16)
                sp.dma_start(starts[:], d["tile_starts"].partition_broadcast(P)).then_inc(loaded, 16)
                sp.dma_start(number[:], d["tile_numbers"].partition_broadcast(1)).then_inc(loaded, 16)

            @block.tensor
            def _(pe):
                pe.wait_ge(loaded, 112)
                for g in range(GROUPS):
                    pe.matmul(pr[g][0:R1, :], wr[:], xT[:, g * BANK:(g + 1) * BANK], start=True, stop=True)\
                        .then_inc(r_made, 1)
                for b in range(B):
                    pe.wait_ge(r_ready, b // GROUP + 1)
                    mm = pe.matmul(pl[:, b * E1:(b + 1) * E1], rT[:, b * T:(b + 1) * T], cb[:], start=True, stop=True)
                mm.then_inc(logits_made, 1)
                pe.wait_ge(chosen, 1)
                both = rest[:].rearrange("p b e -> p (b e)")
                for half in range(2):
                    part = slice(half * BANK, (half + 1) * BANK)
                    pe.matmul(pl[:, part], upto[:], both[:, part], start=True, stop=True)
                    mm = pe.matmul(pn[:, part], ones[:], both[:, part], start=True, stop=True)
                mm.then_inc(prefixed, 1)
                pe.wait_ge(combined, 1)
                for b in range(B):
                    mm = pe.transpose(pr[b // GROUP][0:E1, (b % GROUP) * T:(b % GROUP + 1) * T], combine[:, :, b],
                                      core.ident[:])
                    if b % GROUP == GROUP - 1:
                        mm.then_inc(c_turned, 1)
                for g in range(GROUPS):
                    pe.wait_ge(c_ready, g + 1)
                    for k in range(GROUP):
                        b = g * GROUP + k
                        mm = pe.matmul(pr[g][:, k * D:(k + 1) * D], cT[:, b * T:(b + 1) * T], b2[:], start=True, stop=True)
                    mm.then_inc(made, 1)

            @block.scalar
            def _(act):
                for g in range(GROUPS):
                    act.wait_ge(r_made, g + 1)
                    act.activation(rT[:, g * BANK:(g + 1) * BANK], pr[g][0:R1, :], ACT.Copy).then_inc(r_ready, 1)
                act.wait_ge(lowered, 1)
                act.activation(prob[:], prob[:], ACT.Exp, scale=1.0 / 0.7).then_inc(exp_ready, 1)
                for g in range(GROUPS):
                    act.wait_ge(c_turned, g + 1)
                    act.activation(cT[:, g * BANK:(g + 1) * BANK], pr[g][0:E1, :], ACT.Copy).then_inc(c_ready, 1)

            @block.vector
            def _(dve):
                link = Link(dve, dve_step)
                dve.wait_ge(loaded, 112)
                link(dve.memset(ones[:], 1.0))
                link(dve.memset(one_row[:], 1.0))
                link(dve.memset(before[:, 0, :], 0.0))
                dve.wait_ge(logits_made, 1)
                logits = pl[:].rearrange("p (b e) -> p b e", e=E1)
                link(dve.tensor_reduce(top[:], logits, AX.X, ALU.max))
                dve.tensor_tensor(prob[:], logits, over_last(top[:], E1), ALU.subtract).then_inc(lowered, 1)
                dve.wait_ge(exp_ready, 1)
                link(dve.tensor_reduce(top[:], prob[:], AX.X, ALU.add))
                link(dve.reciprocal(top[:], top[:]))
                link(dve.tensor_tensor(prob[:], prob[:], over_last(top[:], E1), ALU.mult))
                first_hot(link, dve, hot[:], best1[:], prob[:], order[:], key[:], kb[:])
                link(dve.scalar_tensor_tensor(rest[:], hot[:], -2.0, prob[:], ALU.mult, ALU.add))
                link(dve.tensor_reduce(best2[:], rest[:], AX.X, ALU.max))
                link(dve.tensor_tensor(total[:], best1[:], best2[:], ALU.add))
                link(dve.reciprocal(total[:], total[:]))
                link(dve.tensor_tensor(best1[:], best1[:], total[:], ALU.mult))
                link(dve.tensor_tensor(combine[:].rearrange("p e b -> p b e"), hot[:], over_last(best1[:], E1), ALU.mult))
                first_hot(link, dve, hot2[:], best2[:], rest[:], order[:], key[:], kb[:])
                dve.tensor_tensor(rest[:], hot[:], hot2[:], ALU.add).then_inc(chosen, 1)
                link(dve.tensor_tensor(best2[:], best2[:], total[:], ALU.mult))
                link(dve.tensor_copy(share[:, 0, :], best1[:]))
                link(dve.tensor_copy(share[:, 1, :], best2[:]))
                link(dve.tensor_tensor(key[:], hot2[:], over_last(best2[:], E1), ALU.mult))
                dve.tensor_tensor(combine[:].rearrange("p e b -> p b e"), combine[:].rearrange("p e b -> p b e"), key[:],
                                  ALU.add).then_inc(combined, 1)
                dve.wait_ge(prefixed, 1)
                here = pn[:].rearrange("p (b e) -> p b e", e=E1)
                for b in range(1, B):
                    link(dve.tensor_tensor(before[:, b, :], before[:, b - 1, :], here[:, b - 1, :], ALU.add))
                link(dve.tensor_tensor(count[:], before[:, B - 1, :], here[:, B - 1, :], ALU.add))
                link(dve.tensor_tensor(over[:], over_last(count[:], B), over_mid(starts[:], E1), ALU.is_gt))
                link(dve.tensor_reduce(tiles[:], over[:], AX.X, ALU.add))
                link(dve.tensor_tensor_scan(until[:], one_row[:], tiles[:], 0.0, ALU.mult, ALU.add))
                link(dve.tensor_tensor(past[:], over_last(number[:], E1), over_mid(until[0:1, :], TILES), ALU.is_ge))
                link(dve.tensor_reduce(owner_f[:], past[:], AX.X, ALU.add))
                link(dve.tensor_scalar(owner_f[:], owner_f[:], float(E1 - 1), None, ALU.min))
                link(dve.tensor_copy(owner, owner_f[:]))
                link(dve.tensor_tensor(count[:], until[:], tiles[:], ALU.subtract))
                link(dve.tensor_scalar(count[:], count[:], float(P), -1.0, ALU.mult, ALU.add))
                link(dve.tensor_tensor(place[:], pl[:].rearrange("p (b e) -> p b e", e=E1), before[:], ALU.add))
                link(dve.tensor_tensor(place[:], place[:], over_mid(count[:], B), ALU.add))
                for c, mine in enumerate((hot, hot2)):
                    link(dve.tensor_tensor(key[:], place[:], mine[:], ALU.mult))
                    link(dve.tensor_reduce(slot_f[:, c, :], key[:], AX.X, ALU.add))
                link(dve.tensor_copy(slot, slot_f[:]))
                for g in range(GROUPS):
                    dve.wait_ge(made, g + 1)
                    dve.tensor_copy(flat(dst)[:, g * BANK:(g + 1) * BANK], pr[g][:]).then_inc(done, 1)
                dve.wait_ge(done, GROUPS)


def experts64(nc, core, d, x, slot, share, owner, dst):
    SETS = 4
    with Stage(nc, "e0") as s:
        zeros = s.sb("zeros", [P, 8, D])
        zero_ready, cleared, placed = s.sem("zero_ready"), s.sem("cleared"), s.sem("placed")
        with nc.Block() as block:
            @block.vector
            def _(dve):
                dve.memset(zeros[:], 0.0).then_inc(zero_ready, 1)

            @block.sync
            def _(sp):
                sp.wait_ge(zero_ready, 1)
                for i in range(TILES // 8):
                    sp.dma_start(core.in_scratch.rearrange("(i p) d -> p i d", p=P)[:, 8 * i:8 * i + 8, :], zeros[:])\
                        .then_inc(cleared, 16)

            @block.gpsimd
            def _(pool):
                pool.wait_ge(cleared, 16 * (TILES // 8))
                for c in range(2):
                    for b in range(B):
                        pool.indirect_dma_start(core.in_scratch, bass.IndirectOffsetOnAxis(
                            ap=slot[:, c, b:b + 1], axis=0), x[:, b, :], None).then_inc(placed, 16)
                pool.wait_ge(placed, 16 * 2 * B)
    with Stage(nc, "e1") as s:
        def sets(n, shape, k=SETS):
            return [s.sb(f"{n}{p}", shape) for p in range(k)]

        w1, w2, b1 = sets("w1", [P, F1 * P]), sets("w2", [P, F1, D]), sets("b1", [P, F1])
        rows, xT, y = sets("rows", [P, D]), sets("xT", [P, P]), sets("y", [P, D])
        mid = sets("mid", [P, F1, P], 2)
        turned, up, down = ([s.ps(f"{n}{r}", [P, BANK]) for r in range(2)] for n in ("turned", "up", "down"))
        loaded, x_turned, x_ready, up_made, mid_ready, out_made, y_ready, stored, y_free = (
            [s.sem(f"{n}{p}") for p in range(SETS)] for n in (
                "loaded", "x_turned", "x_ready", "up_made", "mid_ready", "out_made", "y_ready", "stored", "y_free"))
        s.start_at_one(*out_made, *y_ready, *y_free)
        TURNS = TILES // SETS
        with nc.Block() as block:
            @block.sync
            def _(sp):
                with sp.Fori(0, TURNS) as j:
                    for p in range(SETS):
                        sp.wait_ge(out_made[p], j + 1)
                        e = sp.value_load(owner[0:1, bass.ds(SETS * j + p, 1)], min_val=0, max_val=E1 - 1)
                        sp.dma_start(rows[p][:], core.in_scratch[bass.ds((SETS * j + p) * P, P), :]).then_inc(loaded[p], 16)
                        sp.dma_start(w1[p][:], d["L1f_W1"][bass.ds(e, 1), :, :].rearrange("e k n -> k (e n)"))\
                            .then_inc(loaded[p], 16)
                        sp.dma_start(w2[p][:], d["L1f_W2"][bass.ds(e, 1), :, :].rearrange("e (c k) n -> k (e c) n", k=P))\
                            .then_inc(loaded[p], 16)
                        sp.dma_start(b1[p][:], d["L1f_b1"][bass.ds(e, 1), :, :].rearrange("e k c -> k (e c)"))\
                            .then_inc(loaded[p], 16)

            @block.tensor
            def _(pe):
                with pe.Fori(0, TURNS) as j:
                    for half in range(2):
                        for r in range(2):
                            p = 2 * half + r
                            pe.wait_ge(loaded[p], 64 * j + 64)
                            pe.transpose(turned[r][:, 0:P], rows[p][:], core.ident[:]).then_inc(x_turned[p], 1)
                        for r in range(2):
                            p = 2 * half + r
                            pe.wait_ge(x_ready[p], j + 1)
                            for c in range(F1):
                                mm = pe.matmul(up[r][:, c * P:(c + 1) * P], w1[p][:, c * P:(c + 1) * P], xT[p][:],
                                               start=True, stop=True)
                            mm.then_inc(up_made[p], 1)
                        for r in range(2):
                            p = 2 * half + r
                            pe.wait_ge(mid_ready[p], F1 * j + F1)
                            if half:
                                pe.wait_ge(y_ready[r], j + 2)
                            else:
                                pe.wait_ge(y_ready[2 + r], j + 1)
                            for c in range(F1):
                                mm = pe.matmul(down[r][:, 0:D], mid[r][:, c, :], w2[p][:, c, :], start=(c == 0),
                                               stop=(c == F1 - 1))
                            mm.then_inc(out_made[p], 1)

            @block.scalar
            def _(act):
                with act.Fori(0, TURNS) as j:
                    for p in range(SETS):
                        act.wait_ge(up_made[p], j + 1)
                        for c in range(F1):
                            act.activation(mid[p % 2][:, c, :], up[p % 2][:, c * P:(c + 1) * P], ACT.Silu,
                                           bias=b1[p][:, c:c + 1]).then_inc(mid_ready[p], 1)

            @block.vector
            def _(dve):
                with dve.Fori(0, TURNS) as j:
                    for half in range(2):
                        for r in range(2):
                            p = 2 * half + r
                            dve.wait_ge(x_turned[p], j + 1)
                            dve.tensor_copy(xT[p][:], turned[r][:, 0:P]).then_inc(x_ready[p], 1)
                        for r in range(2):
                            p = 2 * half + r
                            dve.wait_ge(out_made[p], j + 2)
                            dve.wait_ge(y_free[p], j + 1)
                            dve.tensor_copy(y[p][:], down[r][:, 0:D]).then_inc(y_ready[p], 1)

            @block.gpsimd
            def _(pool):
                with pool.Fori(0, TURNS) as j:
                    for p in range(SETS):
                        pool.wait_ge(y_ready[p], j + 2)
                        pool.dma_start(core.out_scratch[bass.ds((SETS * j + p) * P, P), :], y[p][:]).then_inc(stored[p], 16)
                        for done in {0: (), SETS - 1: (p - 1, p)}.get(p, (p - 1,)):
                            pool.wait_ge(stored[done], 16 * j + 16)
                            pool.sem_inc(y_free[done], 1)
    with Stage(nc, "e1back") as s:
        back = [s.sb(f"back{c}", [P, B, D]) for c in range(2)]
        fetched, dve_step = s.pair("fetched"), s.sem("dve_step")
        with nc.Block() as block:
            @block.gpsimd
            def _(pool):
                for c in range(2):
                    for b in range(B):
                        pool.indirect_dma_start(back[c][:, b, :], None, core.out_scratch, bass.IndirectOffsetOnAxis(
                            ap=slot[:, c, b:b + 1], axis=0)).then_inc(fetched[c], 16)

            @block.vector
            def _(dve):
                link = Link(dve, dve_step)
                for c in range(2):
                    dve.wait_ge(fetched[c], 16 * B)
                    link(dve.tensor_tensor(back[c][:], back[c][:], over_last(share[:, c, :], D), ALU.mult))
                    link(dve.tensor_tensor(dst, dst, back[c][:], ALU.add))


def add_all(nc, name, dst, terms):
    with Stage(nc, name) as s:
        added = s.sem("added")
        with nc.Block() as block:
            @block.vector
            def _(dve):
                link = Link(dve, added)
                for x in terms:
                    link(dve.tensor_tensor(dst, dst, x, ALU.add))


def l1_ffn(nc, core, d):
    with ExitStack() as st:
        def sb(n, shape, dt=F32):
            return st.enter_context(nc.sbuf_tensor(f"l1f_{n}", shape, dt))

        u, x, xT, hmoe = sb("u", [P, B, D]), sb("x", [P, B, D]), sb("xT", [P, N]), sb("hmoe", [P, B, D])
        share, slot, owner = sb("share", [P, 2, B]), sb("slot", [P, 2, B], U32), sb("owner", [1, TILES], I32)
        layer_norm(nc, "l1f_n", core.h[:], u[:], 1e-5)
        layer_norm(nc, "l1f_n1", u[:], x[:], 1e-5, d["L1f_ln1"])
        to_features(nc, "l1f_t", core, x[:], xT[:])
        router64(nc, core, d, xT[:], slot[:], share[:], owner[:], hmoe[:])
        experts64(nc, core, d, x[:], slot[:], share[:], owner[:], hmoe[:])
        mlp(nc, "l1f_s", core, xT[:], d["L1f_Ws1"], d["L1f_bs1"], d["L1f_Ws2"], d["L1f_bs2"], 256, ACT.Silu, hmoe[:],
            scale=0.25)
        layer_norm(nc, "l1f_n2", hmoe[:], x[:], 1e-5, d["L1f_ffln"])
        to_features(nc, "l1f_t2", core, x[:], xT[:])
        add_all(nc, "l1f_a", core.h[:], (u[:], hmoe[:]))
        mlp(nc, "l1f_f", core, xT[:], d["L1f_Wf1"], d["L1f_bf1"], d["L1f_Wf2"], d["L1f_bf2"], 512, ACT.Silu, core.h[:])


QN = 8


def l2_attention(nc, core, d):
    W6 = 6 * D
    with ExitStack() as st:
        def sb(n, shape):
            return st.enter_context(nc.sbuf_tensor(f"l2a_{n}", shape, F32))

        u, uT = sb("u", [P, B, D]), sb("uT", [P, N])
        layer_norm(nc, "l2a_n", core.h[:], u[:], 1e-5)
        to_features(nc, "l2a_t", core, u[:], uT[:])
        with Stage(nc, "l2a") as s:
            w, bias = s.sb("w", [P, W6]), s.sb("bias", [P, W6])

            def two(n, shape):
                return [s.sb(f"{n}{p}", shape) for p in range(2)]

            xs, lin, low = two("xs", [P, T]), two("lin", [P, W6]), two("low", [P, D])
            f, fsum, fmax = two("f", [P, D]), two("fsum", [P, 1]), two("fmax", [P, 1])
            high_k, low_k, other = two("high_k", [P, 1]), two("low_k", [P, 1]), two("other", [P, D])
            e, ev = two("e", [P, QN, D]), two("ev", [P, QN, D])
            mass, ctx = two("mass", [P, D]), two("ctx", [P, D])
            ps = [s.ps(f"ps{p}", [P, 2 * BANK]) for p in range(2)]
            loaded = s.sem("loaded")
            x_in, made, lin_ready, f_low, f_exp, low_ready, batch_done, dve_step = (s.pair(n) for n in (
                "x_in", "made", "lin_ready", "f_low", "f_exp", "low_ready", "batch_done", "dve_step"))
            e_ready, e_used, ev_ready, weighted = (s.sem(n) for n in ("e_ready", "e_used", "ev_ready", "weighted"))
            ctx_made = s.pair("ctx_made")
            NQ = D // QN
            s.start_at_one(*batch_done, *lin_ready, e_used, weighted, *ctx_made)
            with nc.Block() as block:
                @block.sync
                def _(sp):
                    sp.dma_start(w[:], d["L2a_w"]).then_inc(loaded, 16)
                    sp.dma_start(bias[:], d["L2a_b"].partition_broadcast(P)).then_inc(loaded, 16)

                @block.tensor
                def _(pe):
                    pe.wait_ge(loaded, 32)
                    with pe.Fori(0, B // 2) as j:
                        for p in range(2):
                            pe.wait_ge(x_in[p], j + 1)
                            pe.wait_ge(lin_ready[p], j + 1)
                            pe.matmul(ps[p][:, 0:BANK], xs[p][:], w[:, 0:BANK], start=True, stop=True)
                            pe.matmul(ps[p][:, BANK:W6], xs[p][:], w[:, BANK:W6], start=True, stop=True)\
                                .then_inc(made[p], 1)

                @block.scalar
                def _(act):
                    with act.Fori(0, B // 2) as j:
                        for p in range(2):
                            act.wait_ge(batch_done[p], j + 1)
                            act.activation(xs[p][:], uT[:, bass.ds((2 * j + p) * T, T)], ACT.Copy).then_inc(x_in[p], 1)
                        for p in range(2):
                            act.wait_ge(f_low[p], j + 1)
                            act.activation(f[p][:], f[p][:], ACT.Exp).then_inc(f_exp[p], 1)
                        for p in range(2):
                            act.wait_ge(low_ready[p], j + 1)
                            for n in range(NQ):
                                act.wait_ge(e_used, (2 * j + p) * NQ + n if (p or n) else 2 * j * NQ + 1)
                                if n % 2:
                                    act.wait_ge(weighted, (2 * j + p) * (NQ // 2) + n // 2 + 1)
                                for q in range(QN):
                                    i = n * QN + q
                                    ins = act.activation(e[n % 2][:, q, :], lin[p][:, 4 * D:5 * D], ACT.Exp,
                                                         scale=lin[p][:, 3 * D + i:3 * D + i + 1], bias=low[p][:, i:i + 1])
                                ins.then_inc(e_ready, 1)

                @block.gpsimd
                def _(pool):
                    with pool.Fori(0, B // 2) as j:
                        for p in range(2):
                            pool.wait_ge(lin_ready[p], j + 2)
                            for n in range(1, NQ, 2):
                                pool.wait_ge(e_ready, (2 * j + p) * NQ + n + 1)
                                pool.wait_ge(ctx_made[1], (2 * j + p) * (NQ // 2) + n // 2 + 1)
                                pool.tensor_tensor(ev[1][:], e[1][:], over_mid(lin[p][:, 5 * D:6 * D], QN), ALU.mult)\
                                    .then_inc(weighted, 1)

                @block.vector
                def _(dve):
                    dve.wait_ge(loaded, 32)
                    with dve.Fori(0, B // 2) as j:
                        links = [Link(dve, dve_step[p], j * 12) for p in range(2)]
                        for p in range(2):
                            link = links[p]
                            qf, kf, vf, qt, kt, vt = (lin[p][:, k * D:(k + 1) * D] for k in range(6))
                            dve.wait_ge(made[p], j + 1)
                            dve.tensor_tensor(lin[p][:], ps[p][:, 0:W6], bias[:], ALU.add).then_inc(lin_ready[p], 1)
                            dve.wait_ge(lin_ready[p], j + 2)
                            link(dve.tensor_reduce(high_k[p][:], kt, AX.X, ALU.max))
                            link(dve.tensor_reduce(low_k[p][:], kt, AX.X, ALU.min))
                            link(dve.tensor_scalar(other[p][:], qt, low_k[p][:], None, ALU.mult))
                            link(dve.scalar_tensor_tensor(low[p][:], qt, high_k[p][:], other[p][:], ALU.mult, ALU.max))
                            dve.tensor_scalar(low[p][:], low[p][:], -1.0, None, ALU.mult).then_inc(low_ready[p], 1)
                            link(dve.tensor_tensor(f[p][:], qf, kf, ALU.mult))
                            link(dve.tensor_reduce(fmax[p][:], f[p][:], AX.X, ALU.max))
                            dve.tensor_scalar(f[p][:], f[p][:], fmax[p][:], None, ALU.subtract).then_inc(f_low[p], 1)
                        for p in range(2):
                            link = links[p]
                            vf, vt = lin[p][:, 2 * D:3 * D], lin[p][:, 5 * D:6 * D]
                            dve.wait_ge(f_exp[p], j + 1)
                            link(dve.tensor_reduce(fsum[p][:], f[p][:], AX.X, ALU.add))
                            link(dve.reciprocal(fsum[p][:], fsum[p][:]))
                            link(dve.scalar_tensor_tensor(f[p][:], f[p][:], fsum[p][:], vf, ALU.mult, ALU.mult))
                            for n in range(NQ):
                                dve.wait_ge(e_ready, (2 * j + p) * NQ + n + 1)
                                mine = n % 2 == 0
                                if mine:
                                    dve.wait_ge(ctx_made[0], (2 * j + p) * (NQ // 2) + n // 2 + 1)
                                    dve.tensor_tensor(ev[0][:], e[0][:], over_mid(vt, QN), ALU.mult)\
                                        .then_inc(ev_ready, 1)
                                dve.tensor_reduce(mass[p][:, n * QN:(n + 1) * QN], e[n % 2][:], AX.X, ALU.add)\
                                    .then_inc(e_used, 1)
                                if mine:
                                    dve.wait_ge(ev_ready, (2 * j + p) * (NQ // 2) + n // 2 + 1)
                                else:
                                    dve.wait_ge(weighted, (2 * j + p) * (NQ // 2) + n // 2 + 2)
                                dve.tensor_reduce(ctx[p][:, n * QN:(n + 1) * QN], ev[n % 2][:], AX.X, ALU.add)\
                                    .then_inc(ctx_made[n % 2], 1)
                            dve.wait_ge(ctx_made[1], (2 * j + p + 1) * (NQ // 2) + 1)
                            dve.wait_ge(e_used, (2 * j + p + 1) * NQ + 1)
                            link(dve.reciprocal(mass[p][:], mass[p][:]))
                            link(dve.tensor_tensor(ctx[p][:], ctx[p][:], mass[p][:], ALU.mult))
                            here = flat(core.h[:])[:, bass.ds((2 * j + p) * D, D)]
                            link(dve.tensor_tensor(ctx[p][:], ctx[p][:], f[p][:], ALU.add))
                            dve.tensor_tensor(here, here, ctx[p][:], ALU.add).then_inc(batch_done[p], 1)
                    for p in range(2):
                        dve.wait_ge(batch_done[p], B // 2 + 1)


E2 = 8


def router8(nc, core, d, u, uT, combine, dst):
    with Stage(nc, "r2") as s:
        wr, br, order, index, last = (s.sb("wr", [P, E2]), s.sb("br", [P, E2]), s.sb("order", [P, E2]),
                                      s.sb("index", [P, E2]), s.sb("last", [P, B]))
        ones = s.sb("ones", [P, P])
        logit, rest, key, hot1, hot2, cut = (s.sb(n, [P, B, E2]) for n in ("logit", "rest", "key", "hot1", "hot2", "cut"))
        best1, best2, kb, e2, s1, s2, v1, v2, a1, a2, w1 = (s.sb(n, [P, B]) for n in (
            "best1", "best2", "kb", "e2", "s1", "s2", "v1", "v2", "a1", "a2", "w1"))
        count, full = s.sb("count", [P, 2, E2]), s.sb("full", [P, 2, E2])
        pl, pc = s.ps("pl", [P, BANK]), s.ps("pc", [P, BANK])
        loaded, dve_step, made, gap_ready, exp_ready, counted, total_ready = (s.sem(n) for n in (
            "loaded", "dve_step", "made", "gap_ready", "exp_ready", "counted", "total_ready"))
        with nc.Block() as block:
            @block.sync
            def _(sp):
                sp.dma_start(wr[:], d["L2f_Wr"]).then_inc(loaded, 16)
                for dst_, src in ((br, "L2f_br"), (order, "order8"), (index, "index8")):
                    sp.dma_start(dst_[:], d[src].partition_broadcast(P)).then_inc(loaded, 16)
                sp.dma_start(last[:], d["last_token"]).then_inc(loaded, 16)

            @block.tensor
            def _(pe):
                pe.wait_ge(loaded, 80)
                for b in range(B):
                    mm = pe.matmul(pl[:, b * E2:(b + 1) * E2], uT[:, b * T:(b + 1) * T], wr[:], start=True, stop=True)
                mm.then_inc(made, 1)
                pe.wait_ge(counted, 1)
                pe.matmul(pc[:, 0:2 * E2], ones[:], count[:].rearrange("p a e -> p (a e)"), start=True, stop=True)\
                    .then_inc(total_ready, 1)

            @block.scalar
            def _(act):
                act.wait_ge(gap_ready, 1)
                act.activation(e2[:], e2[:], ACT.Exp).then_inc(exp_ready, 1)

            @block.vector
            def _(dve):
                link = Link(dve, dve_step)
                dve.wait_ge(loaded, 80)
                link(dve.memset(ones[:], 1.0))
                dve.wait_ge(made, 1)
                link(dve.tensor_tensor(logit[:], pl[:, 0:B * E2].rearrange("p (b e) -> p b e", e=E2),
                                       over_mid(br[:], B), ALU.add))
                first_hot(link, dve, hot1[:], best1[:], logit[:], order[:], key[:], kb[:])
                link(dve.scalar_tensor_tensor(rest[:], hot1[:], NEVER, logit[:], ALU.mult, ALU.add))
                first_hot(link, dve, hot2[:], best2[:], rest[:], order[:], key[:], kb[:])
                dve.tensor_tensor(e2[:], best2[:], best1[:], ALU.subtract).then_inc(gap_ready, 1)
                dve.wait_ge(exp_ready, 1)
                link(dve.tensor_scalar(s1[:], e2[:], 1.0, None, ALU.add))
                link(dve.reciprocal(s1[:], s1[:]))
                link(dve.tensor_tensor(s2[:], s1[:], e2[:], ALU.mult))
                link(dve.tensor_reduce(count[:, 0, :], hot1[:].rearrange("p b e -> p e b"), AX.X, ALU.add))
                link(dve.tensor_reduce(count[:, 1, :], hot2[:].rearrange("p b e -> p e b"), AX.X, ALU.add))
                dve.tensor_tensor(count[:, 1, :], count[:, 1, :], count[:, 0, :], ALU.add).then_inc(counted, 1)
                dve.wait_ge(total_ready, 1)
                link(dve.tensor_scalar(full[:].rearrange("p a e -> p (a e)"), pc[:, 0:2 * E2], float(N), None, ALU.is_ge))
                for n, (hot, valid, expert) in enumerate(((hot1, v1, a1), (hot2, v2, a2))):
                    link(dve.tensor_tensor(cut[:], over_last(last[:], E2), over_mid(full[:, n, :], B), ALU.mult))
                    link(dve.tensor_scalar(cut[:], cut[:], -1.0, 1.0, ALU.mult, ALU.add))
                    link(dve.tensor_tensor(hot[:], hot[:], cut[:], ALU.mult))
                    link(dve.tensor_reduce(valid[:], hot[:], AX.X, ALU.add))
                    link(dve.tensor_tensor(cut[:], hot[:], over_mid(index[:], B), ALU.mult))
                    link(dve.tensor_reduce(expert[:], cut[:], AX.X, ALU.add))
                link(dve.tensor_tensor(a1[:], a1[:], a2[:], ALU.max))
                link(dve.tensor_tensor(cut[:], over_last(a1[:], E2), over_mid(index[:], B), ALU.is_equal))
                link(dve.tensor_tensor(v1[:], v1[:], s1[:], ALU.mult))
                link(dve.tensor_tensor(v2[:], v2[:], s2[:], ALU.mult))
                link(dve.tensor_tensor(w1[:], v1[:], v2[:], ALU.add))
                link(dve.tensor_tensor(combine.rearrange("p e b -> p b e"), cut[:], over_last(w1[:], E2), ALU.mult))
                link(dve.tensor_tensor(s1[:], s1[:], v1[:], ALU.subtract))
                link(dve.tensor_tensor(s2[:], s2[:], v2[:], ALU.subtract))
                link(dve.tensor_tensor(s1[:], s1[:], s2[:], ALU.add))
                link(dve.tensor_tensor(dst, u, over_last(s1[:], D), ALU.mult))


def experts8(nc, core, d, xT, combine, dst):
    with Stage(nc, "e2") as s:
        w12 = [s.sb(f"w12{p}", [P, 2, F1 * P]) for p in range(2)]
        w3 = [s.sb(f"w3{p}", [P, F1, D]) for p in range(2)]
        left, prod = ([s.sb(f"{n}{q}", [P, BANK]) for q in range(2)] for n in ("left", "prod"))
        mid = [s.sb(f"mid{q}", [P, F1, BANK]) for q in range(2)]
        part = s.sb("part", [P, GROUP, D])
        up1, up2 = ([s.ps(f"{n}{q}", [P, BANK]) for q in range(2)] for n in ("upa", "upb"))
        down = [s.ps(f"down{q}", [P, BANK]) for q in range(2)]
        made, left_ready, prod_ready, mid_ready, out_made, weighted, added = (s.sem(n) for n in (
            "made", "left_ready", "prod_ready", "mid_ready", "out_made", "weighted", "added"))
        w_in = s.pair("w_in")
        STEPS = GROUPS * F1
        s.start_at_one(added, out_made, mid_ready, weighted, prod_ready)
        with nc.Block() as block:
            @block.sync
            def _(sp):
                def load(e, p):
                    for n, src in enumerate(("L2f_W1", "L2f_W2")):
                        sp.dma_start(w12[p][:, n, :], d[src][bass.ds(e, 1), :, :].rearrange("e k n -> k (e n)"))\
                            .then_inc(w_in[p], 16)
                    sp.dma_start(w3[p][:], d["L2f_W3"][bass.ds(e, 1), :, :].rearrange("e (c k) n -> k (e c) n", k=P))\
                        .then_inc(w_in[p], 16)

                for p in range(2):
                    load(p, p)
                with sp.Fori(1, E2 // 2) as j:
                    for p in range(2):
                        sp.wait_ge(out_made, (2 * j + p - 1) * GROUPS + 1)
                        load(2 * j + p, p)

            @block.tensor
            def _(pe):
                with pe.Fori(0, E2 // 2) as j:
                    def down_group(p, g):
                        i = (2 * j + p) * GROUPS + g
                        pe.wait_ge(mid_ready, i * F1 + F1 + 1)
                        pe.wait_ge(weighted, i if (p or g >= 1) else i + 1)
                        for k in range(GROUP):
                            for c in range(F1):
                                mm = pe.matmul(down[g % 2][:, k * D:(k + 1) * D], mid[g % 2][:, c, k * T:(k + 1) * T],
                                               w3[p][:, c, :], start=(c == 0), stop=(c == F1 - 1))
                        mm.then_inc(out_made, 1)

                    for p in range(2):
                        pe.wait_ge(w_in[p], 48 * j + 48)
                        for g in range(GROUPS):
                            for c in range(F1):
                                k = (2 * j + p) * STEPS + g * F1 + c
                                pe.wait_ge(prod_ready, k if (p or g or c) else k + 1)
                                pe.matmul(up1[c % 2][:], w12[p][:, 0, c * P:(c + 1) * P],
                                          xT[:, g * BANK:(g + 1) * BANK], start=True, stop=True)
                                pe.matmul(up2[c % 2][:], w12[p][:, 1, c * P:(c + 1) * P],
                                          xT[:, g * BANK:(g + 1) * BANK], start=True, stop=True).then_inc(made, 1)
                            if g:
                                down_group(p, g - 1)
                        down_group(p, GROUPS - 1)

            @block.scalar
            def _(act):
                with act.Fori(0, E2 // 2) as j:
                    for p in range(2):
                        base = (2 * j + p) * STEPS

                        def take_left(k):
                            act.wait_ge(made, base + k + 1)
                            act.activation(left[k % 2][:], up1[k % 2][:], ACT.Copy).then_inc(left_ready, 1)

                        take_left(0)
                        for k in range(STEPS):
                            if k + 1 < STEPS:
                                take_left(k + 1)
                            if k % F1 == 0:
                                g = k // F1
                                i = (2 * j + p) * GROUPS + g
                                act.wait_ge(out_made, i if (p or g >= 1) else i + 1)
                            act.wait_ge(prod_ready, base + k + 2)
                            act.activation(mid[k // F1 % 2][:, k % F1, :], prod[k % 2][:], ACT.Gelu).then_inc(mid_ready, 1)

            @block.vector
            def _(dve):
                with dve.Fori(0, E2 // 2) as j:
                    for p in range(2):
                        def weigh(g):
                            i = (2 * j + p) * GROUPS + g
                            dve.wait_ge(out_made, i + 2)
                            dve.wait_ge(added, i + 1)
                            dve.tensor_tensor(part[:], down[g % 2][:].rearrange("p (b d) -> p b d", d=D),
                                              over_last(combine[:, bass.ds((2 * j + p) * B + g * GROUP, GROUP)], D),
                                              ALU.mult).then_inc(weighted, 1)
                            dve.wait_ge(weighted, i + 2)
                            here = flat(dst)[:, g * BANK:(g + 1) * BANK]
                            dve.tensor_tensor(here, here, flat(part[:]), ALU.add).then_inc(added, 1)

                        for k in range(STEPS):
                            n = (2 * j + p) * STEPS + k
                            dve.wait_ge(left_ready, n + 1)
                            dve.wait_ge(mid_ready, n if (p or k) else n + 1)
                            dve.tensor_tensor(prod[k % 2][:], left[k % 2][:], up2[k % 2][:], ALU.mult)\
                                .then_inc(prod_ready, 1)
                            if k % F1 == 2 and k > F1:
                                weigh(k // F1 - 1)
                        weigh(GROUPS - 1)
                dve.wait_ge(added, E2 * GROUPS + 1)


def l2_ffn(nc, core, d):
    with ExitStack() as st:
        def sb(n, shape):
            return st.enter_context(nc.sbuf_tensor(f"l2f_{n}", shape, F32))

        u, uT, y, combine = sb("u", [P, B, D]), sb("uT", [P, N]), sb("y", [P, B, D]), sb("combine", [P, E2, B])
        layer_norm(nc, "l2f_n", core.h[:], u[:], 1e-5)
        to_features(nc, "l2f_t", core, u[:], uT[:])
        router8(nc, core, d, u[:], uT[:], combine[:], y[:])
        experts8(nc, core, d, uT[:], combine[:].rearrange("p e b -> p (e b)"), y[:])
        add_all(nc, "l2f_a", core.h[:], (y[:],))


DI, DS, DR, DC = 256, 16, 8, 4
CI = DI // P


def mamba_inputs(nc, core, d, uT, xa, gate, dt, dtu, bc_dram):
    with Stage(nc, "mi") as s:
        w_in, w_x, w_dt = s.sb("w_in", [P, 2 * DI]), s.sb("w_x", [P, CI, DR + 2 * DS]), s.sb("w_dt", [DR, DI])
        conv_w, conv_b, dt_b = s.sb("conv_w", [P, CI, DC]), s.sb("conv_b", [P, CI]), s.sb("dt_b", [P, CI])
        pad = s.sb("pad", [P, CI, B, T + DC - 1])
        dbl = s.sb("dbl", [DR + 2 * DS, N])
        mag = s.sb("mag", [P, CI, N])
        ratio = pad[:].rearrange("p c b t -> p (c b t)")[:, 0:CI * N].rearrange("p (c n) -> p c n", c=CI)
        ps = [s.ps(f"ps{i}", [P, BANK]) for i in range(8)]
        loaded, dve_step, made, evacuated, conv_ready, xa_ready, dbl_made, dbl_ready, stored, dt_made, to_act, from_act = (
            s.sem(n) for n in ("loaded", "dve_step", "made", "evacuated", "conv_ready", "xa_ready", "dbl_made",
                               "dbl_ready", "stored", "dt_made", "to_act", "from_act"))
        with nc.Block() as block:
            @block.sync
            def _(sp):
                for dst, src in ((w_in, "L3a_in"), (w_x, "L3a_x"), (w_dt, "L3a_dt"), (conv_w, "L3a_conv_w"),
                                 (conv_b, "L3a_conv_b"), (dt_b, "L3a_dt_b")):
                    sp.dma_start(dst[:], d[src]).then_inc(loaded, 16)
                sp.wait_ge(dbl_ready, 4)
                sp.dma_start(bc_dram, dbl[DR:, :]).then_inc(stored, 16)
                sp.wait_ge(stored, 16)

            @block.tensor
            def _(pe):
                pe.wait_ge(loaded, 96)
                for i in range(16):
                    c, g = i // 4, i % 4
                    if i >= 8:
                        pe.wait_ge(evacuated, i - 7)
                    pe.matmul(ps[i % 8][:], w_in[:, c * P:(c + 1) * P], uT[:, g * BANK:(g + 1) * BANK],
                              start=True, stop=True).then_inc(made, 1)
                pe.wait_ge(xa_ready, CI)
                pe.wait_ge(evacuated, 16)
                for g in range(4):
                    for c in range(CI):
                        mm = pe.matmul(ps[g][0:DR + 2 * DS, :], w_x[:, c, :], xa[:, c, g * BANK:(g + 1) * BANK],
                                       start=(c == 0), stop=(c == CI - 1))
                    mm.then_inc(dbl_made, 1)
                pe.wait_ge(dbl_ready, 4)
                for i in range(4 * CI):
                    c, g = i // 4, i % 4
                    pe.matmul(ps[i][:], w_dt[:, c * P:(c + 1) * P], dbl[0:DR, g * BANK:(g + 1) * BANK],
                              start=True, stop=True).then_inc(dt_made, 1)

            @block.scalar
            def _(act):
                act.wait_ge(loaded, 96)
                for i in range(16):
                    c, g = i // 4, i % 4
                    act.wait_ge(made, i + 1)
                    if c < CI:
                        act.activation(pad[:, c, 4 * g:4 * g + 4, DC - 1:], ps[i % 8][:].rearrange(
                            "p (b t) -> p b t", t=T), ACT.Copy).then_inc(evacuated, 1)
                    else:
                        act.activation(gate[:, c - CI, g * BANK:(g + 1) * BANK], ps[i % 8][:], ACT.Silu)\
                            .then_inc(evacuated, 1)
                for c in range(CI):
                    act.wait_ge(conv_ready, c + 1)
                    act.activation(xa[:, c, :], xa[:, c, :], ACT.Silu).then_inc(xa_ready, 1)
                for g in range(4):
                    act.wait_ge(dbl_made, g + 1)
                    act.activation(dbl[:, g * BANK:(g + 1) * BANK], ps[g][0:DR + 2 * DS, :], ACT.Copy)\
                        .then_inc(dbl_ready, 1)
                for i in range(4 * CI):
                    c, g = i // 4, i % 4
                    act.wait_ge(dt_made, i + 1)
                    act.activation(dt[:, c, g * BANK:(g + 1) * BANK], ps[i][:], ACT.Identity, bias=dt_b[:, c:c + 1])\
                        .then_inc(from_act, 1)
                act.wait_ge(to_act, 1)
                act.activation(mag[:], mag[:], ACT.Exp, scale=-1.0).then_inc(from_act, 1)

            @block.vector
            def _(dve):
                link = Link(dve, dve_step)
                link(dve.memset(pad[:, :, :, 0:DC - 1], 0.0))
                dve.wait_ge(evacuated, 4 * CI)
                for c in range(CI):
                    out3 = xa[:, c, :].rearrange("p (b t) -> p b t", t=T)
                    link(dve.tensor_scalar(out3, pad[:, c, :, 0:T], conv_w[:, c, 0:1], conv_b[:, c:c + 1],
                                           ALU.mult, ALU.add))
                    for k in range(1, DC):
                        link(dve.scalar_tensor_tensor(out3, pad[:, c, :, k:k + T], conv_w[:, c, k:k + 1], out3,
                                                      ALU.mult, ALU.add))
                    dve.sem_inc(conv_ready, 1)
                dve.wait_ge(from_act, 4 * CI)
                dve.scalar_tensor_tensor(mag[:], dt, -1.0, dt, ALU.mult, ALU.max).then_inc(to_act, 1)
                dve.wait_ge(to_act, 1)
                link(dve.tensor_scalar(dt, dt, 0.0, None, ALU.max))
                dve.wait_ge(from_act, 4 * CI + 1)
                log1p(link, dve, mag[:], ratio, dtu)
                link(dve.tensor_tensor(dt, dt, mag[:], ALU.add))
                dve.wait_ge(xa_ready, CI)
                link(dve.tensor_tensor(dtu, dt, xa, ALU.mult))


def mamba_scan(nc, core, d, xa, gate, dt, dtu, bc_dram, yT):
    with Stage(nc, "ms") as s:
        a, skip, w_out = s.sb("a", [P, CI * DS]), s.sb("skip", [P, CI]), s.sb("w_out", [P, CI, D])
        a_here = [s.sb(f"a_here{p}", [P, CI]) for p in range(2)]
        bn, cn = ([s.sb(f"{n}{p}", [P, N]) for p in range(2)] for n in ("bn", "cn"))
        decay, fed, state = ([s.sb(f"{n}{c}", [P, N]) for c in range(CI)] for n in ("decay", "fed", "state"))
        py = [s.ps(f"py{c}", [P, N]) for c in range(CI)]
        loaded, a_ready, a_copied = s.sem("loaded"), s.sem("a_ready"), s.sem("a_copied")
        bc_in = s.pair("bc_in")
        decay_ready, fed_ready, scanned, read, summed, dve_step = ([s.sem(f"{n}{c}") for c in range(CI)] for n in (
            "decay_ready", "fed_ready", "scanned", "read", "summed", "dve_step"))
        mixed, projected, out_ready = s.sem("mixed"), s.sem("projected"), s.sem("out_ready")

        def over_states(eng, turn):
            turn(0, 0, True)
            turn(1, 1, False)
            with eng.Fori(1, DS // 2) as j:
                for p in range(2):
                    turn(2 * j + p, p, False)

        with nc.Block() as block:
            @block.sync
            def _(sp):
                sp.dma_start(a[:], d["L3a_A_log"]).then_inc(loaded, 16)
                sp.dma_start(skip[:], d["L3a_D"]).then_inc(loaded, 16)
                sp.dma_start(w_out[:], d["L3a_out"]).then_inc(loaded, 16)

                def turn(n, p, first):
                    if not isinstance(n, int):
                        sp.wait_ge(read[CI - 1], n - 1)
                        sp.wait_ge(fed_ready[CI - 1], n - 1)
                    for half, dst in ((0, bn), (1, cn)):
                        sp.dma_start(dst[p][:], bc_dram[bass.ds(n + half * DS, 1), :].rearrange("a n -> (a n)")
                                     .partition_broadcast(P)).then_inc(bc_in[p], 16)

                over_states(sp, turn)

            @block.gpsimd
            def _(pool):
                def turn(n, p, first):
                    turns = n // 2 if isinstance(n, int) else (n - p) // 2
                    pool.wait_ge(bc_in[p], 32 * turns + 32)
                    for c in range(CI):
                        if not first:
                            pool.wait_ge(scanned[c], n)
                        pool.tensor_tensor(fed[c][:], dtu[:, c, :], bn[p][:], ALU.mult).then_inc(fed_ready[c], 1)

                over_states(pool, turn)

            @block.scalar
            def _(act):
                act.wait_ge(loaded, 48)
                act.activation(a[:], a[:], ACT.Exp).then_inc(a_ready, 1)
                act.wait_ge(a_ready, 2)

                def turn(n, p, first):
                    act.activation(a_here[p][:], a[:, bass.ds(n * CI, CI)], ACT.Copy).then_inc(a_copied, 1)
                    act.wait_ge(a_copied, n + 1)
                    for c in range(CI):
                        if not first:
                            act.wait_ge(scanned[c], n)
                        act.activation(decay[c][:], dt[:, c, :], ACT.Exp, scale=a_here[p][:, c:c + 1])\
                            .then_inc(decay_ready[c], 1)

                over_states(act, turn)
                for g in range(4):
                    act.wait_ge(projected, g + 1)
                    act.activation(yT[:, g * BANK:(g + 1) * BANK], py[0][:, g * BANK:(g + 1) * BANK], ACT.Copy)\
                        .then_inc(out_ready, 1)
                act.wait_ge(out_ready, 4)

            @block.vector
            def _(dve):
                dve.wait_ge(a_ready, 1)
                dve.tensor_scalar(a[:], a[:], -1.0, None, ALU.mult).then_inc(a_ready, 1)

                def turn(n, p, first):
                    for c in range(CI):
                        link = Link(dve, dve_step[c], n)
                        dve.wait_ge(decay_ready[c], n + 1)
                        link(dve.memset(decay[c][:].rearrange("p (b t) -> p b t", t=T)[:, :, 0:1], 0.0))
                        dve.wait_ge(fed_ready[c], n + 1)
                        if not first:
                            dve.wait_ge(summed[c], n)
                        dve.tensor_tensor_scan(state[c][:], decay[c][:], fed[c][:], 0.0, ALU.mult, ALU.add)\
                            .then_inc(scanned[c], 1)
                        dve.wait_ge(scanned[c], n + 1)
                        dve.tensor_tensor(state[c][:], state[c][:], cn[p][:], ALU.mult).then_inc(read[c], 1)

                over_states(dve, turn)
                for c in range(CI):
                    dve.wait_ge(summed[c], DS)
                    for g in range(4):
                        part = slice(g * BANK, (g + 1) * BANK)
                        dve.scalar_tensor_tensor(state[c][:, part], xa[:, c, part], skip[:, c:c + 1], py[c][:, part],
                                                 ALU.mult, ALU.add).then_inc(read[c], 1)
                    dve.wait_ge(read[c], DS + 4)
                    dve.tensor_tensor(state[c][:], state[c][:], gate[:, c, :], ALU.mult).then_inc(mixed, 1)

            @block.tensor
            def _(pe):
                def turn(n, p, first):
                    for c in range(CI):
                        pe.wait_ge(read[c], n + 1)
                        for g in range(4):
                            part = slice(g * BANK, (g + 1) * BANK)
                            mm = pe.matmul(py[c][:, part], core.ident[:], state[c][:, part], start=first, stop=True,
                                           skip_group_check=True)
                        mm.then_inc(summed[c], 1)

                over_states(pe, turn)
                pe.wait_ge(mixed, CI)
                for g in range(4):
                    part = slice(g * BANK, (g + 1) * BANK)
                    for c in range(CI):
                        mm = pe.matmul(py[0][:, part], w_out[:, c, :], state[c][:, part], start=(c == 0),
                                       stop=(c == CI - 1))
                    mm.then_inc(projected, 1)


def l3_attention(nc, core, d):
    with ExitStack() as st:
        def sb(n, shape):
            return st.enter_context(nc.sbuf_tensor(f"l3a_{n}", shape, F32))

        u, yT = sb("u", [P, B, D]), sb("yT", [P, N])
        layer_norm(nc, "l3a_n", core.h[:], u[:], 1e-5)
        to_features(nc, "l3a_t", core, u[:], yT[:])
        xa, gate, dt, dtu = (sb(n, [P, CI, N]) for n in ("xa", "gate", "dt", "dtu"))
        mamba_inputs(nc, core, d, yT[:], xa[:], gate[:], dt[:], dtu[:], core.bc_scratch)
        mamba_scan(nc, core, d, xa[:], gate[:], dt[:], dtu[:], core.bc_scratch, yT[:])
        add_features(nc, "l3a_r", core, yT[:], u[:])
        layer_norm(nc, "l3a_n2", u[:], u[:], 1e-12, d["L3a_ln"])
        add_all(nc, "l3a_a", core.h[:], (u[:],))


def route_sequences(nc, core, d, uT, choice, choice_dram):
    K = 4
    with Stage(nc, "rs") as s:
        w1, b1, w2, b2 = s.sb("w1", [P, P]), s.sb("b1", [P, 1]), s.sb("w2", [P, 2 * K]), s.sb("b2", [B, 2 * K])
        order, index = s.sb("order", [B, K]), s.sb("index", [B, K])
        pooled, mid = s.sb("pooled", [P, B]), s.sb("mid", [P, B])
        route, top = s.sb("route", [B, 2, K]), s.sb("top", [B, 1])
        hot, key, best, kb = s.sb("hot", [B, 2, K]), s.sb("key", [B, 2, K]), s.sb("best", [B, 2]), s.sb("kb", [B, 2])
        whole = s.sb("whole", [B, 2], I32)
        ps = [s.ps(f"ps{i}", [P, BANK]) for i in range(2)]
        loaded, dve_step, pooled_ready, mid_made, mid_ready, made, lowered, exp_ready, chosen, stored, back = (
            s.sem(n) for n in ("loaded", "dve_step", "pooled_ready", "mid_made", "mid_ready", "made", "lowered",
                               "exp_ready", "chosen", "stored", "back"))
        with nc.Block() as block:
            @block.sync
            def _(sp):
                for dst, src in ((w1, "L3f_rw1"), (b1, "L3f_rb1"), (w2, "L3f_rw2")):
                    sp.dma_start(dst[:], d[src]).then_inc(loaded, 16)
                for dst, src in ((b2, "L3f_rb2"), (order, "order4"), (index, "index4")):
                    sp.dma_start(dst[:], d[src].partition_broadcast(B)).then_inc(loaded, 16)
                sp.wait_ge(chosen, 1)
                sp.dma_start(choice_dram, whole[:]).then_inc(stored, 16)
                sp.wait_ge(stored, 16)
                sp.dma_start(choice, choice_dram.rearrange("(a b) k -> a (b k)", a=1)).then_inc(back, 16)
                sp.wait_ge(back, 16)

            @block.tensor
            def _(pe):
                pe.wait_ge(loaded, 96)
                pe.wait_ge(pooled_ready, 1)
                pe.matmul(ps[0][:, 0:B], w1[:], pooled[:], start=True, stop=True).then_inc(mid_made, 1)
                pe.wait_ge(mid_ready, 1)
                pe.matmul(ps[1][0:B, 0:2 * K], mid[:], w2[:], start=True, stop=True).then_inc(made, 1)

            @block.scalar
            def _(act):
                act.wait_ge(mid_made, 1)
                act.activation(mid[:], ps[0][:, 0:B], ACT.Gelu, bias=b1[:]).then_inc(mid_ready, 1)
                act.wait_ge(lowered, 1)
                act.activation(route[:], route[:], ACT.Exp).then_inc(exp_ready, 1)

            @block.vector
            def _(dve):
                link = Link(dve, dve_step)
                link(dve.tensor_reduce(pooled[:], uT.rearrange("p (b t) -> p b t", t=T), AX.X, ALU.add))
                dve.tensor_scalar(pooled[:], pooled[:], 1.0 / T, None, ALU.mult).then_inc(pooled_ready, 1)
                dve.wait_ge(loaded, 96)
                dve.wait_ge(made, 1)
                flat_route = route[:].rearrange("p a k -> p (a k)")
                link(dve.tensor_tensor(flat_route, ps[1][0:B, 0:2 * K], b2[:], ALU.add))
                link(dve.tensor_reduce(top[:], flat_route, AX.X, ALU.max))
                dve.tensor_scalar(flat_route, flat_route, top[:], None, ALU.subtract).then_inc(lowered, 1)
                dve.wait_ge(exp_ready, 1)
                link(dve.tensor_reduce(top[:], flat_route, AX.X, ALU.add))
                link(dve.reciprocal(top[:], top[:]))
                link(dve.tensor_scalar(flat_route, flat_route, top[:], None, ALU.mult))
                first_hot(link, dve, hot[:], best[:], route[:], order[:], key[:], kb[:])
                link(dve.tensor_tensor(hot[:], hot[:], over_mid(index[:], 2), ALU.mult))
                link(dve.tensor_reduce(best[:], hot[:], AX.X, ALU.add))
                dve.tensor_copy(whole[:], best[:]).then_inc(chosen, 1)


def l3_ffn(nc, core, d):
    with ExitStack() as st:
        def sb(n, shape, dt=F32):
            return st.enter_context(nc.sbuf_tensor(f"l3f_{n}", shape, dt))

        u, x, xT, spatialT, temporalT = (sb("u", [P, B, D]), sb("x", [P, B, D]), sb("xT", [P, N]),
                                         sb("spatialT", [P, N]), sb("temporalT", [P, N]))
        choice = sb("choice", [1, 2 * B], I32)
        layer_norm(nc, "l3f_n", core.h[:], u[:], 1e-5)
        to_features(nc, "l3f_t", core, u[:], xT[:])
        route_sequences(nc, core, d, xT[:], choice[:], core.choice_scratch)
        layer_norm(nc, "l3f_n1", u[:], x[:], 1e-5, d["L3f_norm_s"])
        to_features(nc, "l3f_t1", core, x[:], xT[:])
        attention(nc, "l3s", core, xT[:], xT[:], spatialT[:], d["L3f_spatial_w"], d["L3f_spatial_b"],
                  choice=(choice[:], 0))
        layer_norm(nc, "l3f_n2", u[:], x[:], 1e-5, d["L3f_norm_t"])
        to_features(nc, "l3f_t2", core, x[:], xT[:])
        attention(nc, "l3t", core, xT[:], xT[:], temporalT[:], d["L3f_temporal_w"], d["L3f_temporal_b"],
                  choice=(choice[:], 1), causal=True, keep=True)
        attention(nc, "l3c", core, spatialT[:], temporalT[:], xT[:], d["L3f_cross_w"], d["L3f_cross_b"])
        add_features(nc, "l3f_r", core, xT[:], u[:])
        layer_norm(nc, "l3f_n3", u[:], x[:], 1e-5, d["L3f_norm_mlp"])
        to_features(nc, "l3f_t3", core, x[:], xT[:])
        mlp(nc, "l3f_m", core, xT[:], d["L3f_mw1"], d["L3f_mb1"], d["L3f_mw2"], d["L3f_mb2"], 512, ACT.Gelu, u[:])
        add_all(nc, "l3f_a", core.h[:], (u[:],))


def layout(i):
    i = {k: np.asarray(v) for k, v in i.items()}
    f = np.float32
    o = {}

    def put(name, a):
        o[name] = np.ascontiguousarray(a)

    x = i["x"]
    pad = np.concatenate([np.zeros((B, 2), x.dtype), x, np.zeros((B, 1), x.dtype)], 1)
    put("x_windows", np.stack([pad[:, k:k + T] for k in range(4)], 0).transpose(2, 0, 1))
    inside = np.zeros((P, 3), f)
    for n, c in ((0, 1), (1, 1), (2, 2)):
        inside[c:c + T - (n + 2) + 1, n] = 1
    put("inside", inside)
    put("tok_w", i["L0_tok_proj_w"].T.reshape(3, D, D).transpose(1, 0, 2))
    put("tok_b", i["L0_tok_proj_b"])
    for n in (2, 3, 4):
        put(f"L0_tok_emb_{n}", i[f"L0_tok_emb_{n}"])
    put("ident", np.eye(P, dtype=f))
    put("head_mask", np.repeat(np.eye(H, dtype=f), HD, 0))
    put("causal", np.where(np.arange(T)[:, None] >= np.arange(T)[None], 0, NEVER).astype(f))
    put("L0_attn_w", np.concatenate([i["L0_attn_W_qkv"].T, i["L0_attn_W_out"].T], 1))
    zero = np.zeros(D, f)
    put("L0_attn_b", np.stack([i["L0_attn_pos_bias_u"].reshape(D), zero, zero, i["L0_attn_b_out"]], 1))
    put("L0_bias_v", i["L0_attn_pos_bias_v"].reshape(D, 1))
    put("L0_ln1", np.stack([i["L0_attn_ln1_g"], i["L0_attn_ln1_b"]]))
    put("L0_ln2", np.stack([i["L0_attn_ln2_g"], i["L0_attn_ln2_b"]]))
    put("L0_pos_w", i["L0_attn_W_pos"].T)
    inv = (1.0 / 10000.0 ** (np.arange(0, D, 2, dtype=f) / D)).astype(f)
    put("freq", np.broadcast_to(np.concatenate([inv, inv]), (P, D)))
    put("phase", np.broadcast_to(np.repeat(np.array([0, np.pi / 2], f), D // 2), (P, D)))
    put("L0_gates_w", np.concatenate([i["L0_ffn_Wgate"], i["L0_ffn_Wb"], i["L0_ffn_Wa"]], 1))
    put("L0_dt_bias", i["L0_ffn_dt_bias"])
    put("L0_A_log", i["L0_ffn_A_log"])
    put("L0_qkv_w", np.stack([i["L0_ffn_Wq"], i["L0_ffn_Wk"], i["L0_ffn_Wv"]], 1))
    put("L0_gate_w", i["L0_ffn_Wg"])
    put("L0_out_w", i["L0_ffn_Wo"].reshape(4, D, D).transpose(1, 0, 2))
    put("L0_o_norm", i["L0_ffn_o_norm_weight"])
    s_, t_ = np.arange(T)[:, None], np.arange(T)[None]
    put("strict_upper", (s_ < t_).astype(f))
    put("up_to", (s_ <= t_).astype(f))
    put("eye_wide", np.eye(T, 2 * T, dtype=f))
    put("places", np.arange(2 * T, dtype=f))
    put("number", np.stack([np.arange(T), np.arange(T) + T], 1).astype(f))
    put("level_masks", np.stack([((s_ >> (l + 1)) == (t_ >> (l + 1))) & ((s_ >> l) != (t_ >> l)) & (s_ < t_)
                                 for l in range(7)], 1).astype(f))

    def gate_order(a, n):
        return np.concatenate([a[..., 0:2 * n], a[..., 3 * n:4 * n], a[..., 2 * n:3 * n]], -1)

    put("L1_W0", gate_order(i["L1_attn_W0"], H1))
    put("L1_U0", gate_order(i["L1_attn_U0"], H1).reshape(K1, P, 4 * H1).transpose(1, 0, 2))
    put("L1_b0", gate_order(i["L1_attn_b0"], H1).reshape(C1, P).T)
    put("L1_W1", gate_order(i["L1_attn_W1"], H2).reshape(K1, P, 4 * H2).transpose(1, 0, 2))
    put("L1_U1", gate_order(i["L1_attn_U1"], H2))
    put("L1_b1", gate_order(i["L1_attn_b1"], H2).reshape(C2, P).T)

    def columns(a):
        return a.reshape(-1, P).T

    def chunks(a):
        return a.reshape(-1, P, a.shape[1]).transpose(1, 0, 2)

    put("L1f_ln1", np.stack([i["L1_ffn_ln1_g"], i["L1_ffn_ln1_b"]]))
    put("L1f_ffln", np.stack([i["L1_ffn_ffln_g"], i["L1_ffn_ffln_b"]]))
    put("L1f_Wr", i["L1_ffn_Wr"])
    put("L1f_codebook", i["L1_ffn_codebook"].T)
    put("order64", np.arange(E1, 0, -1).astype(f))
    put("L1f_W1", i["L1_ffn_W1"])
    put("L1f_W2", i["L1_ffn_W2"])
    put("L1f_b1", i["L1_ffn_b1"].reshape(E1, F1, P).transpose(0, 2, 1))
    put("tile_starts", np.arange(0, N, P).astype(f))
    put("tile_numbers", np.arange(TILES).astype(f))
    put("L1f_b2", i["L1_ffn_b2"])
    put("L1f_Ws1", i["L1_ffn_Ws1"])
    put("L1f_bs1", columns(i["L1_ffn_bs1"]))
    put("L1f_Ws2", chunks(i["L1_ffn_Ws2"]))
    put("L1f_bs2", i["L1_ffn_bs2"])
    put("L1f_Wf1", i["L1_ffn_Wf1"])
    put("L1f_bf1", columns(i["L1_ffn_bf1"]))
    put("L1f_Wf2", chunks(i["L1_ffn_Wf2"]))
    put("L1f_bf2", i["L1_ffn_bf2"])
    six = ("qf", "kf", "vf", "qt", "kt", "vt")
    put("L2a_w", np.concatenate([i[f"L2_attn_W_{n}"].T for n in six], 1))
    put("L2a_b", np.concatenate([i[f"L2_attn_b_{n}"] for n in six]))
    put("L2f_Wr", i["L2_ffn_Wr"])
    put("L2f_br", i["L2_ffn_br"])
    put("order8", np.arange(E2, 0, -1).astype(f))
    put("index8", np.arange(E2).astype(f))
    last = np.zeros((P, B), f)
    last[T - 1, B - 1] = 1
    put("last_token", last)
    for n in (1, 2, 3):
        put(f"L2f_W{n}", i[f"L2_ffn_W{n}"])
    put("L3a_in", i["L3_attn_in_proj_w"].T)
    put("L3a_x", chunks(i["L3_attn_x_proj_w"].T))
    put("L3a_dt", i["L3_attn_dt_proj_w"].T)
    put("L3a_conv_w", chunks(i["L3_attn_conv_w"]))
    put("L3a_conv_b", columns(i["L3_attn_conv_b"]))
    put("L3a_dt_b", columns(i["L3_attn_dt_proj_b"]))
    put("L3a_A_log", chunks(i["L3_attn_A_log"]).transpose(0, 2, 1).reshape(P, DS * CI))
    put("L3a_D", columns(i["L3_attn_D"]))
    put("L3a_out", chunks(i["L3_attn_out_proj_w"].T))
    put("L3a_ln", np.stack([i["L3_attn_ln_gamma"], i["L3_attn_ln_beta"]]))
    put("L3f_rw1", i["L3_ffn_router_w1"].T)
    put("L3f_rb1", i["L3_ffn_router_b1"].reshape(P, 1))
    put("L3f_rw2", i["L3_ffn_router_w2"].T)
    put("L3f_rb2", i["L3_ffn_router_b2"])
    put("order4", np.arange(4, 0, -1).astype(f))
    put("index4", np.arange(4).astype(f))
    for n in ("s", "t", "mlp"):
        put(f"L3f_norm_{n}", np.stack([i[f"L3_ffn_norm_{n}_w"], i[f"L3_ffn_norm_{n}_b"]]))
    put("L3f_spatial_w", np.concatenate([i["L3_ffn_sp_in_w"], i["L3_ffn_sp_out_w"]], 1).transpose(0, 2, 1))
    put("L3f_spatial_b", np.concatenate([i["L3_ffn_sp_in_b"], i["L3_ffn_sp_out_b"]], 1).reshape(4, 4, P)
        .transpose(0, 2, 1))
    put("L3f_temporal_w", np.concatenate([i[f"L3_ffn_t{n}_w"] for n in "qkvp"], 1).transpose(0, 2, 1))
    put("L3f_temporal_b", np.stack([i[f"L3_ffn_t{n}_b"] for n in "qkvp"], 2))
    put("L3f_cross_w", np.concatenate([i["L3_ffn_cross_in_w"], i["L3_ffn_cross_out_w"]], 0).T)
    put("L3f_cross_b", columns(np.concatenate([i["L3_ffn_cross_in_b"], i["L3_ffn_cross_out_b"]])))
    put("L3f_mw1", i["L3_ffn_mlp_w1"].T)
    put("L3f_mb1", columns(i["L3_ffn_mlp_b1"]))
    put("L3f_mw2", chunks(i["L3_ffn_mlp_w2"].T))
    put("L3f_mb2", i["L3_ffn_mlp_b2"])
    return o

STAGES = (tokens, l0_attention, l0_ffn, l1_attention, l1_ffn, l2_attention, l2_ffn, l3_attention, l3_ffn)


def build(nc, d, out):
    with ExitStack() as st:
        core = Core()
        core.d = d
        core.h = st.enter_context(nc.sbuf_tensor("resid", [P, B, D], F32))
        core.ident = st.enter_context(nc.sbuf_tensor("ident_sb", [P, P], F32))
        core.rel_scratch = nc.dram_tensor("rel_scratch", [B, H, T * (T + 1)], F32, kind="Internal").ap()
        core.decay_scratch = nc.dram_tensor("decay_scratch", [BH, SLOTS], F32, kind="Internal").ap()
        core.in_scratch = nc.dram_tensor("in_scratch", [TILES * P, D], F32, kind="Internal").ap()
        core.out_scratch = nc.dram_tensor("out_scratch", [TILES * P, D], F32, kind="Internal").ap()
        core.slot_scratch = nc.dram_tensor("slot_scratch", [B, T, SLOTS], F32, kind="Internal").ap()
        core.back_scratch = nc.dram_tensor("back_scratch", [B, T, 2, T], F32, kind="Internal").ap()
        core.mask_scratch = nc.dram_tensor("mask_scratch", [T, B], F32, kind="Internal").ap()
        core.bc_scratch = nc.dram_tensor("bc_scratch", [2 * DS, N], F32, kind="Internal").ap()
        core.choice_scratch = nc.dram_tensor("choice_scratch", [B, 2], I32, kind="Internal").ap()
        for stage in STAGES:
            stage(nc, core, d)
        with Stage(nc, "store") as s:
            stored = s.sem("stored")
            with nc.Block() as block:
                @block.sync
                def _(sp):
                    sp.dma_start(out.rearrange("b t d -> t b d"), core.h[:]).then_inc(stored, 16)
                    sp.wait_ge(stored, 16)


def kernel(**inputs):
    import concourse.bacc as bacc
    from concourse.bass_utils import run_bass_kernel_spmd

    nc = bacc.Bacc("TRN2", target_bir_lowering=False, num_devices=1)
    arrays = layout(inputs)
    d = {k: nc.dram_tensor(k, a.shape, mybir.dt.from_np(a.dtype), kind="ExternalInput").ap() for k, a in arrays.items()}
    out = nc.dram_tensor("out", (B, T, D), F32, kind="ExternalOutput").ap()
    build(nc, d, out)
    r = run_bass_kernel_spmd(nc, [arrays], core_ids=[0])
    return r.results[0]["out"]
```
